# Optimizing a Trainium2 kernel written in Bass

```python
import numpy as np
import jax
import jax.numpy as jnp

def _softmax(x, axis=-1):
    return jax.nn.softmax(x, axis=axis)

def _gelu(x):
    return jax.nn.gelu(x, approximate=True)

def _silu(x):
    return jax.nn.silu(x)

def _sigmoid(x):
    return jax.nn.sigmoid(x)

def _layernorm(x, axis=-1, eps=1e-05):
    m = jnp.mean(x, axis=axis, keepdims=True)
    v = jnp.var(x, axis=axis, keepdims=True)
    return (x - m) / jnp.sqrt(v + eps)

def _scatter_add(tgt, idx, src, axis=0):
    return tgt.at[idx].add(src)

def _segment_sum(src, seg, n):
    return jax.ops.segment_sum(src, seg, n)
kernel_name = 'mk_prb_d1_jaxref_r4_7fe732'

def setup_inputs(seed: int=0):
    np.random.seed(seed)
    _w = jnp.asarray

    def _L0_attn_setup():
        import jax, jax.numpy as jnp
        import numpy as np
        HEADS = 16
        DIM_HEAD = 64
        EPS = 1e-08
        key = jax.random.key(seed)
        ks = jax.random.split(key, 5)
        B, N, D = (2, 512, 256)
        inner = HEADS * DIM_HEAD
        return {'x': jax.random.normal(ks[0], (B, N, D), jnp.float32), 'Wq': jax.random.normal(ks[1], (D, inner), jnp.float32) * D ** (-0.5), 'Wkv': jax.random.normal(ks[2], (D, 2 * inner), jnp.float32) * D ** (-0.5), 'Wo': jax.random.normal(ks[3], (inner, D), jnp.float32) * inner ** (-0.5), 'bo': jax.random.normal(ks[4], (D,), jnp.float32) * 0.02}
    _L0_attn_in = _L0_attn_setup()

    def _L0_ffn_setup():
        import jax, jax.numpy as jnp
        import numpy as np
        import math
        D_MODEL = 256
        D_FF = 1024
        NUM_EXPERTS = 8
        NUM_SHARED = 1
        E_ROUTED = NUM_EXPERTS - NUM_SHARED
        TOP_K = 2
        CAP_FACTOR = 1.25
        B, S = (4, 512)
        T = B * S
        CAPACITY = math.ceil(CAP_FACTOR * T * TOP_K / E_ROUTED)
        SHARED_SCALE = 1.0

        def _layernorm(x, g, b, eps=1e-05):
            mu = jnp.mean(x, axis=-1, keepdims=True)
            var = jnp.mean((x - mu) ** 2, axis=-1, keepdims=True)
            return (x - mu) * jax.lax.rsqrt(var + eps) * g + b
        key = jax.random.key(seed)
        ks = jax.random.split(key, 10)
        s = 0.02
        return {'x': jax.random.normal(ks[0], (B, S, D_MODEL), dtype=jnp.float32), 'ln_g': jnp.ones((D_MODEL,), jnp.float32), 'ln_b': jnp.zeros((D_MODEL,), jnp.float32), 'Wr': jax.random.normal(ks[1], (D_MODEL, E_ROUTED), jnp.float32) * s, 'W1': jax.random.normal(ks[2], (E_ROUTED, D_MODEL, D_FF), jnp.float32) * s, 'W3': jax.random.normal(ks[3], (E_ROUTED, D_MODEL, D_FF), jnp.float32) * s, 'W2': jax.random.normal(ks[4], (E_ROUTED, D_FF, D_MODEL), jnp.float32) * s, 'W1s': jax.random.normal(ks[5], (D_MODEL, D_FF), jnp.float32) * s, 'W3s': jax.random.normal(ks[6], (D_MODEL, D_FF), jnp.float32) * s, 'W2s': jax.random.normal(ks[7], (D_FF, D_MODEL), jnp.float32) * s}
    _L0_ffn_in = _L0_ffn_setup()
    _d = {'L0_attn_x': _L0_attn_in['x'], 'L0_attn_Wq': _L0_attn_in['Wq'], 'L0_attn_Wkv': _L0_attn_in['Wkv'], 'L0_attn_Wo': _L0_attn_in['Wo'], 'L0_attn_bo': _L0_attn_in['bo'], 'L0_ffn_ln_g': _L0_ffn_in['ln_g'], 'L0_ffn_ln_b': _L0_ffn_in['ln_b'], 'L0_ffn_Wr': _L0_ffn_in['Wr'], 'L0_ffn_W1': _L0_ffn_in['W1'], 'L0_ffn_W3': _L0_ffn_in['W3'], 'L0_ffn_W2': _L0_ffn_in['W2'], 'L0_ffn_W1s': _L0_ffn_in['W1s'], 'L0_ffn_W3s': _L0_ffn_in['W3s'], 'L0_ffn_W2s': _L0_ffn_in['W2s']}
    _x0 = _d['L0_attn_x']
    _d['L0_attn_x'] = jax.random.normal(jax.random.fold_in(jax.random.key(seed), 1), (16, 512, 256), dtype=_x0.dtype)
    del _x0
    return _d

def reference(L0_attn_x, L0_attn_Wq, L0_attn_Wkv, L0_attn_Wo, L0_attn_bo, L0_ffn_ln_g, L0_ffn_ln_b, L0_ffn_Wr, L0_ffn_W1, L0_ffn_W3, L0_ffn_W2, L0_ffn_W1s, L0_ffn_W3s, L0_ffn_W2s):

    def _L0_attn_ref(x, Wq, Wkv, Wo, bo):
        import jax, jax.numpy as jnp
        import numpy as np
        HEADS = 16
        DIM_HEAD = 64
        EPS = 1e-08
        B, N, D = x.shape
        H, Dh = (HEADS, DIM_HEAD)
        scale = Dh ** (-0.5)
        q = (x @ Wq).reshape(B, N, H, Dh).transpose(0, 2, 1, 3)
        kv = x @ Wkv
        k = kv[..., :H * Dh].reshape(B, N, H, Dh).transpose(0, 2, 1, 3)
        v = kv[..., H * Dh:].reshape(B, N, H, Dh).transpose(0, 2, 1, 3)
        s = jnp.einsum('bhid,bhjd->bhij', q * scale, k)
        gm = jax.lax.stop_gradient(jnp.max(s, axis=-1, keepdims=True))
        causal_mask = jnp.triu(jnp.ones((N, N), bool), 1)
        p = jnp.where(causal_mask, 0.0, jnp.exp(s - gm))
        num = jnp.einsum('bhij,bhjd->bhid', p, v)
        out = num / (jnp.sum(p, axis=-1, keepdims=True) + EPS)
        out = out.transpose(0, 2, 1, 3).reshape(B, N, H * Dh)
        return out @ Wo + bo

    def _L0_ffn_ref(x, ln_g, ln_b, Wr, W1, W3, W2, W1s, W3s, W2s):
        import jax, jax.numpy as jnp
        import numpy as np
        import math
        D_MODEL = 256
        D_FF = 1024
        NUM_EXPERTS = 8
        NUM_SHARED = 1
        E_ROUTED = NUM_EXPERTS - NUM_SHARED
        TOP_K = 2
        CAP_FACTOR = 1.25
        B, S = (4, 512)
        T = B * S
        CAPACITY = math.ceil(CAP_FACTOR * T * TOP_K / E_ROUTED)
        SHARED_SCALE = 1.0

        def _layernorm(x, g, b, eps=1e-05):
            mu = jnp.mean(x, axis=-1, keepdims=True)
            var = jnp.mean((x - mu) ** 2, axis=-1, keepdims=True)
            return (x - mu) * jax.lax.rsqrt(var + eps) * g + b
        Bx, Sx, D = x.shape
        Tn = Bx * Sx
        h = _layernorm(x, ln_g, ln_b).reshape(Tn, D)
        logits = h @ Wr
        top_vals, top_idx = jax.lax.top_k(logits, TOP_K)
        gates = jax.nn.softmax(top_vals, axis=-1)
        idx = top_idx.T.reshape(-1)
        gat = gates.T.reshape(-1)
        tok = jnp.tile(jnp.arange(Tn), TOP_K)
        onehot = jax.nn.one_hot(idx, E_ROUTED, dtype=jnp.int32)
        pos = jnp.sum(jnp.cumsum(onehot, axis=0) * onehot, axis=-1) - 1
        keep = pos < CAPACITY
        pos_c = jnp.where(keep, pos, CAPACITY)
        xe = jnp.zeros((E_ROUTED, CAPACITY, D), h.dtype).at[idx, pos_c].set(h[tok], mode='drop')
        a = jnp.einsum('ecd,edf->ecf', xe, W1)
        b = jnp.einsum('ecd,edf->ecf', xe, W3)
        ye = jnp.einsum('ecf,efd->ecd', jax.nn.silu(a) * b, W2)
        out_slots = ye[jnp.clip(idx, 0, E_ROUTED - 1), jnp.clip(pos_c, 0, CAPACITY - 1)]
        out_slots = out_slots * (gat * keep.astype(gat.dtype))[:, None]
        routed = jnp.zeros((Tn, D), h.dtype).at[tok].add(out_slots)
        shared = jax.nn.silu(h @ W1s) * (h @ W3s) @ W2s
        out = routed + SHARED_SCALE * shared
        return out.reshape(Bx, Sx, D)
    x = L0_attn_x
    xn = _layernorm(x, axis=-1)
    x = x + _L0_attn_ref(xn, L0_attn_Wq, L0_attn_Wkv, L0_attn_Wo, L0_attn_bo) + _L0_ffn_ref(xn, L0_ffn_ln_g, L0_ffn_ln_b, L0_ffn_Wr, L0_ffn_W1, L0_ffn_W3, L0_ffn_W2, L0_ffn_W1s, L0_ffn_W3s, L0_ffn_W2s)
    return x

_drawn_inputs = setup_inputs


def setup_inputs(seed=0):
    import zlib

    import numpy as np

    out = dict(_drawn_inputs(seed))
    spreads = {'L0_ffn_ln_g': (1.0, 0.6), 'L0_ffn_ln_b': (0.0, 0.8)}
    factors = {'L0_attn_bo': 8.854,
     'L0_ffn_Wr': 3.715,
     'L0_ffn_W1': 3.522,
     'L0_ffn_W3': 3.48,
     'L0_ffn_W2': 3.484}
    for name, (base, spread) in spreads.items():
        noise = np.random.default_rng([zlib.crc32(name.encode()), seed]).standard_normal(out[name].shape)
        drawn = base * np.exp(spread * noise) if base else spread * noise
        out[name] = jnp.asarray(drawn.astype(out[name].dtype))
    for name, factor in factors.items():
        out[name] = (out[name] * factor).astype(out[name].dtype)
    return out
```

```python
from collections import namedtuple
from contextlib import ExitStack

import concourse.bass as bass
from concourse import mybir

ALU = mybir.AluOpType
ACT = mybir.ActivationFunctionType
AX_X = mybir.AxisListType.X
F32 = mybir.dt.float32
F32R = mybir.dt.float32r
BF16 = mybir.dt.bfloat16
I32 = mybir.dt.int32
U32 = mybir.dt.uint32

P = 128
HEADS = 16
LN_EPS = 1e-5
SOFTMAX_EPS = 1e-8
TOP_K = 2
CAPACITY_TOKENS = 4 * 512
LOWEST = -3.0e38

Env = namedtuple("Env", """
    B NB KC D E F DH CAP SLOTS tiles
    x Wq Wkv Wo bo ln_g ln_b Wr W1 W3 W2 W1s W3s W2s out
    xnT_dram hT_dram h_dram attn_dram ids_dram ye_dram
    ident upper ones causal logits gates token read_slot write_slot""")


def phase_constants(nc, env):
    with ExitStack() as cx:
        made = cx.enter_context(nc.semaphore("c_made"))
        block = cx.enter_context(nc.Block())

        @block.gpsimd
        def _(pool):
            nc.gpsimd.memset(env.ident[:], 0.0).then_inc(made, 1)
            nc.gpsimd.memset(env.upper[:], 1.0).then_inc(made, 1)
            nc.gpsimd.memset(env.ones[:], 1.0).then_inc(made, 1)
            nc.gpsimd.memset(env.causal[:], 0.0).then_inc(made, 1)
            pool.wait_ge(made, 4)
            nc.gpsimd.affine_select(out=env.ident[:], in_=env.ident[:], compare_op=ALU.not_equal, fill=1.0, base=0,
                                    pattern=[[-1, P]], channel_multiplier=1).then_inc(made, 1)
            nc.gpsimd.affine_select(out=env.upper[:], in_=env.upper[:], compare_op=ALU.is_ge, fill=0.0, base=0,
                                    pattern=[[1, P]], channel_multiplier=-1).then_inc(made, 1)
            nc.gpsimd.affine_select(out=env.causal[:], in_=env.causal[:], compare_op=ALU.is_ge, fill=LOWEST, base=0,
                                    pattern=[[0, 2], [-1, P]], channel_multiplier=1).then_inc(made, 1)
            pool.wait_ge(made, 7)


def phase_norm(nc, env):
    B, NB, KC, D, E = env.B, env.NB, env.KC, env.D, env.E
    N = NB * P
    with ExitStack() as cx:
        def sb(name, shape, dt=F32):
            return cx.enter_context(nc.sbuf_tensor(name, shape, dt))

        def sem(name):
            return cx.enter_context(nc.semaphore(name))

        x_sb = sb("n_x", [P, 2, NB, D])
        xn_sb = sb("n_xn", [P, 2, NB, D])
        z_sb = sb("n_z", [P, 2, NB, D])
        h_sb = sb("n_h", [P, 2, NB, D])
        xnT_sb = sb("n_xnT", [P, 2, KC, N])
        hT_sb = sb("n_hT", [P, 2, KC, N])
        g_sb = sb("n_g", [P, 1, D])
        b_sb = sb("n_b", [P, 1, D])
        wr_sb = sb("n_wr", [P, KC, E])
        stats = sb("n_stats", [P, NB, 6])
        mv = sb("n_mv", [P, NB, 2])
        ve = sb("n_ve", [P, NB])
        sd = sb("n_sd", [P, NB])
        rs = sb("n_rs", [P, NB])
        tmp = sb("n_tmp", [P, NB])
        xnT_ps = cx.enter_context(nc.psum_tensor("n_xnT_ps", [P, KC, N], F32))
        hT_ps = cx.enter_context(nc.psum_tensor("n_hT_ps", [P, KC, N], F32))
        lg_ps = cx.enter_context(nc.psum_tensor("n_lg_ps", [P, NB, E], F32))

        params_in = sem("n_params_in")
        x_in = [sem("n_x_in0"), sem("n_x_in1")]
        dve_step = sem("n_dve_step")
        turnstile = sem("n_turnstile")
        ve_ready = sem("n_ve_ready")
        sd_ready = sem("n_sd_ready")
        xn_ready = sem("n_xn_ready")
        z_ready = sem("n_z_ready")
        z_scaled = sem("n_z_scaled")
        h_ready = sem("n_h_ready")
        xnT_done = sem("n_xnT_done")
        hT_done = sem("n_hT_done")
        lg_done = sem("n_lg_done")
        xnT_copied = sem("n_xnT_copied")
        hT_copied = sem("n_hT_copied")
        lg_copied = sem("n_lg_copied")
        xnT_out = [sem("n_xnT_out0"), sem("n_xnT_out1")]
        hT_out = [sem("n_hT_out0"), sem("n_hT_out1")]
        h_out = [sem("n_h_out0"), sem("n_h_out1")]

        x_dram = env.x.rearrange("b (j p) d -> b p j d", p=P)
        h_dram = env.h_dram.rearrange("(b j p) d -> b p j d", p=P, j=NB)

        def one(t, b):
            return t[b] if isinstance(b, int) else t[bass.ds(b, 1)].rearrange("o p j d -> (o p) j d")

        def pipelined(eng, front, back):
            front(0, 0, 0)
            with eng.Fori(0, B // 2 - 1) as i:
                front(i * 2 + 1, 1, i)
                back(i * 2, 0, i)
                front(i * 2 + 2, 0, i + 1)
                back(i * 2 + 1, 1, i)
            front(B - 1, 1, B // 2 - 1)
            back(B - 2, 0, B // 2 - 1)
            back(B - 1, 1, B // 2 - 1)

        block = cx.enter_context(nc.Block())

        @block.sync
        def _(sp):
            for src, dst in ((env.ln_g, g_sb), (env.ln_b, b_sb)):
                row = src.rearrange("(a d) -> a d", a=1).broadcast_to([P, D])
                sp.dma_start(dst[:, 0, :], row).then_inc(params_in, 16)
            sp.dma_start(wr_sb[:], env.Wr.rearrange("(c p) e -> p c e", p=P)).then_inc(params_in, 16)
            for s in range(2):
                sp.dma_start(x_sb[:, s], x_dram[s]).then_inc(x_in[s], 16)

            def stores(k, s):
                sp.wait_ge(xnT_copied, k + 2)
                sp.dma_start(one(env.xnT_dram, k), xnT_sb[:, s]).then_inc(xnT_out[s], 16)
                sp.wait_ge(h_ready, k + 3)
                sp.dma_start(one(h_dram, k), h_sb[:, s]).then_inc(h_out[s], 16)
                sp.wait_ge(hT_copied, k + 2)
                sp.dma_start(one(env.hT_dram, k), hT_sb[:, s]).then_inc(hT_out[s], 16)

            with sp.Fori(0, B // 2 - 1) as i:
                for s in range(2):
                    sp.wait_ge(xn_ready, i * 2 + (s + 1))
                    sp.dma_start(x_sb[:, s], one(x_dram, i * 2 + (s + 2))).then_inc(x_in[s], 16)
                    stores(i * 2 + s, s)
            for s in range(2):
                stores(B - 2 + s, s)
            for s in range(2):
                for q in (xnT_out, h_out, hT_out):
                    sp.wait_ge(q[s], 16 * (B // 2) + 16)

        @block.vector
        def _(dve):
            dve.sem_inc(lg_copied, 1)
            steps = 2 * NB + 5

            def normalise(dst, src, k, nth):
                before = k * (2 * steps) + nth * steps
                for j in range(NB):
                    nc.vector.bn_stats(stats[:, j, :], src[:, j, :]).then_inc(dve_step, 1)
                dve.wait_ge(dve_step, before + NB)
                dve.sem_inc(turnstile, 1)
                for j in range(NB):
                    nc.vector.bn_aggr(mv[:, j, :], stats[:, j, :]).then_inc(dve_step, 1)
                dve.wait_ge(dve_step, before + 2 * NB)
                nc.vector.tensor_scalar(ve[:], mv[:, :, 1], LN_EPS, None, ALU.add).then_inc(ve_ready, 1)
                dve.wait_ge(sd_ready, k * 2 + (nth + 1))
                nc.vector.reciprocal(rs[:], sd[:]).then_inc(dve_step, 1)
                dve.wait_ge(dve_step, before + 2 * NB + 1)
                nc.vector.tensor_tensor(tmp[:], ve[:], rs[:], ALU.mult).then_inc(dve_step, 1)
                dve.wait_ge(dve_step, before + 2 * NB + 2)
                nc.vector.tensor_tensor(tmp[:], tmp[:], rs[:], ALU.mult).then_inc(dve_step, 1)
                dve.wait_ge(dve_step, before + 2 * NB + 3)
                nc.vector.tensor_scalar(tmp[:], tmp[:], -0.5, 1.5, ALU.mult, ALU.add).then_inc(dve_step, 1)
                dve.wait_ge(dve_step, before + 2 * NB + 4)
                nc.vector.tensor_tensor(rs[:], rs[:], tmp[:], ALU.mult).then_inc(dve_step, 1)
                dve.wait_ge(dve_step, before + steps)
                for j in range(NB):
                    last = nc.vector.tensor_scalar(dst[:, j, :], src[:, j, :], mv[:, j, 0:1], rs[:, j:j + 1],
                                                   ALU.subtract, ALU.mult)
                return last

            def front(k, s, i):
                dve.wait_ge(x_in[s], i * 16 + 16)
                dve.wait_ge(xnT_done, k + 1)
                normalise(xn_sb[:, s], x_sb[:, s], k, 0).then_inc(xn_ready, 1)
                dve.wait_ge(xn_ready, k + 1)
                dve.wait_ge(h_ready, k + 1)
                normalise(z_sb[:, s], xn_sb[:, s], k, 1).then_inc(z_ready, 1)

            def back(k, s, i):
                dve.wait_ge(lg_done, k + 3)
                at = slice(k * NB, k * NB + NB) if isinstance(k, int) else bass.ds(k * NB, NB)
                nc.vector.tensor_copy(env.logits[:, at, :], lg_ps[:]).then_inc(lg_copied, 1)

            pipelined(dve, front, back)

        @block.scalar
        def _(act):
            act.sem_inc(xnT_copied, 1)
            act.sem_inc(hT_copied, 1)
            for s in range(2):
                act.sem_inc(xnT_out[s], 16)
                act.sem_inc(hT_out[s], 16)

            def front(k, s, i):
                for nth in range(2):
                    act.wait_ge(ve_ready, k * 2 + (nth + 1))
                    nc.scalar.activation(sd[:], ve[:], ACT.Sqrt).then_inc(sd_ready, 1)
                act.wait_ge(xnT_done, k + 3)
                act.wait_ge(xnT_out[s], i * 16 + 16)
                nc.scalar.copy(xnT_sb[:, s], xnT_ps[:]).then_inc(xnT_copied, 1)

            def back(k, s, i):
                act.wait_ge(hT_done, k + 3)
                act.wait_ge(hT_out[s], i * 16 + 16)
                act.wait_ge(lg_done, k + 1)
                nc.scalar.copy(hT_sb[:, s], hT_ps[:]).then_inc(hT_copied, 1)

            pipelined(act, front, back)

        @block.gpsimd
        def _(pool):
            pool.sem_inc(h_ready, 2)
            for s in range(2):
                pool.sem_inc(h_out[s], 16)
            g_row, b_row = g_sb[:].broadcast_to([P, NB, D]), b_sb[:].broadcast_to([P, NB, D])
            pool.wait_ge(params_in, 48)
            with pool.Fori(0, B // 2) as i:
                for s in range(2):
                    k = i * 2 + s
                    pool.wait_ge(z_ready, k + 1)
                    nc.gpsimd.tensor_tensor(z_sb[:, s], z_sb[:, s], g_row, ALU.mult).then_inc(z_scaled, 1)
                    pool.wait_ge(z_scaled, k + 1)
                    pool.wait_ge(h_out[s], i * 16 + 16)
                    pool.wait_ge(hT_done, k + 1)
                    nc.gpsimd.tensor_tensor(h_sb[:, s], z_sb[:, s], b_row, ALU.add).then_inc(h_ready, 1)

        @block.tensor
        def _(pe):
            pe.sem_inc(xnT_done, 2)
            pe.sem_inc(hT_done, 2)
            pe.sem_inc(lg_done, 2)
            pe.wait_ge(params_in, 48)

            def transposes(dst, src):
                for c in range(KC):
                    for j in range(NB):
                        last = nc.tensor.transpose(dst[:, c, j * P:(j + 1) * P], src[:, j, c * P:(c + 1) * P],
                                                   env.ident[:])
                return last

            def front(k, s, i):
                pe.wait_ge(xn_ready, k + 1)
                pe.wait_ge(xnT_copied, k + 1)
                transposes(xnT_ps, xn_sb[:, s]).then_inc(xnT_done, 1)

            def back(k, s, i):
                pe.wait_ge(h_ready, k + 3)
                pe.wait_ge(hT_copied, k + 1)
                transposes(hT_ps, h_sb[:, s]).then_inc(hT_done, 1)
                pe.wait_ge(hT_copied, k + 2)
                pe.wait_ge(lg_copied, k + 1)
                for j in range(NB):
                    for c in range(KC):
                        last = nc.tensor.matmul(lg_ps[:, j, :], hT_sb[:, s, c, j * P:(j + 1) * P], wr_sb[:, c, :],
                                                start=c == 0, stop=c == KC - 1)
                last.then_inc(lg_done, 1)

            pipelined(pe, front, back)


def phase_route(nc, env):
    T, E, CAP = env.tiles, env.E, env.CAP
    with ExitStack() as cx:
        def sb(name, shape, dt=F32):
            return cx.enter_context(nc.sbuf_tensor(name, shape, dt))

        weight = sb("r_weight", [P, T, E])
        ebase = sb("r_ebase", [P, TOP_K * T, E])
        onehot = sb("r_onehot", [P, TOP_K * T, E])
        onehot16 = sb("r_onehot16", [P, TOP_K * T, E], BF16)
        a = sb("r_a", [P, T, E])
        b = sb("r_b", [P, T, E])
        rest = sb("r_rest", [P, T, E])
        top = sb("r_top", [P, TOP_K, T])
        mark = sb("r_mark", [P, T])
        run = sb("r_run", [P, 2, TOP_K * T, E])
        totals = sb("r_totals", [P, TOP_K * T, E])
        place = sb("r_place", [P, TOP_K * T, E])
        pos = sb("r_pos", [P, TOP_K * T])
        start = sb("r_start", [P, TOP_K * T])
        kept = sb("r_kept", [P, TOP_K * T])
        slot = sb("r_slot", [P, TOP_K * T])
        diff = sb("r_diff", [P, T])
        gate = sb("r_gate", [P, TOP_K, T])
        zero_ids = sb("r_zero_ids", [P, env.SLOTS // P], I32)
        W = TOP_K * T * E // 2
        within_ps = cx.enter_context(nc.psum_tensor("r_within_ps", [P, 2, 512], F32))
        totals_ps = cx.enter_context(nc.psum_tensor("r_totals_ps", [P, 2, 512], F32))

        step = cx.enter_context(nc.semaphore("r_step"))
        iotas = cx.enter_context(nc.semaphore("r_iotas"))
        zeroed = cx.enter_context(nc.semaphore("r_zeroed"))
        onehot_ready = cx.enter_context(nc.semaphore("r_onehot_ready"))
        counted = cx.enter_context(nc.semaphore("r_counted"))
        diff_ready = cx.enter_context(nc.semaphore("r_diff_ready"))
        exp_ready = cx.enter_context(nc.semaphore("r_exp_ready"))
        block = cx.enter_context(nc.Block())

        @block.gpsimd
        def _(pool):
            nc.gpsimd.iota(weight[:], [[0, T], [-1, E]], base=E, channel_multiplier=0,
                           allow_small_or_imprecise_dtypes=True).then_inc(iotas, 1)
            nc.gpsimd.iota(ebase[:], [[0, TOP_K * T], [CAP, E]], base=0, channel_multiplier=0,
                           allow_small_or_imprecise_dtypes=True).then_inc(iotas, 1)
            nc.gpsimd.iota(env.token[:], [[0, TOP_K], [P, T]], base=0, channel_multiplier=1).then_inc(iotas, 1)
            nc.gpsimd.memset(zero_ids[:], 0).then_inc(iotas, 1)
            pool.wait_ge(iotas, 4)

        @block.sync
        def _(sp):
            sp.wait_ge(iotas, 4)
            sp.dma_start(env.ids_dram.rearrange("(p c) o -> p (c o)", p=P), zero_ids[:]).then_inc(zeroed, 16)
            sp.wait_ge(zeroed, 16)

        @block.scalar
        def _(act):
            act.wait_ge(diff_ready, 1)
            nc.scalar.activation(gate[:, 1, :], diff[:], ACT.Exp).then_inc(exp_ready, 1)

        @block.tensor
        def _(pe):
            pe.wait_ge(onehot_ready, 1)
            flat = onehot16[:].rearrange("p t e -> p (t e)")
            for half in range(2):
                cols = slice(half * W, half * W + W)
                nc.tensor.matmul(within_ps[:, half, 0:W], env.upper[:], flat[:, cols], start=True, stop=True)
                last = nc.tensor.matmul(totals_ps[:, half, 0:W], env.ones[:], flat[:, cols], start=True, stop=True)
            last.then_inc(counted, 1)

        @block.vector
        def _(dve):
            n = [0]

            def done(ins):
                n[0] += 1
                ins.then_inc(step, 1)
                dve.wait_ge(step, n[0])

            def per_token(t):
                return t.unsqueeze(2).broadcast_to([P, t.shape[1], E])

            def choose(logits, k):
                rows = slice(k * T, k * T + T)
                done(nc.vector.tensor_reduce(top[:, k, :], logits, AX_X, ALU.max))
                done(nc.vector.tensor_tensor(a[:], logits, per_token(top[:, k, :]), ALU.is_equal))
                done(nc.vector.tensor_tensor(a[:], a[:], weight[:], ALU.mult))
                done(nc.vector.tensor_reduce(mark[:], a[:], AX_X, ALU.max))
                done(nc.vector.tensor_tensor(onehot[:, rows, :], weight[:], per_token(mark[:]), ALU.is_equal))

            dve.wait_ge(iotas, 4)
            choose(env.logits[:], 0)
            done(nc.vector.tensor_scalar(b[:], onehot[:, 0:T, :], LOWEST, None, ALU.mult))
            done(nc.vector.tensor_tensor(rest[:], env.logits[:], b[:], ALU.add))
            choose(rest[:], 1)
            nc.vector.tensor_copy(onehot16[:], onehot[:]).then_inc(onehot_ready, 1)
            nc.vector.tensor_tensor(diff[:], top[:, 1, :], top[:, 0, :], ALU.subtract).then_inc(diff_ready, 1)

            dve.wait_ge(exp_ready, 1)
            done(nc.vector.tensor_scalar(mark[:], gate[:, 1, :], 1.0, None, ALU.add))
            done(nc.vector.reciprocal(gate[:, 0, :], mark[:]))
            done(nc.vector.tensor_tensor(gate[:, 1, :], gate[:, 1, :], gate[:, 0, :], ALU.mult))

            dve.wait_ge(counted, 1)

            def halves(t):
                return t.rearrange("p (h t) e -> p h (t e)", h=2)

            done(nc.vector.tensor_copy(halves(totals[:]), totals_ps[:, :, 0:W]))
            src, reach, i = totals[:], 1, 0
            while reach < TOP_K * T:
                dst = run[:, i % 2]
                done(nc.vector.tensor_copy(dst[:, 0:reach, :], src[:, 0:reach, :]))
                done(nc.vector.tensor_tensor(dst[:, reach:, :], src[:, reach:, :], src[:, :TOP_K * T - reach, :], ALU.add))
                src, reach, i = dst, reach * 2, i + 1
            done(nc.vector.tensor_tensor(place[:], src, totals[:], ALU.subtract))
            done(nc.vector.tensor_tensor(halves(place[:]), halves(place[:]), within_ps[:, :, 0:W], ALU.add))
            done(nc.vector.tensor_tensor(place[:], place[:], onehot[:], ALU.mult))
            done(nc.vector.tensor_reduce(pos[:], place[:], AX_X, ALU.add))
            done(nc.vector.tensor_scalar(pos[:], pos[:], -1.0, None, ALU.add))
            done(nc.vector.tensor_tensor(ebase[:], ebase[:], onehot[:], ALU.mult))
            done(nc.vector.tensor_reduce(start[:], ebase[:], AX_X, ALU.add))
            done(nc.vector.tensor_scalar(kept[:], pos[:], float(CAP), None, ALU.is_lt))
            done(nc.vector.tensor_tensor(env.gates[:], gate[:].rearrange("p k t -> p (k t)"), kept[:], ALU.mult))
            done(nc.vector.tensor_scalar(slot[:], pos[:], float(CAP - 1), None, ALU.min))
            done(nc.vector.tensor_tensor(slot[:], slot[:], start[:], ALU.add))
            done(nc.vector.tensor_copy(env.read_slot[:], slot[:]))
            done(nc.vector.tensor_scalar(kept[:], kept[:], -float(env.SLOTS), float(env.SLOTS), ALU.mult, ALU.add))
            done(nc.vector.tensor_tensor(slot[:], slot[:], kept[:], ALU.add))
            done(nc.vector.tensor_copy(env.write_slot[:], slot[:]))


def split_weights(nc, jobs):
    with ExitStack() as cx:
        stages = [cx.enter_context(nc.sbuf_tensor(f"w_stage{n}", shape, F32)) for n, (_, _, _, shape) in enumerate(jobs)]
        loaded = [cx.enter_context(nc.semaphore(f"w_loaded{n}")) for n in range(len(jobs))]
        hi_done = cx.enter_context(nc.semaphore("w_hi_done"))
        lo_done = cx.enter_context(nc.semaphore("w_lo_done"))
        block = cx.enter_context(nc.Block())

        @block.sync
        def _(sp):
            for n, (_, _, src, _) in enumerate(jobs):
                sp.dma_start(stages[n][:], src).then_inc(loaded[n], 16)

        @block.scalar
        def _(act):
            for n, (hi, _, _, _) in enumerate(jobs):
                act.wait_ge(loaded[n], 16)
                nc.scalar.copy(hi, stages[n][:]).then_inc(hi_done, 1)

        @block.vector
        def _(dve):
            for n, (hi, lo, _, _) in enumerate(jobs):
                dve.wait_ge(hi_done, n + 1)
                nc.vector.tensor_tensor(lo, stages[n][:], hi.bitcast(F32), ALU.subtract).then_inc(lo_done, 1)
            dve.wait_ge(lo_done, len(jobs))


def phase_attention(nc, env):
    B, NB, KC, D, DH = env.B, env.NB, env.KC, env.D, env.DH
    N = NB * P
    PAIRS = HEADS // 2
    UNITS = PAIRS * NB
    INNER = HEADS * DH
    SCALE = float(DH) ** -0.5
    S_RING, P_RING = 2, 4
    STACKS = 16 * 8

    with ExitStack() as cx:
        def sb(name, shape, dt=F32):
            return cx.enter_context(nc.sbuf_tensor(name, shape, dt))

        def sem(name):
            return cx.enter_context(nc.semaphore(name))

        w_hi = sb("a_w_hi", [P, 3, KC, INNER], F32R)
        w_lo = sb("a_w_lo", [P, 3, KC, INNER], F32R)
        wo_hi = sb("a_wo_hi", [P, PAIRS, D], F32R)
        wo_lo = sb("a_wo_lo", [P, PAIRS, D], F32R)
        wkv = env.Wkv.rearrange("(c p) (m n) -> m p c n", p=P, m=2)
        split_weights(nc, [(w_hi[:, 0], w_lo[:, 0], env.Wq.rearrange("(c p) n -> p c n", p=P), [P, KC, INNER]),
                           (w_hi[:, 1], w_lo[:, 1], wkv[0], [P, KC, INNER]),
                           (w_hi[:, 2], w_lo[:, 2], wkv[1], [P, KC, INNER]),
                           (wo_hi[:], wo_lo[:], env.Wo.rearrange("(r p) n -> p r n", p=P), [P, PAIRS, D])])

        x_sb = sb("a_x", [P, KC, N])
        x_hi = sb("a_x_hi", [P, KC, N], F32R)
        x_lo = sb("a_x_lo", [P, KC, N], F32R)
        v_sb = sb("a_v", [P, 2, NB, 2 * P])
        nat = {m: sb(f"a_{m}_halves", [P, 2, N], F32R) for m in "qk"}
        q_st = sb("a_q_stack", [P, 2, 2, N], F32R)
        k_st = sb("a_k_stack", [P, 2, 2, 2, N], F32R)
        probs = sb("a_probs", [P, P_RING, 2, N])
        pT = sb("a_pT", [P, 2, 2, NB, N])
        o_hi = sb("a_o_hi", [P, PAIRS, N], F32R)
        o_lo = sb("a_o_lo", [P, PAIRS, N], F32R)
        ao = sb("a_ao", [P, NB, D])
        nmax = sb("a_nmax", [P, P_RING, 2])
        den = sb("a_den", [P, P_RING, 2])
        rden = sb("a_rden", [P, P_RING, 2])
        ids8 = sb("a_ids8", [P, TOP_K, NB], I32)
        slot8 = sb("a_slot8", [P, TOP_K, NB], I32)
        s_ps = cx.enter_context(nc.psum_tensor("a_s_ps", [P, S_RING, 2, N], F32))
        pt_ps = cx.enter_context(nc.psum_tensor("a_pt_ps", [P, 2, N], F32))
        ot_ps = cx.enter_context(nc.psum_tensor("a_ot_ps", [P, N], F32))
        pj_ps = cx.enter_context(nc.psum_tensor("a_pj_ps", [P, N], F32))

        turnstile = sem("a_turnstile")
        x_in = sem("a_x_in")
        xhi_done = sem("a_xhi_done")
        x_split = sem("a_x_split")
        pj_done = sem("a_pj_done")
        pj_evac = sem("a_pj_evac")
        hi_done = sem("a_hi_done")
        stacked = [sem("a_stacked0"), sem("a_stacked1")]
        s_done = sem("a_s_done")
        max_done = sem("a_max_done")
        masked = sem("a_masked")
        exp_done = sem("a_exp_done")
        den_step = sem("a_den_step")
        rden_ready = sem("a_rden_ready")
        normed = sem("a_normed")
        pt_done = sem("a_pt_done")
        pt_evac = sem("a_pt_evac")
        ot_done = sem("a_ot_done")
        ohi_done = sem("a_ohi_done")
        ot_evac = sem("a_ot_evac")
        ao_out = sem("a_ao_out")
        slots_copied = sem("a_slots_copied")
        scattered = sem("a_scattered")

        def piece_at(u):
            p, qb = divmod(u, NB)
            if qb == 2:
                return ("q", p + 2, 0)
            if qb == 3:
                return ("k", p + 2, 0)
            if p % 2 == 1:
                return ("v", (p + 1) // 2, qb)
            return None

        AHEAD = [("q", 0, 0), ("k", 0, 0), ("v", 0, 0), ("v", 0, 1), ("q", 1, 0), ("k", 1, 0)]
        USES = len([u for u in range(UNITS) if piece_at(u)]) + 1
        PT_USES = UNITS + 1
        order = [u for u in range(UNITS) if piece_at(u)]
        QK = 2 * PAIRS

        def of_next(piece):
            return piece[1] >= (PAIRS // 2 if piece[0] == "v" else PAIRS)

        def uses_before(b, u):
            return b * USES + (len(AHEAD) + len([v for v in order if v < u]))

        def highs_before(b, u):
            return b * QK + (4 + len([v for v in order if v < u and piece_at(v)[0] in "qk"]))

        def over_batches(eng, batch):
            with eng.Fori(0, B - 1) as b:
                batch(b, False)
            batch(B - 1, True)

        block = cx.enter_context(nc.Block())

        @block.tensor
        def _(pe):
            pe.sem_inc(pt_done, P_RING)
            pe.sem_inc(ot_done, 2)

            def project(piece, used, batches):
                kind, which, part = piece
                pe.wait_ge(x_split, batches)
                if not isinstance(used, int) or used > 0:
                    pe.wait_ge(pj_evac, used)
                if kind in "qk":
                    m, r = "qk".index(kind), which % PAIRS
                    passes = [(w, x, c) for c in range(KC) for w, x in ((w_hi, x_hi), (w_hi, x_lo), (w_lo, x_hi))]
                    for n, (w, x, c) in enumerate(passes):
                        last = nc.tensor.matmul(pj_ps[:], w[:, m, c, r * P:(r + 1) * P], x[:, c, :],
                                                start=n == 0, stop=n == len(passes) - 1)
                else:
                    g = which % (PAIRS // 2)
                    passes = [(w, x, c) for c in range(KC) for w, x in ((w_hi, x_hi), (w_lo, x_hi), (w_hi, x_lo))]
                    for j in range(2):
                        t = 2 * part + j
                        for n, (w, x, c) in enumerate(passes):
                            last = nc.tensor.matmul(pj_ps[:, j * 2 * P:(j + 1) * 2 * P], x[:, c, t * P:(t + 1) * P],
                                                    w[:, 2, c, g * 2 * P:(g + 1) * 2 * P],
                                                    start=n == 0, stop=n == len(passes) - 1)
                last.then_inc(pj_done, 1)

            def scores(b, u):
                p, qb = divmod(u, NB)
                if not (isinstance(b, int) and u < S_RING and b == 0):
                    pe.wait_ge(exp_done, b * UNITS + (u - S_RING + 1))
                if qb == 0:
                    pe.wait_ge(stacked[p % 2], b * (STACKS * PAIRS // 2) + STACKS * (p // 2 + 1))
                for h in range(2):
                    lhsT = q_st[:, p % 2, h, qb * P:(qb + 1) * P]
                    nc.tensor.matmul(s_ps[:, u % S_RING, h, :], lhsT, k_st[:, p % 2, h, 0, :], start=True, stop=False)
                    last = nc.tensor.matmul(s_ps[:, u % S_RING, h, :], lhsT, k_st[:, p % 2, h, 1, :], start=False, stop=True)
                last.then_inc(s_done, 1)

            def turn(b, u):
                qb = u % NB
                pe.wait_ge(normed, b * UNITS + (u + 1))
                pe.wait_ge(pt_evac, b * PT_USES + (u + 1))
                for h in range(2):
                    for k in range(qb + 1):
                        last = nc.tensor.transpose(pt_ps[:, h, k * P:(k + 1) * P], probs[:, u % P_RING, h, k * P:(k + 1) * P],
                                                   env.ident[:])
                last.then_inc(pt_done, 1)

            def values(b, p, ks):
                if ks[0] == 0:
                    pe.wait_ge(pt_evac, b * PT_USES + (NB * p + NB - 1 + 2))
                    pe.wait_ge(pj_evac, uses_before(b, 2 * NB * (p // 2)))
                    pe.wait_ge(ot_evac, b * PAIRS + (p + 1))
                for k in ks:
                    for h in range(2):
                        col = (p % 2) * P + h * DH
                        last = nc.tensor.matmul(ot_ps[h * DH:(h + 1) * DH, k * P:N],
                                                v_sb[:, (p // 2) % 2, k, col:col + DH], pT[:, p % 2, h, k, k * P:N],
                                                start=k == 0, stop=k == NB - 1)
                if ks[-1] == NB - 1:
                    last.then_inc(ot_done, 1)

            def out_project(bank, tiles, pairs):
                passes = [(o, w) for o, w in ((o_hi, wo_hi), (o_hi, wo_lo), (o_lo, wo_hi))]
                for j, t in enumerate(tiles):
                    for r in pairs:
                        for n, (o, w) in enumerate(passes):
                            last = nc.tensor.matmul(bank[:, j * D:(j + 1) * D], o[:, r, t * P:(t + 1) * P], w[:, r, :],
                                                    start=j == 0 and r == 0 and n == 0,
                                                    stop=r == PAIRS - 1 and n == len(passes) - 1, skip_group_check=True)
                return last

            for n, piece in enumerate(AHEAD):
                project(piece, n, 1)
            scores(0, 0)
            scores(0, 1)

            def batch(b, is_last):
                for u in range(UNITS):
                    p, qb = divmod(u, NB)
                    if u + S_RING < UNITS or not is_last:
                        scores(b, u + S_RING)
                    turn(b, u)
                    piece = piece_at(u)
                    if piece and not (is_last and of_next(piece)):
                        project(piece, uses_before(b, u), b + 1 + of_next(piece))
                    if p > 0 and qb < 2:
                        values(b, p - 1, (2 * qb, 2 * qb + 1))
                uses = uses_before(b, UNITS) - (len([u for u in order if of_next(piece_at(u))]) if is_last else 0)
                pe.wait_ge(pj_evac, uses)
                pe.wait_ge(ot_evac, b * PAIRS + PAIRS)
                out_project(pj_ps, (0, 1), range(PAIRS - 1))
                values(b, PAIRS - 1, (0, 1, 2, 3))
                pe.wait_ge(pt_evac, b * PT_USES + (UNITS + 1))
                out_project(pt_ps[:, 0, :], (2, 3), range(PAIRS - 1))
                pe.wait_ge(ot_evac, b * PAIRS + (PAIRS + 1))
                out_project(pj_ps, (0, 1), (PAIRS - 1,)).then_inc(pj_done, 1)
                out_project(pt_ps[:, 0, :], (2, 3), (PAIRS - 1,)).then_inc(pt_done, 1)

            over_batches(pe, batch)

        @block.vector
        def _(dve):
            dve.sem_inc(ot_evac, 1)

            def split_x(batches):
                dve.wait_ge(xhi_done, batches)
                nc.vector.tensor_tensor(x_lo[:], x_sb[:], x_hi[:].bitcast(F32), ALU.subtract).then_inc(x_split, 1)

            def low(piece, used, highs, b):
                kind, which, part = piece
                if kind == "v":
                    dve.wait_ge(pj_done, used + 1)
                    if b is not None:
                        dve.wait_ge(ot_done, b * PAIRS + 2 * which)
                    dst = v_sb[:, which % 2, 2 * part:2 * part + 2, :]
                    nc.vector.tensor_copy(dst, pj_ps[:].rearrange("p (j n) -> p j n", j=2)).then_inc(pj_evac, 1)
                    return
                hi, lo = nat[kind][:, 0, :], nat[kind][:, 1, :]
                dve.wait_ge(hi_done, highs + 1)
                if kind == "q":
                    nc.vector.scalar_tensor_tensor(out=lo, in0=pj_ps[:], scalar=SCALE, in1=hi.bitcast(F32),
                                                   op0=ALU.mult, op1=ALU.subtract).then_inc(pj_evac, 1)
                else:
                    nc.vector.tensor_tensor(lo, pj_ps[:], hi.bitcast(F32), ALU.subtract).then_inc(pj_evac, 1)

            def maxima(b, u):
                qb = u % NB
                dve.wait_ge(s_done, b * UNITS + (u + 1))
                s = s_ps[:, u % S_RING]
                nc.vector.tensor_reduce(nmax[:, u % P_RING, :], s, AX_X, ALU.max, negate=True).then_inc(max_done, 1)
                dve.wait_ge(max_done, b * UNITS + (u + 1))
                diagonal = s[:, :, qb * P:(qb + 1) * P]
                nc.vector.tensor_tensor(diagonal, diagonal, env.causal[:], ALU.add).then_inc(masked, 1)

            def denominators(b, u):
                dve.wait_ge(exp_done, b * UNITS + (u + 1))
                d = den[:, u % P_RING, :]
                nc.vector.tensor_scalar(d, d, SOFTMAX_EPS, None, ALU.add).then_inc(den_step, 1)
                dve.wait_ge(den_step, b * UNITS + (u + 1))
                nc.vector.reciprocal(rden[:, u % P_RING, :], d).then_inc(rden_ready, 1)
                dve.wait_ge(rden_ready, b * UNITS + (u + 1))
                for h in range(2):
                    pr = probs[:, u % P_RING, h, 0:(u % NB + 1) * P]
                    last = nc.vector.tensor_scalar(pr, pr, rden[:, u % P_RING, h:h + 1], None, ALU.mult)
                last.then_inc(normed, 1)

            def output_low(b, p):
                dve.wait_ge(ohi_done, b * PAIRS + (p + 1))
                nc.vector.tensor_tensor(o_lo[:, p, :], ot_ps[:], o_hi[:, p, :].bitcast(F32), ALU.subtract).then_inc(ot_evac, 1)

            split_x(1)
            highs = 0
            for n, piece in enumerate(AHEAD):
                low(piece, n, highs, None)
                highs += piece[0] != "v"
            maxima(0, 0)
            maxima(0, 1)
            denominators(0, 0)

            def batch(b, is_last):
                for u in range(UNITS):
                    p, qb = divmod(u, NB)
                    if u + 1 < UNITS or not is_last:
                        denominators(b, u + 1)
                    if u + S_RING < UNITS or not is_last:
                        maxima(b, u + S_RING)
                    piece = piece_at(u)
                    if piece and not (is_last and of_next(piece)):
                        low(piece, uses_before(b, u), highs_before(b, u), b)
                    if p > 0 and qb == 1:
                        output_low(b, p - 1)
                    if u == UNITS - 2 * NB and not is_last:
                        split_x(b + 2)
                output_low(b, PAIRS - 1)
                uses = uses_before(b, UNITS) - (len([u for u in order if of_next(piece_at(u))]) if is_last else 0)
                dve.wait_ge(pj_done, uses + 1)
                dve.wait_ge(ao_out, b * 16 + 16)
                nc.vector.tensor_copy(ao[:, 0:2, :], pj_ps[:].rearrange("p (j n) -> p j n", j=2)).then_inc(pj_evac, 1)

            over_batches(dve, batch)

        @block.scalar
        def _(act):
            act.sem_inc(pt_evac, 1)

            def split_x(batches, pj):
                act.wait_ge(x_in, batches * 16)
                if pj is not None:
                    act.wait_ge(pj_done, pj)
                nc.scalar.copy(x_hi[:], x_sb[:]).then_inc(xhi_done, 1)

            def high(piece, used, stack_before):
                kind, which, part = piece
                if kind == "v":
                    return
                act.wait_ge(pj_done, used + 1)
                if stack_before is not None:
                    act.wait_ge(*stack_before)
                nc.scalar.activation(nat[kind][:, 0, :], pj_ps[:], ACT.Copy, scale=SCALE if kind == "q" else 1.0)\
                    .then_inc(hi_done, 1)

            def exps(b, u):
                qb = u % NB
                act.wait_ge(masked, b * UNITS + (u + 1))
                if u >= P_RING:
                    act.wait_ge(pt_done, b * PT_USES + (u + 1))
                elif not (isinstance(b, int) and b == 0 and u < S_RING):
                    act.wait_ge(pt_done, b * PT_USES + u)
                n = (qb + 1) * P
                for h in range(2):
                    last = nc.scalar.activation(probs[:, u % P_RING, h, 0:n], s_ps[:, u % S_RING, h, 0:n], ACT.Exp,
                                                bias=nmax[:, u % P_RING, h:h + 1], accum_out=den[:, u % P_RING, h:h + 1])
                last.then_inc(exp_done, 1)

            def turned(b, u):
                p, qb = divmod(u, NB)
                act.wait_ge(pt_done, b * PT_USES + (u + 1 + P_RING))
                if qb == 0:
                    act.wait_ge(ot_done, b * PAIRS + (p + 1))
                src = pt_ps[:, :, 0:(qb + 1) * P].rearrange("p h (k q) -> p h k q", q=P)
                nc.scalar.copy(pT[:, p % 2, :, 0:qb + 1, qb * P:(qb + 1) * P], src).then_inc(pt_evac, 1)

            def output_high(b, p):
                act.wait_ge(ot_done, b * PAIRS + (p + 3))
                if p == 0:
                    act.wait_ge(pt_done, b * PT_USES + P_RING)
                nc.scalar.copy(o_hi[:, p, :], ot_ps[:]).then_inc(ohi_done, 1)

            split_x(1, None)
            for n, piece in enumerate(AHEAD):
                high(piece, n, (stacked[0], STACKS) if piece[1] == 1 and piece[0] in "qk" else None)
            exps(0, 0)
            exps(0, 1)

            def batch(b, is_last):
                for u in range(UNITS):
                    p, qb = divmod(u, NB)
                    turned(b, u)
                    piece = piece_at(u)
                    if piece and not (is_last and of_next(piece)):
                        high(piece, uses_before(b, u), (stacked[(p + 1) % 2], b * (STACKS * PAIRS // 2) + STACKS * ((p + 1) // 2 + 1)))
                    if u + S_RING < UNITS or not is_last:
                        exps(b, u + S_RING)
                    if p > 0 and qb == 1:
                        output_high(b, p - 1)
                    if u == UNITS - 2 * NB and not is_last:
                        split_x(b + 2, uses_before(b, UNITS - 2 * NB))
                output_high(b, PAIRS - 1)
                act.wait_ge(pt_done, b * PT_USES + (PT_USES + P_RING))
                act.wait_ge(ao_out, b * 16 + 16)
                nc.scalar.copy(ao[:, 2:4, :], pt_ps[:, 0, :].rearrange("p (j n) -> p j n", j=2)).then_inc(pt_evac, 1)

            over_batches(act, batch)

        @block.gpsimd
        def _(pool):
            PER = TOP_K * NB
            ids = env.token[:].rearrange("p (k t) -> p k t", k=TOP_K)
            slots = env.write_slot[:].rearrange("p (k t) -> p k t", k=TOP_K)

            with pool.Fori(0, B) as b:
                for u in range(UNITS):
                    if u == 0:
                        nc.gpsimd.tensor_copy(ids8[:], ids[:, :, bass.ds(b * NB, NB)]).then_inc(slots_copied, 1)
                        nc.gpsimd.tensor_copy(slot8[:], slots[:, :, bass.ds(b * NB, NB)]).then_inc(slots_copied, 1)
                    if u % 3 == 1 and u // 3 < PER:
                        n = u // 3
                        if n == 0:
                            pool.wait_ge(slots_copied, b * 2 + 2)
                            pool.sem_inc(turnstile, 1)
                        k, j = divmod(n, NB)
                        nc.gpsimd.indirect_dma_start(
                            out=env.ids_dram, out_offset=bass.IndirectOffsetOnAxis(ap=slot8[:, k, j:j + 1].bitcast(U32), axis=0),
                            in_=ids8[:, k, j:j + 1], in_offset=None, bounds_check=env.SLOTS - 1, oob_is_err=False,
                            compute_op=ALU.bypass).then_inc(scattered, 16)
                pool.wait_ge(scattered, b * (16 * PER) + 16 * PER)

        @block.sync
        def _(sp):
            sp.sem_inc(ao_out, 16)
            sp.dma_start(x_sb[:], env.xnT_dram[0]).then_inc(x_in, 16)
            a_dram = env.attn_dram.rearrange("(b j p) d -> b p j d", p=P, j=NB)

            def one(t, b):
                return t[b] if isinstance(b, int) else t[bass.ds(b, 1)].rearrange("o p j d -> (o p) j d")

            def raw(t):
                return t.bitcast(F32)

            HALF = (slice(0, DH), slice(DH, P))

            def stack_q(par):
                for h in range(2):
                    for part in range(2):
                        sp.dma_start(raw(q_st[HALF[part], par, h, :]), raw(nat["q"][HALF[h], part, :])).then_inc(stacked[par], 16)

            def stack_k(par):
                for h in range(2):
                    for to in range(2):
                        sp.dma_start(raw(k_st[HALF[to], par, h]), raw(nat["k"][HALF[h]])).then_inc(stacked[par], 16)

            for par in range(2):
                sp.wait_ge(pj_evac, (1, 5)[par])
                stack_q(par)
                sp.wait_ge(pj_evac, (2, 6)[par])
                stack_k(par)

            def batch(b, is_last):
                if not is_last:
                    sp.wait_ge(x_split, b + 1)
                    sp.dma_start(x_sb[:], one(env.xnT_dram, b + 1)).then_inc(x_in, 16)
                for p in range(PAIRS):
                    u = NB * p + NB - 2
                    if is_last and of_next(piece_at(u)):
                        continue
                    sp.wait_ge(s_done, b * UNITS + NB * (p + 1))
                    sp.sem_inc(turnstile, 1)
                    sp.wait_ge(pj_evac, uses_before(b, u) + 1)
                    stack_q(p % 2)
                    sp.wait_ge(pj_evac, uses_before(b, u) + 2)
                    stack_k(p % 2)
                uses = uses_before(b, UNITS) - (len([u for u in order if of_next(piece_at(u))]) if is_last else 0)
                sp.wait_ge(pj_evac, uses + 1)
                sp.wait_ge(pt_evac, b * PT_USES + (PT_USES + 1))
                sp.dma_start(one(a_dram, b), ao[:]).then_inc(ao_out, 16)

            over_batches(sp, batch)
            sp.wait_ge(ao_out, 16 * (B + 1))


def phase_experts(nc, env, routed):
    B, NB, KC, D, E, F, T = env.B, env.NB, env.KC, env.D, env.E, env.F, env.tiles
    FB = F // P
    GROUPS = E if routed else B // 2
    W = env.CAP // 2 if routed else NB * P
    BLOCKS = [(t, min(P, W - t)) for t in range(0, W, P)]
    R = len(BLOCKS)
    name = "e" if routed else "f"

    with ExitStack() as cx:
        def sb(n, shape, dt=F32):
            return cx.enter_context(nc.sbuf_tensor(f"{name}_{n}", shape, dt))

        def ps(n, shape):
            return cx.enter_context(nc.psum_tensor(f"{name}_{n}", shape, F32))

        def sem(n):
            return cx.enter_context(nc.semaphore(f"{name}_{n}"))

        w13_hi = sb("w13_hi", [P, 2, KC, F], F32R)
        w13_lo = sb("w13_lo", [P, 2, KC, F], F32R)
        w2_hi = sb("w2_hi", [P, FB, D], F32R)
        w2_lo = sb("w2_lo", [P, FB, D], F32R)
        w13_st = sb("w13_st", [P, 2, KC, F])
        w2_st = sb("w2_st", [P, FB, D])
        x_hi = sb("x_hi", [P, 2, KC, W], F32R)
        x_lo = sb("x_lo", [P, 2, KC, W], F32R)
        silu = sb("silu", [P, 2, W])
        g = sb("g", [P, 2, W])
        g_hi = sb("g_hi", [P, FB, W], F32R)
        g_lo = sb("g_lo", [P, FB, W], F32R)
        ab_ps = ps("ab_ps", [P, 2, 2, 512])
        y_ps = ps("y_ps", [P, 2, 512])

        turnstile = sem("turnstile")
        w_in = sem("w_in")
        w13hi_done = sem("w13hi_done")
        w13_ready = sem("w13_ready")
        w2hi_done = sem("w2hi_done")
        w2_ready = sem("w2_ready")
        xhi_done = sem("xhi_done")
        x_ready = sem("x_ready")
        ab_done = sem("ab_done")
        silu_done = sem("silu_done")
        g_done = sem("g_done")
        ghi_done = sem("ghi_done")
        glo_done = sem("glo_done")
        y_done = sem("y_done")
        y_read = sem("y_read")

        if routed:
            ids = sb("ids", [P, 2, R], I32)
            xg = sb("xg", [P, 2, R, D])
            y_sb = sb("y_sb", [P, 2, R, D])
            xT_ps = ps("xT_ps", [P, KC, 512])
            ids_in = [sem("ids_in0"), sem("ids_in1")]
            gathered = [sem("gathered0"), sem("gathered1")]
            xT_done = sem("xT_done")
            y_out = [sem("y_out0"), sem("y_out1")]
        else:
            hT = sb("hT", [P, 2, KC, W])
            base = sb("base", [P, 2, NB, D])
            attn = sb("attn", [P, 2, NB, D])
            bo = sb("bo", [P, 1, D])
            yg = sb("yg", [P, 2, TOP_K * NB, D])
            slot8 = sb("slot8", [P, 2, TOP_K, NB], I32)
            gate8 = sb("gate8", [P, 2, TOP_K, NB])
            bo_in = sem("bo_in")
            hT_in = [sem("hT_in0"), sem("hT_in1")]
            base_in = [sem("base_in0"), sem("base_in1")]
            base_step = sem("base_step")
            base_ready = sem("base_ready")
            slots_copied = sem("slots_copied")
            gathered = [sem("gathered0"), sem("gathered1")]
            acc_step = sem("acc_step")
            gate_step = sem("gate_step")
            out_out = [sem("out_out0"), sem("out_out1")]

        def w_views(e):
            if not routed:
                return env.W1s.rearrange("(c p) f -> p c f", p=P), env.W3s.rearrange("(c p) f -> p c f", p=P), \
                    env.W2s.rearrange("(n p) d -> p n d", p=P)

            def pick(t):
                return t[e] if isinstance(e, int) else t[bass.ds(e, 1)].rearrange("o a b -> (o a) b")
            return pick(env.W1).rearrange("(c p) f -> p c f", p=P), pick(env.W3).rearrange("(c p) f -> p c f", p=P), \
                pick(env.W2).rearrange("(n p) d -> p n d", p=P)

        def over_groups(eng, group):
            with eng.Fori(0, GROUPS - 1) as i:
                group(i, False)
            group(GROUPS - 1, True)

        block = cx.enter_context(nc.Block())

        @block.tensor
        def _(pe):
            pe.sem_inc(y_done, R)
            if routed:
                pe.sem_inc(xT_done, 2)

            def hidden(c, s):
                pe.wait_ge(x_ready, c + 1)
                for f in range(FB):
                    pe.wait_ge(g_done, c * FB + (f + 1))
                    for m in range(2):
                        passes = [(w, x, k) for k in range(KC) for w, x in ((w13_hi, x_hi), (w13_hi, x_lo), (w13_lo, x_hi))]
                        for n, (w, x, k) in enumerate(passes):
                            last = nc.tensor.matmul(ab_ps[:, f % 2, m, 0:W], w[:, m, k, f * P:(f + 1) * P], x[:, s, k, :],
                                                    start=n == 0, stop=n == len(passes) - 1)
                    last.then_inc(ab_done, 1)

            def rows(c, s):
                pe.wait_ge(glo_done, c * FB + (FB + 2))
                for j, (t, n_t) in enumerate(BLOCKS):
                    pe.wait_ge(y_read, c * R + (j + 1))
                    passes = [(a, w, f) for f in range(FB) for a, w in ((g_hi, w2_hi), (g_hi, w2_lo), (g_lo, w2_hi))]
                    for n, (a, w, f) in enumerate(passes):
                        last = nc.tensor.matmul(y_ps[0:n_t, (s * R + j) % 2, 0:D], a[:, f, t:t + n_t], w[:, f, :],
                                                start=n == 0, stop=n == len(passes) - 1)
                    last.then_inc(y_done, 1)

            def turn(c, s, i):
                pe.wait_ge(gathered[s], i * (16 * R) + 16 * R)
                if not isinstance(c, int) or c > 0:
                    pe.wait_ge(x_ready, c)
                for k in range(KC):
                    for j, (t, n_t) in enumerate(BLOCKS):
                        last = nc.tensor.transpose(xT_ps[:, k, t:t + n_t], xg[0:n_t, s, j, k * P:(k + 1) * P],
                                                   env.ident[0:n_t, 0:n_t])
                last.then_inc(xT_done, 1)

            if routed:
                turn(0, 0, 0)
            else:
                pe.wait_ge(w13_ready, 1)
                pe.wait_ge(w2_ready, 1)

            def group(i, is_last):
                for s in range(2):
                    c = i * 2 + s
                    if routed and s == 0:
                        pe.wait_ge(w13_ready, i + 1)
                    hidden(c, s)
                    if routed and not (is_last and s == 1):
                        turn(c + 1, 1 - s, i + s)
                    if routed and s == 0:
                        pe.wait_ge(w2_ready, i + 1)
                    rows(c, s)

            over_groups(pe, group)

        @block.scalar
        def _(act):
            def split_w13(e):
                act.wait_ge(w_in, e * 48 + 48)
                nc.scalar.copy(w13_hi[:], w13_st[:]).then_inc(w13hi_done, 1)

            def split_w2():
                nc.scalar.copy(w2_hi[:], w2_st[:]).then_inc(w2hi_done, 1)

            def gate(c, s, i):
                for f in range(FB + 1):
                    if f < FB:
                        act.wait_ge(ab_done, c * FB + (f + 1))
                        nc.scalar.activation(silu[:, f % 2, :], ab_ps[:, f % 2, 0, 0:W], ACT.Silu).then_inc(silu_done, 1)
                    if f > 0:
                        act.wait_ge(g_done, c * FB + (f + 2))
                        if f == 1:
                            act.wait_ge(y_done, c * R + R)
                        nc.scalar.copy(g_hi[:, f - 1, :], g[:, (f - 1) % 2, :]).then_inc(ghi_done, 1)

            def split_x(c, s, i):
                if routed:
                    act.wait_ge(xT_done, c + 3)
                    nc.scalar.copy(x_hi[:, s], xT_ps[:, :, 0:W]).then_inc(xhi_done, 1)
                else:
                    act.wait_ge(hT_in[s], i * 16 + 16)
                    nc.scalar.copy(x_hi[:, s], hT[:, s]).then_inc(xhi_done, 1)

            def rows_out(c, s, i):
                act.wait_ge(y_out[s], i * (16 * R) + 16 * R)
                for j, (t, n_t) in enumerate(BLOCKS):
                    act.wait_ge(y_done, c * R + (j + 1 + R))
                    nc.scalar.copy(y_sb[0:n_t, s, j, :], y_ps[0:n_t, (s * R + j) % 2, 0:D]).then_inc(y_read, 1)

            if routed:
                act.sem_inc(y_read, 2)
                for s in range(2):
                    act.sem_inc(y_out[s], 16 * R)
            split_w13(0)
            split_w2()
            split_x(0, 0, 0)

            def group(i, is_last):
                for s in range(2):
                    c = i * 2 + s
                    gate(c, s, i)
                    if not (is_last and s == 1):
                        split_x(c + 1, 1 - s, i + s)
                    if routed and s == 1 and not is_last:
                        split_w13(i + 1)
                    if routed:
                        rows_out(c, s, i)
                    if routed and s == 1 and not is_last:
                        split_w2()

            over_groups(act, group)

        @block.vector
        def _(dve):
            dve.sem_inc(g_done, 2)
            dve.sem_inc(glo_done, 2)

            def split_w13(e):
                dve.wait_ge(w13hi_done, e + 1)
                nc.vector.tensor_tensor(w13_lo[:], w13_st[:], w13_hi[:].bitcast(F32), ALU.subtract).then_inc(w13_ready, 1)

            def split_w2(e):
                dve.wait_ge(w2hi_done, e + 1)
                nc.vector.tensor_tensor(w2_lo[:], w2_st[:], w2_hi[:].bitcast(F32), ALU.subtract).then_inc(w2_ready, 1)

            def gate(c, s):
                for f in range(FB + 1):
                    if f < FB:
                        dve.wait_ge(silu_done, c * FB + (f + 1))
                        dve.wait_ge(glo_done, c * FB + (f + 1))
                        nc.vector.tensor_tensor(g[:, f % 2, :], silu[:, f % 2, :], ab_ps[:, f % 2, 1, 0:W],
                                                ALU.mult).then_inc(g_done, 1)
                    if f > 0:
                        dve.wait_ge(ghi_done, c * FB + f)
                        nc.vector.tensor_tensor(g_lo[:, f - 1, :], g[:, (f - 1) % 2, :], g_hi[:, f - 1, :].bitcast(F32),
                                                ALU.subtract).then_inc(glo_done, 1)

            def split_x(c, s):
                dve.wait_ge(xhi_done, c + 1)
                src = xT_ps[:, :, 0:W] if routed else hT[:, s]
                nc.vector.tensor_tensor(x_lo[:, s], src, x_hi[:, s].bitcast(F32), ALU.subtract).then_inc(x_ready, 1)

            def total(c, s, i):
                gates = env.gates[:].rearrange("p (k t) -> p k t", k=TOP_K)
                at = slice(c * NB, c * NB + NB) if isinstance(c, int) else bass.ds(c * NB, NB)
                nc.vector.tensor_copy(gate8[:, s], gates[:, :, at]).then_inc(gate_step, 1)
                dve.wait_ge(base_ready, c + 1)
                dve.wait_ge(gathered[s], i * (16 * TOP_K * NB) + 16 * TOP_K * NB)
                dve.wait_ge(gate_step, c + 1)
                for k in range(TOP_K):
                    for j in range(NB):
                        last = nc.vector.scalar_tensor_tensor(out=base[:, s, j, :], in0=yg[:, s, k * NB + j, :],
                                                              scalar=gate8[:, s, k, j:j + 1], in1=base[:, s, j, :],
                                                              op0=ALU.mult, op1=ALU.add)
                    last.then_inc(acc_step, 1)
                    dve.wait_ge(acc_step, c * 2 + (k + 5))
                for j in range(NB):
                    dve.wait_ge(y_done, c * R + (j + 1 + R))
                    last = nc.vector.tensor_tensor(base[:, s, j, :], base[:, s, j, :], y_ps[:, (s * R + j) % 2, 0:D], ALU.add)
                    last.then_inc(y_read, 1)

            split_w13(0)
            split_w2(0)
            split_x(0, 0)
            if not routed:
                dve.sem_inc(y_read, 2)
                dve.sem_inc(acc_step, 4)

            def group(i, is_last):
                for s in range(2):
                    c = i * 2 + s
                    gate(c, s)
                    if not (is_last and s == 1):
                        split_x(c + 1, 1 - s)
                    if routed and s == 1 and not is_last:
                        split_w13(i + 1)
                        split_w2(i + 1)
                    if not routed:
                        total(c, s, i)

            over_groups(dve, group)

        @block.gpsimd
        def _(pool):
            def gather_tokens(c, s, i):
                pool.wait_ge(ids_in[s], i * (16 * R) + 16 * R)
                pool.wait_ge(xT_done, c + 1)
                pool.sem_inc(turnstile, 1)
                for j, (t, n_t) in enumerate(BLOCKS):
                    nc.gpsimd.indirect_dma_start(
                        out=xg[0:n_t, s, j, :], out_offset=None, in_=env.h_dram,
                        in_offset=bass.IndirectOffsetOnAxis(ap=ids[0:n_t, s, j:j + 1].bitcast(U32), axis=0),
                        compute_op=ALU.bypass).then_inc(gathered[s], 16)

            def gather_rows(c, s, i):
                slots = env.read_slot[:].rearrange("p (k t) -> p k t", k=TOP_K)
                pool.wait_ge(acc_step, c * 2 + 2)
                nc.gpsimd.tensor_copy(slot8[:, s], slots[:, :, bass.ds(c * NB, NB)]).then_inc(slots_copied, 1)
                pool.wait_ge(slots_copied, c + 1)
                pool.sem_inc(turnstile, 1)
                for k in range(TOP_K):
                    for j in range(NB):
                        nc.gpsimd.indirect_dma_start(
                            out=yg[:, s, k * NB + j, :], out_offset=None, in_=env.ye_dram,
                            in_offset=bass.IndirectOffsetOnAxis(ap=slot8[:, s, k, j:j + 1].bitcast(U32), axis=0),
                            compute_op=ALU.bypass).then_inc(gathered[s], 16)
                pool.wait_ge(base_in[s], i * 32 + 32)
                nc.gpsimd.tensor_tensor(base[:, s], base[:, s], attn[:, s], ALU.add).then_inc(base_step, 1)
                pool.wait_ge(base_step, c + 1)
                nc.gpsimd.tensor_tensor(base[:, s], base[:, s], bo[:].broadcast_to([P, NB, D]), ALU.add).then_inc(base_ready, 1)

            if routed:
                with pool.Fori(0, GROUPS) as i:
                    for s in range(2):
                        gather_tokens(i * 2 + s, s, i)
            else:
                pool.wait_ge(bo_in, 16)
                with pool.Fori(0, GROUPS) as i:
                    for s in range(2):
                        gather_rows(i * 2 + s, s, i)

        @block.sync
        def _(sp):
            def weights(e):
                w1, w3, w2 = w_views(e)
                sp.dma_start(w13_st[:, 0], w1).then_inc(w_in, 16)
                sp.dma_start(w13_st[:, 1], w3).then_inc(w_in, 16)
                sp.dma_start(w2_st[:], w2).then_inc(w_in, 16)

            def one(t, b):
                return t[b] if isinstance(b, int) else t[bass.ds(b, 1)].rearrange("o p j d -> (o p) j d")

            def rows_of(t, c, t0, n_t):
                if isinstance(c, int):
                    return t[c * W + t0:c * W + t0 + n_t, :]
                return t[bass.ds(c * W + t0, n_t), :]

            def load_ids(c, s):
                for j, (t, n_t) in enumerate(BLOCKS):
                    sp.dma_start(ids[0:n_t, s, j:j + 1], rows_of(env.ids_dram, c, t, n_t)).then_inc(ids_in[s], 16)

            def load_batch(c, s):
                sp.dma_start(hT[:, s], one(env.hT_dram, c)).then_inc(hT_in[s], 16)

            def load_base(c, s):
                sp.dma_start(base[:, s], one(env.x.rearrange("b (j p) d -> b p j d", p=P), c)).then_inc(base_in[s], 16)
                sp.dma_start(attn[:, s], one(env.attn_dram.rearrange("(b j p) d -> b p j d", p=P, j=NB), c)).then_inc(base_in[s], 16)

            weights(0)
            if routed:
                for s in range(2):
                    load_ids(s, s)
            else:
                sp.dma_start(bo[:, 0, :], env.bo.rearrange("(a d) -> a d", a=1).broadcast_to([P, D])).then_inc(bo_in, 16)
                for s in range(2):
                    load_batch(s, s)
                    load_base(s, s)

            def group(i, is_last):
                if routed and not is_last:
                    sp.wait_ge(w13_ready, i + 1)
                    sp.wait_ge(w2_ready, i + 1)
                    weights(i + 1)
                for s in range(2):
                    c = i * 2 + s
                    if routed:
                        if not is_last:
                            sp.wait_ge(gathered[s], i * (16 * R) + 16 * R)
                            load_ids(c + 2, s)
                        for j, (t, n_t) in enumerate(BLOCKS):
                            sp.wait_ge(y_read, c * R + (j + 3))
                            sp.dma_start(rows_of(env.ye_dram, c, t, n_t), y_sb[0:n_t, s, j, :]).then_inc(y_out[s], 16)
                    else:
                        if not is_last:
                            sp.wait_ge(x_ready, c + 1)
                            load_batch(c + 2, s)
                        sp.wait_ge(y_read, c * R + (R + 2))
                        sp.dma_start(one(env.out.rearrange("b (j p) d -> b p j d", p=P), c), base[:, s]).then_inc(out_out[s], 16)
                        if not is_last:
                            sp.wait_ge(out_out[s], i * 16 + 16)
                            load_base(c + 2, s)

            over_groups(sp, group)
            for s in range(2):
                if routed:
                    sp.wait_ge(y_out[s], 16 * R * (GROUPS + 1))
                else:
                    sp.wait_ge(out_out[s], 16 * GROUPS)


def transformer_layer(nc, x, Wq, Wkv, Wo, bo, ln_g, ln_b, Wr, W1, W3, W2, W1s, W3s, W2s, out):
    B, N, D = x.shape
    E, _, F = W1.shape
    NB, tokens = N // P, B * N
    CAP = -(-5 * CAPACITY_TOKENS * TOP_K // (4 * E))
    SLOTS = -(-E * CAP // P) * P
    assert N % P == 0 and D % P == 0 and B % 2 == 0 and CAP % 2 == 0

    with ExitStack() as cx:
        def sb(name, shape, dt=F32):
            return cx.enter_context(nc.sbuf_tensor(name, shape, dt))

        def dram(name, shape, dt=F32):
            return nc.dram_tensor(name, shape, dt, kind="Internal").ap()

        T = tokens // P
        env = Env(
            B=B, NB=NB, KC=D // P, D=D, E=E, F=F, DH=Wq.shape[1] // HEADS, CAP=CAP, SLOTS=SLOTS, tiles=T,
            x=x, Wq=Wq, Wkv=Wkv, Wo=Wo, bo=bo, ln_g=ln_g, ln_b=ln_b, Wr=Wr, W1=W1, W3=W3, W2=W2,
            W1s=W1s, W3s=W3s, W2s=W2s, out=out,
            xnT_dram=dram("xnT_dram", (B, P, D // P, N)), hT_dram=dram("hT_dram", (B, P, D // P, N)),
            h_dram=dram("h_dram", (tokens, D)), attn_dram=dram("attn_dram", (tokens, D)),
            ids_dram=dram("ids_dram", (SLOTS, 1), I32), ye_dram=dram("ye_dram", (E * CAP, D)),
            ident=sb("ident", [P, P]), upper=sb("upper", [P, P], BF16), ones=sb("ones", [P, P], BF16),
            causal=sb("causal", [P, 2, P]), logits=sb("logits", [P, T, E]),
            gates=sb("gates", [P, TOP_K * T]), token=sb("token", [P, TOP_K * T], I32),
            read_slot=sb("read_slot", [P, TOP_K * T], I32), write_slot=sb("write_slot", [P, TOP_K * T], I32))
        phase_constants(nc, env)
        phase_norm(nc, env)
        phase_route(nc, env)
        phase_attention(nc, env)
        phase_experts(nc, env, routed=True)
        phase_experts(nc, env, routed=False)


_INS = ["L0_attn_x", "L0_attn_Wq", "L0_attn_Wkv", "L0_attn_Wo", "L0_attn_bo", "L0_ffn_ln_g", "L0_ffn_ln_b", "L0_ffn_Wr",
        "L0_ffn_W1", "L0_ffn_W3", "L0_ffn_W2", "L0_ffn_W1s", "L0_ffn_W3s", "L0_ffn_W2s"]


def kernel(**inputs):
    import numpy as np
    import concourse.bacc as bacc
    from concourse.bass_utils import run_bass_kernel_spmd

    nc = bacc.Bacc("TRN2", target_bir_lowering=False, num_devices=1)
    arrays, args = {}, []
    for name in _INS:
        a = np.ascontiguousarray(inputs[name])
        arrays[f"in_{name}"] = a
        args.append(nc.dram_tensor(f"in_{name}", a.shape, mybir.dt.from_np(a.dtype), kind="ExternalInput").ap())
    x = arrays["in_L0_attn_x"]
    out = nc.dram_tensor("out", x.shape, mybir.dt.from_np(x.dtype), kind="ExternalOutput").ap()
    transformer_layer(nc, *args, out)
    result = run_bass_kernel_spmd(nc, [arrays], core_ids=[0])
    return result.results[0]["out"]
```

```python
from collections import namedtuple
from contextlib import ExitStack

import concourse.bass as bass
from concourse import mybir

ALU = mybir.AluOpType
ACT = mybir.ActivationFunctionType
AX_X = mybir.AxisListType.X
F32 = mybir.dt.float32
F32R = mybir.dt.float32r
BF16 = mybir.dt.bfloat16
I32 = mybir.dt.int32
U32 = mybir.dt.uint32

P = 128
HEADS = 16
LN_EPS = 1e-5
SOFTMAX_EPS = 1e-8
TOP_K = 2
CAPACITY_TOKENS = 4 * 512
LOWEST = -3.0e38

Env = namedtuple("Env", """
    B NB KC D E F DH CAP SLOTS tiles
    x Wq Wkv Wo bo ln_g ln_b Wr W1 W3 W2 W1s W3s W2s out
    xnT_dram hT_dram h_dram attn_dram ids_dram ye_dram
    ident upper ones causal logits gates token read_slot write_slot""")


def phase_constants(nc, env):
    with ExitStack() as cx:
        made = cx.enter_context(nc.semaphore("c_made"))
        block = cx.enter_context(nc.Block())

        @block.gpsimd
        def _(pool):
            nc.gpsimd.memset(env.ident[:], 0.0).then_inc(made, 1)
            nc.gpsimd.memset(env.upper[:], 1.0).then_inc(made, 1)
            nc.gpsimd.memset(env.ones[:], 1.0).then_inc(made, 1)
            nc.gpsimd.memset(env.causal[:], 0.0).then_inc(made, 1)
            pool.wait_ge(made, 4)
            nc.gpsimd.affine_select(out=env.ident[:], in_=env.ident[:], compare_op=ALU.not_equal, fill=1.0, base=0,
                                    pattern=[[-1, P]], channel_multiplier=1).then_inc(made, 1)
            nc.gpsimd.affine_select(out=env.upper[:], in_=env.upper[:], compare_op=ALU.is_ge, fill=0.0, base=0,
                                    pattern=[[1, P]], channel_multiplier=-1).then_inc(made, 1)
            nc.gpsimd.affine_select(out=env.causal[:], in_=env.causal[:], compare_op=ALU.is_ge, fill=LOWEST, base=0,
                                    pattern=[[0, 2], [-1, P]], channel_multiplier=1).then_inc(made, 1)
            pool.wait_ge(made, 7)


def phase_norm(nc, env):
    B, NB, KC, D, E = env.B, env.NB, env.KC, env.D, env.E
    N = NB * P
    with ExitStack() as cx:
        def sb(name, shape, dt=F32):
            return cx.enter_context(nc.sbuf_tensor(name, shape, dt))

        def sem(name):
            return cx.enter_context(nc.semaphore(name))

        x_sb = sb("n_x", [P, 2, NB, D])
        xn_sb = sb("n_xn", [P, 2, NB, D])
        z_sb = sb("n_z", [P, 2, NB, D])
        h_sb = sb("n_h", [P, 2, NB, D])
        xnT_sb = sb("n_xnT", [P, 2, KC, N])
        hT_sb = sb("n_hT", [P, 2, KC, N])
        g_sb = sb("n_g", [P, 1, D])
        b_sb = sb("n_b", [P, 1, D])
        wr_sb = sb("n_wr", [P, KC, E])
        stats = sb("n_stats", [P, 2, NB, 6])
        mv = sb("n_mv", [P, 2, NB, 2])
        ve = sb("n_ve", [P, 2, NB])
        sd = sb("n_sd", [P, 2, NB])
        rs = sb("n_rs", [P, 2, NB])
        tmp = sb("n_tmp", [P, 2, NB])
        xnT_ps = cx.enter_context(nc.psum_tensor("n_xnT_ps", [P, KC, N], F32))
        hT_ps = cx.enter_context(nc.psum_tensor("n_hT_ps", [P, KC, N], F32))
        lg_ps = cx.enter_context(nc.psum_tensor("n_lg_ps", [P, NB, E], F32))

        params_in = sem("n_params_in")
        x_in = [sem("n_x_in0"), sem("n_x_in1")]
        dve_step = sem("n_dve_step")
        turnstile = sem("n_turnstile")
        ve_ready = sem("n_ve_ready")
        sd_ready = sem("n_sd_ready")
        xn_ready = sem("n_xn_ready")
        z_ready = sem("n_z_ready")
        z_scaled = sem("n_z_scaled")
        h_ready = sem("n_h_ready")
        xnT_done = sem("n_xnT_done")
        hT_done = sem("n_hT_done")
        lg_done = sem("n_lg_done")
        xnT_copied = sem("n_xnT_copied")
        hT_copied = sem("n_hT_copied")
        lg_copied = sem("n_lg_copied")
        xnT_out = [sem("n_xnT_out0"), sem("n_xnT_out1")]
        hT_out = [sem("n_hT_out0"), sem("n_hT_out1")]
        h_out = [sem("n_h_out0"), sem("n_h_out1")]

        x_dram = env.x.rearrange("b (j p) d -> b p j d", p=P)
        h_dram = env.h_dram.rearrange("(b j p) d -> b p j d", p=P, j=NB)

        def one(t, b):
            return t[b] if isinstance(b, int) else t[bass.ds(b, 1)].rearrange("o p j d -> (o p) j d")

        LAST_STEP = B + 2

        def earlier(batch, n):
            k, s, half = batch
            return k - n, (s - n) % 2, half - (n - s + 1) // 2

        def exists(batch):
            return not isinstance(batch[0], int) or 0 <= batch[0] < B

        def over_steps(eng, step):
            for k in range(4):
                step((k, k % 2, k // 2))
            with eng.Fori(0, B // 2 - 2) as i:
                for s in range(2):
                    step((i * 2 + (s + 4), s, i + 2))
            for k in range(B, LAST_STEP + 1):
                step((k, k % 2, k // 2))

        block = cx.enter_context(nc.Block())

        @block.sync
        def _(sp):
            for src, dst in ((env.ln_g, g_sb), (env.ln_b, b_sb)):
                row = src.rearrange("(a d) -> a d", a=1).broadcast_to([P, D])
                sp.dma_start(dst[:, 0, :], row).then_inc(params_in, 16)
            sp.dma_start(wr_sb[:], env.Wr.rearrange("(c p) e -> p c e", p=P)).then_inc(params_in, 16)
            for s in range(2):
                sp.dma_start(x_sb[:, s], x_dram[s]).then_inc(x_in[s], 16)

            def stores(k, s):
                sp.wait_ge(xnT_copied, k + 2)
                sp.dma_start(one(env.xnT_dram, k), xnT_sb[:, s]).then_inc(xnT_out[s], 16)
                sp.wait_ge(h_ready, k + 3)
                sp.dma_start(one(h_dram, k), h_sb[:, s]).then_inc(h_out[s], 16)
                sp.wait_ge(hT_copied, k + 2)
                sp.dma_start(one(env.hT_dram, k), hT_sb[:, s]).then_inc(hT_out[s], 16)

            with sp.Fori(0, B // 2 - 1) as i:
                for s in range(2):
                    sp.wait_ge(xn_ready, i * 2 + (s + 1))
                    sp.dma_start(x_sb[:, s], one(x_dram, i * 2 + (s + 2))).then_inc(x_in[s], 16)
                    stores(i * 2 + s, s)
            for s in range(2):
                stores(B - 2 + s, s)
            for s in range(2):
                for q in (xnT_out, h_out, hT_out):
                    sp.wait_ge(q[s], 16 * (B // 2) + 16)

        @block.vector
        def _(dve):
            PER = 4 * NB + 5
            FIRST = 2 * NB + 5

            def step(batch):
                k, s, half = batch
                _, before, _ = earlier(batch, 1)
                both = [n for n, b in enumerate((batch, earlier(batch, 1))) if exists(b)]
                if not both:
                    return
                sel = slice(both[0], both[-1] + 1)
                c = k * PER + (FIRST - PER) if not isinstance(k, int) or k > 0 else 0
                src = (x_sb[:, s], xn_sb[:, before])
                dst = (xn_sb[:, s], z_sb[:, before])
                if 0 in both:
                    dve.wait_ge(x_in[s], half * 16 + 16)
                n_rows = NB * len(both)
                for n in both:
                    if n == 1:
                        dve.wait_ge(xn_ready, k)
                    for j in range(NB):
                        nc.vector.bn_stats(stats[:, n, j, :], src[n][:, j, :]).then_inc(dve_step, 1)
                dve.wait_ge(dve_step, c + n_rows)
                if not isinstance(k, int) or k > 1:
                    dve.wait_ge(z_ready, k - 1)
                dve.sem_inc(turnstile, 1)
                for n in both:
                    for j in range(NB):
                        nc.vector.bn_aggr(mv[:, n, j, :], stats[:, n, j, :]).then_inc(dve_step, 1)
                dve.wait_ge(dve_step, c + 2 * n_rows)
                nc.vector.tensor_scalar(ve[:, sel], mv[:, sel, :, 1], LN_EPS, None, ALU.add).then_inc(ve_ready, 1)
                dve.wait_ge(sd_ready, k + 1)
                nc.vector.reciprocal(rs[:, sel], sd[:, sel]).then_inc(dve_step, 1)
                dve.wait_ge(dve_step, c + (2 * n_rows + 1))
                nc.vector.tensor_tensor(tmp[:, sel], ve[:, sel], rs[:, sel], ALU.mult).then_inc(dve_step, 1)
                dve.wait_ge(dve_step, c + (2 * n_rows + 2))
                nc.vector.tensor_tensor(tmp[:, sel], tmp[:, sel], rs[:, sel], ALU.mult).then_inc(dve_step, 1)
                dve.wait_ge(dve_step, c + (2 * n_rows + 3))
                nc.vector.tensor_scalar(tmp[:, sel], tmp[:, sel], -0.5, 1.5, ALU.mult, ALU.add).then_inc(dve_step, 1)
                dve.wait_ge(dve_step, c + (2 * n_rows + 4))
                nc.vector.tensor_tensor(rs[:, sel], rs[:, sel], tmp[:, sel], ALU.mult).then_inc(dve_step, 1)
                dve.wait_ge(dve_step, c + (2 * n_rows + 5))
                for n in both:
                    dve.wait_ge(*((xnT_done, k + 1) if n == 0 else (h_ready, k)))
                    for j in range(NB):
                        last = nc.vector.tensor_scalar(dst[n][:, j, :], src[n][:, j, :], mv[:, n, j, 0:1], rs[:, n, j:j + 1],
                                                       ALU.subtract, ALU.mult)
                    last.then_inc((xn_ready, z_ready)[n], 1)

            over_steps(dve, step)
            dve.wait_ge(z_ready, B)

        @block.scalar
        def _(act):
            act.sem_inc(xnT_copied, 1)
            act.sem_inc(hT_copied, 1)
            act.sem_inc(lg_copied, 1)
            for s in range(2):
                act.sem_inc(xnT_out[s], 16)
                act.sem_inc(hT_out[s], 16)

            def step(batch):
                k = batch[0]
                if exists(turned := earlier(batch, 1)):
                    k1, s, half = turned
                    act.wait_ge(xnT_done, k1 + 3)
                    act.wait_ge(xnT_out[s], half * 16 + 16)
                    nc.scalar.copy(xnT_sb[:, s], xnT_ps[:]).then_inc(xnT_copied, 1)
                if exists(scored := earlier(batch, 3)):
                    k3 = scored[0]
                    act.wait_ge(lg_done, k3 + 3)
                    at = slice(k3 * NB, k3 * NB + NB) if isinstance(k3, int) else bass.ds(k3 * NB, NB)
                    nc.scalar.copy(env.logits[:, at, :], lg_ps[:]).then_inc(lg_copied, 1)
                both = [n for n in range(2) if exists(earlier(batch, n))]
                if both:
                    sel = slice(both[0], both[-1] + 1)
                    act.wait_ge(ve_ready, k + 1)
                    nc.scalar.activation(sd[:, sel], ve[:, sel], ACT.Sqrt).then_inc(sd_ready, 1)
                if exists(hidden := earlier(batch, 2)):
                    k2, s, half = hidden
                    act.wait_ge(hT_done, k2 + 3)
                    act.wait_ge(hT_out[s], half * 16 + 16)
                    act.wait_ge(lg_done, k2 + 1)
                    nc.scalar.copy(hT_sb[:, s], hT_ps[:]).then_inc(hT_copied, 1)

            over_steps(act, step)

        @block.gpsimd
        def _(pool):
            pool.sem_inc(h_ready, 2)
            for s in range(2):
                pool.sem_inc(h_out[s], 16)
            g_row, b_row = g_sb[:].broadcast_to([P, NB, D]), b_sb[:].broadcast_to([P, NB, D])
            pool.wait_ge(params_in, 48)
            with pool.Fori(0, B // 2) as i:
                for s in range(2):
                    k = i * 2 + s
                    pool.wait_ge(z_ready, k + 1)
                    nc.gpsimd.tensor_tensor(z_sb[:, s], z_sb[:, s], g_row, ALU.mult).then_inc(z_scaled, 1)
                    pool.wait_ge(z_scaled, k + 1)
                    pool.wait_ge(h_out[s], i * 16 + 16)
                    pool.wait_ge(hT_done, k + 1)
                    nc.gpsimd.tensor_tensor(h_sb[:, s], z_sb[:, s], b_row, ALU.add).then_inc(h_ready, 1)

        @block.tensor
        def _(pe):
            pe.sem_inc(xnT_done, 2)
            pe.sem_inc(hT_done, 2)
            pe.sem_inc(lg_done, 2)
            pe.wait_ge(params_in, 48)

            def transposes(dst, src):
                for c in range(KC):
                    for j in range(NB):
                        last = nc.tensor.transpose(dst[:, c, j * P:(j + 1) * P], src[:, j, c * P:(c + 1) * P],
                                                   env.ident[:])
                return last

            def step(batch):
                if exists(batch):
                    k, s, _ = batch
                    pe.wait_ge(xn_ready, k + 1)
                    pe.wait_ge(xnT_copied, k + 1)
                    transposes(xnT_ps, xn_sb[:, s]).then_inc(xnT_done, 1)
                if exists(hidden := earlier(batch, 1)):
                    k, s, _ = hidden
                    pe.wait_ge(h_ready, k + 3)
                    pe.wait_ge(hT_copied, k + 1)
                    transposes(hT_ps, h_sb[:, s]).then_inc(hT_done, 1)
                    pe.wait_ge(hT_copied, k + 2)
                    pe.wait_ge(lg_copied, k + 1)
                    for j in range(NB):
                        for c in range(KC):
                            last = nc.tensor.matmul(lg_ps[:, j, :], hT_sb[:, s, c, j * P:(j + 1) * P], wr_sb[:, c, :],
                                                    start=c == 0, stop=c == KC - 1)
                    last.then_inc(lg_done, 1)

            over_steps(pe, step)


def phase_route(nc, env):
    T, E, CAP = env.tiles, env.E, env.CAP
    with ExitStack() as cx:
        def sb(name, shape, dt=F32):
            return cx.enter_context(nc.sbuf_tensor(name, shape, dt))

        weight = sb("r_weight", [P, T, E])
        ebase = sb("r_ebase", [P, TOP_K * T, E])
        onehot = sb("r_onehot", [P, TOP_K * T, E])
        onehot16 = sb("r_onehot16", [P, TOP_K * T, E], BF16)
        a = sb("r_a", [P, T, E])
        b = sb("r_b", [P, T, E])
        rest = sb("r_rest", [P, T, E])
        top = sb("r_top", [P, TOP_K, T])
        mark = sb("r_mark", [P, T])
        run = sb("r_run", [P, 2, TOP_K * T, E])
        totals = sb("r_totals", [P, TOP_K * T, E])
        place = sb("r_place", [P, TOP_K * T, E])
        pos = sb("r_pos", [P, TOP_K * T])
        start = sb("r_start", [P, TOP_K * T])
        kept = sb("r_kept", [P, TOP_K * T])
        slot = sb("r_slot", [P, TOP_K * T])
        diff = sb("r_diff", [P, T])
        gate = sb("r_gate", [P, TOP_K, T])
        zero_ids = sb("r_zero_ids", [P, env.SLOTS // P], I32)
        W = TOP_K * T * E // 2
        within_ps = cx.enter_context(nc.psum_tensor("r_within_ps", [P, 2, 512], F32))
        totals_ps = cx.enter_context(nc.psum_tensor("r_totals_ps", [P, 2, 512], F32))

        step = cx.enter_context(nc.semaphore("r_step"))
        iotas = cx.enter_context(nc.semaphore("r_iotas"))
        zeroed = cx.enter_context(nc.semaphore("r_zeroed"))
        onehot_ready = cx.enter_context(nc.semaphore("r_onehot_ready"))
        counted = cx.enter_context(nc.semaphore("r_counted"))
        diff_ready = cx.enter_context(nc.semaphore("r_diff_ready"))
        exp_ready = cx.enter_context(nc.semaphore("r_exp_ready"))
        block = cx.enter_context(nc.Block())

        @block.gpsimd
        def _(pool):
            nc.gpsimd.iota(weight[:], [[0, T], [-1, E]], base=E, channel_multiplier=0,
                           allow_small_or_imprecise_dtypes=True).then_inc(iotas, 1)
            nc.gpsimd.iota(ebase[:], [[0, TOP_K * T], [CAP, E]], base=0, channel_multiplier=0,
                           allow_small_or_imprecise_dtypes=True).then_inc(iotas, 1)
            nc.gpsimd.iota(env.token[:], [[0, TOP_K], [P, T]], base=0, channel_multiplier=1).then_inc(iotas, 1)
            nc.gpsimd.memset(zero_ids[:], 0).then_inc(iotas, 1)
            pool.wait_ge(iotas, 4)

        @block.sync
        def _(sp):
            sp.wait_ge(iotas, 4)
            sp.dma_start(env.ids_dram.rearrange("(p c) o -> p (c o)", p=P), zero_ids[:]).then_inc(zeroed, 16)
            sp.wait_ge(zeroed, 16)

        @block.scalar
        def _(act):
            act.wait_ge(diff_ready, 1)
            nc.scalar.activation(gate[:, 1, :], diff[:], ACT.Exp).then_inc(exp_ready, 1)

        @block.tensor
        def _(pe):
            pe.wait_ge(onehot_ready, 1)
            flat = onehot16[:].rearrange("p t e -> p (t e)")
            for half in range(2):
                cols = slice(half * W, half * W + W)
                nc.tensor.matmul(within_ps[:, half, 0:W], env.upper[:], flat[:, cols], start=True, stop=True)
                last = nc.tensor.matmul(totals_ps[:, half, 0:W], env.ones[:], flat[:, cols], start=True, stop=True)
            last.then_inc(counted, 1)

        @block.vector
        def _(dve):
            n = [0]

            def done(ins):
                n[0] += 1
                ins.then_inc(step, 1)
                dve.wait_ge(step, n[0])

            def per_token(t):
                return t.unsqueeze(2).broadcast_to([P, t.shape[1], E])

            def choose(logits, k):
                rows = slice(k * T, k * T + T)
                done(nc.vector.tensor_reduce(top[:, k, :], logits, AX_X, ALU.max))
                done(nc.vector.tensor_tensor(a[:], logits, per_token(top[:, k, :]), ALU.is_equal))
                done(nc.vector.tensor_tensor(a[:], a[:], weight[:], ALU.mult))
                done(nc.vector.tensor_reduce(mark[:], a[:], AX_X, ALU.max))
                done(nc.vector.tensor_tensor(onehot[:, rows, :], weight[:], per_token(mark[:]), ALU.is_equal))

            dve.wait_ge(iotas, 4)
            choose(env.logits[:], 0)
            done(nc.vector.tensor_scalar(b[:], onehot[:, 0:T, :], LOWEST, None, ALU.mult))
            done(nc.vector.tensor_tensor(rest[:], env.logits[:], b[:], ALU.add))
            choose(rest[:], 1)
            nc.vector.tensor_copy(onehot16[:], onehot[:]).then_inc(onehot_ready, 1)
            nc.vector.tensor_tensor(diff[:], top[:, 1, :], top[:, 0, :], ALU.subtract).then_inc(diff_ready, 1)

            dve.wait_ge(exp_ready, 1)
            done(nc.vector.tensor_scalar(mark[:], gate[:, 1, :], 1.0, None, ALU.add))
            done(nc.vector.reciprocal(gate[:, 0, :], mark[:]))
            done(nc.vector.tensor_tensor(gate[:, 1, :], gate[:, 1, :], gate[:, 0, :], ALU.mult))

            dve.wait_ge(counted, 1)

            def halves(t):
                return t.rearrange("p (h t) e -> p h (t e)", h=2)

            done(nc.vector.tensor_copy(halves(totals[:]), totals_ps[:, :, 0:W]))
            src, reach, i = totals[:], 1, 0
            while reach < TOP_K * T:
                dst = run[:, i % 2]
                done(nc.vector.tensor_copy(dst[:, 0:reach, :], src[:, 0:reach, :]))
                done(nc.vector.tensor_tensor(dst[:, reach:, :], src[:, reach:, :], src[:, :TOP_K * T - reach, :], ALU.add))
                src, reach, i = dst, reach * 2, i + 1
            done(nc.vector.tensor_tensor(place[:], src, totals[:], ALU.subtract))
            done(nc.vector.tensor_tensor(halves(place[:]), halves(place[:]), within_ps[:, :, 0:W], ALU.add))
            done(nc.vector.tensor_tensor(place[:], place[:], onehot[:], ALU.mult))
            done(nc.vector.tensor_reduce(pos[:], place[:], AX_X, ALU.add))
            done(nc.vector.tensor_scalar(pos[:], pos[:], -1.0, None, ALU.add))
            done(nc.vector.tensor_tensor(ebase[:], ebase[:], onehot[:], ALU.mult))
            done(nc.vector.tensor_reduce(start[:], ebase[:], AX_X, ALU.add))
            done(nc.vector.tensor_scalar(kept[:], pos[:], float(CAP), None, ALU.is_lt))
            done(nc.vector.tensor_tensor(env.gates[:], gate[:].rearrange("p k t -> p (k t)"), kept[:], ALU.mult))
            done(nc.vector.tensor_scalar(slot[:], pos[:], float(CAP - 1), None, ALU.min))
            done(nc.vector.tensor_tensor(slot[:], slot[:], start[:], ALU.add))
            done(nc.vector.tensor_copy(env.read_slot[:], slot[:]))
            done(nc.vector.tensor_scalar(kept[:], kept[:], -float(env.SLOTS), float(env.SLOTS), ALU.mult, ALU.add))
            done(nc.vector.tensor_tensor(slot[:], slot[:], kept[:], ALU.add))
            done(nc.vector.tensor_copy(env.write_slot[:], slot[:]))


def split_weights(nc, jobs):
    with ExitStack() as cx:
        stages = [cx.enter_context(nc.sbuf_tensor(f"w_stage{n}", shape, F32)) for n, (_, _, _, shape) in enumerate(jobs)]
        loaded = [cx.enter_context(nc.semaphore(f"w_loaded{n}")) for n in range(len(jobs))]
        hi_done = cx.enter_context(nc.semaphore("w_hi_done"))
        lo_done = cx.enter_context(nc.semaphore("w_lo_done"))
        block = cx.enter_context(nc.Block())

        @block.sync
        def _(sp):
            for n, (_, _, src, _) in enumerate(jobs):
                sp.dma_start(stages[n][:], src).then_inc(loaded[n], 16)

        @block.scalar
        def _(act):
            for n, (hi, _, _, _) in enumerate(jobs):
                act.wait_ge(loaded[n], 16)
                nc.scalar.copy(hi, stages[n][:]).then_inc(hi_done, 1)

        @block.vector
        def _(dve):
            for n, (hi, lo, _, _) in enumerate(jobs):
                dve.wait_ge(hi_done, n + 1)
                nc.vector.tensor_tensor(lo, stages[n][:], hi.bitcast(F32), ALU.subtract).then_inc(lo_done, 1)
            dve.wait_ge(lo_done, len(jobs))


def phase_attention(nc, env):
    B, NB, KC, D, DH = env.B, env.NB, env.KC, env.D, env.DH
    N = NB * P
    PAIRS = HEADS // 2
    UNITS = PAIRS * NB
    INNER = HEADS * DH
    SCALE = float(DH) ** -0.5
    S_RING, P_RING = 2, 4
    STACKS = 16 * 8

    with ExitStack() as cx:
        def sb(name, shape, dt=F32):
            return cx.enter_context(nc.sbuf_tensor(name, shape, dt))

        def sem(name):
            return cx.enter_context(nc.semaphore(name))

        w_hi = sb("a_w_hi", [P, 3, KC, INNER], F32R)
        w_lo = sb("a_w_lo", [P, 3, KC, INNER], F32R)
        wo_hi = sb("a_wo_hi", [P, PAIRS, D], F32R)
        wo_lo = sb("a_wo_lo", [P, PAIRS, D], F32R)
        wkv = env.Wkv.rearrange("(c p) (m n) -> m p c n", p=P, m=2)
        split_weights(nc, [(w_hi[:, 0], w_lo[:, 0], env.Wq.rearrange("(c p) n -> p c n", p=P), [P, KC, INNER]),
                           (w_hi[:, 1], w_lo[:, 1], wkv[0], [P, KC, INNER]),
                           (w_hi[:, 2], w_lo[:, 2], wkv[1], [P, KC, INNER]),
                           (wo_hi[:], wo_lo[:], env.Wo.rearrange("(r p) n -> p r n", p=P), [P, PAIRS, D])])

        x_sb = sb("a_x", [P, KC, N])
        x_hi = sb("a_x_hi", [P, KC, N], F32R)
        x_lo = sb("a_x_lo", [P, KC, N], F32R)
        v_sb = sb("a_v", [P, 2, NB, 2 * P])
        nat = {m: sb(f"a_{m}_halves", [P, 2, N], F32R) for m in "qk"}
        q_st = sb("a_q_stack", [P, 2, 2, N], F32R)
        k_st = sb("a_k_stack", [P, 2, 2, 2, N], F32R)
        probs = sb("a_probs", [P, P_RING, 2, N])
        pT = sb("a_pT", [P, 2, 2, NB, N])
        o_hi = sb("a_o_hi", [P, PAIRS, N], F32R)
        o_lo = sb("a_o_lo", [P, PAIRS, N], F32R)
        ao = sb("a_ao", [P, NB, D])
        nmax = sb("a_nmax", [P, P_RING, 2])
        den = sb("a_den", [P, P_RING, 2])
        rden = sb("a_rden", [P, P_RING, 2])
        ids8 = sb("a_ids8", [P, TOP_K, NB], I32)
        slot8 = sb("a_slot8", [P, TOP_K, NB], I32)
        s_ps = cx.enter_context(nc.psum_tensor("a_s_ps", [P, S_RING, 2, N], F32))
        pt_ps = cx.enter_context(nc.psum_tensor("a_pt_ps", [P, 2, N], F32))
        ot_ps = cx.enter_context(nc.psum_tensor("a_ot_ps", [P, N], F32))
        pj_ps = cx.enter_context(nc.psum_tensor("a_pj_ps", [P, N], F32))

        turnstile = sem("a_turnstile")
        x_in = sem("a_x_in")
        xhi_done = sem("a_xhi_done")
        x_split = sem("a_x_split")
        pj_done = sem("a_pj_done")
        pj_evac = sem("a_pj_evac")
        hi_done = sem("a_hi_done")
        stacked = [sem("a_stacked0"), sem("a_stacked1")]
        s_done = sem("a_s_done")
        max_done = sem("a_max_done")
        masked = sem("a_masked")
        exp_done = sem("a_exp_done")
        den_step = sem("a_den_step")
        rden_ready = sem("a_rden_ready")
        normed = sem("a_normed")
        pt_done = sem("a_pt_done")
        pt_evac = sem("a_pt_evac")
        ot_done = sem("a_ot_done")
        ohi_done = sem("a_ohi_done")
        ot_evac = sem("a_ot_evac")
        ao_out = sem("a_ao_out")
        slots_copied = sem("a_slots_copied")
        scattered = sem("a_scattered")

        def piece_at(u):
            p, qb = divmod(u, NB)
            if qb == 2:
                return ("q", p + 2, 0)
            if qb == 3:
                return ("k", p + 2, 0)
            if p % 2 == 1:
                return ("v", (p + 1) // 2, qb)
            return None

        AHEAD = [("q", 0, 0), ("k", 0, 0), ("v", 0, 0), ("v", 0, 1), ("q", 1, 0), ("k", 1, 0)]
        USES = len([u for u in range(UNITS) if piece_at(u)]) + 1
        PT_USES = UNITS + 1
        order = [u for u in range(UNITS) if piece_at(u)]
        QK = 2 * PAIRS

        def of_next(piece):
            return piece[1] >= (PAIRS // 2 if piece[0] == "v" else PAIRS)

        def uses_before(b, u):
            return b * USES + (len(AHEAD) + len([v for v in order if v < u]))

        def highs_before(b, u):
            return b * QK + (4 + len([v for v in order if v < u and piece_at(v)[0] in "qk"]))

        def over_batches(eng, batch):
            with eng.Fori(0, B - 1) as b:
                batch(b, False)
            batch(B - 1, True)

        block = cx.enter_context(nc.Block())

        @block.tensor
        def _(pe):
            pe.sem_inc(pt_done, P_RING)
            pe.sem_inc(ot_done, 2)

            def project(piece, used, batches):
                kind, which, part = piece
                pe.wait_ge(x_split, batches)
                if not isinstance(used, int) or used > 0:
                    pe.wait_ge(pj_evac, used)
                if kind in "qk":
                    m, r = "qk".index(kind), which % PAIRS
                    passes = [(w, x, c) for c in range(KC) for w, x in ((w_hi, x_hi), (w_hi, x_lo), (w_lo, x_hi))]
                    for n, (w, x, c) in enumerate(passes):
                        last = nc.tensor.matmul(pj_ps[:], w[:, m, c, r * P:(r + 1) * P], x[:, c, :],
                                                start=n == 0, stop=n == len(passes) - 1)
                else:
                    g = which % (PAIRS // 2)
                    passes = [(w, x, c) for c in range(KC) for w, x in ((w_hi, x_hi), (w_lo, x_hi), (w_hi, x_lo))]
                    for j in range(2):
                        t = 2 * part + j
                        for n, (w, x, c) in enumerate(passes):
                            last = nc.tensor.matmul(pj_ps[:, j * 2 * P:(j + 1) * 2 * P], x[:, c, t * P:(t + 1) * P],
                                                    w[:, 2, c, g * 2 * P:(g + 1) * 2 * P],
                                                    start=n == 0, stop=n == len(passes) - 1)
                last.then_inc(pj_done, 1)

            def scores(b, u):
                p, qb = divmod(u, NB)
                if not (isinstance(b, int) and u < S_RING and b == 0):
                    pe.wait_ge(exp_done, b * UNITS + (u - S_RING + 1))
                if qb == 0:
                    pe.wait_ge(stacked[p % 2], b * (STACKS * PAIRS // 2) + STACKS * (p // 2 + 1))
                for h in range(2):
                    lhsT = q_st[:, p % 2, h, qb * P:(qb + 1) * P]
                    nc.tensor.matmul(s_ps[:, u % S_RING, h, :], lhsT, k_st[:, p % 2, h, 0, :], start=True, stop=False)
                    last = nc.tensor.matmul(s_ps[:, u % S_RING, h, :], lhsT, k_st[:, p % 2, h, 1, :], start=False, stop=True)
                last.then_inc(s_done, 1)

            def turn(b, u):
                qb = u % NB
                pe.wait_ge(normed, b * UNITS + (u + 1))
                pe.wait_ge(pt_evac, b * PT_USES + (u + 1))
                for h in range(2):
                    for k in range(qb + 1):
                        last = nc.tensor.transpose(pt_ps[:, h, k * P:(k + 1) * P], probs[:, u % P_RING, h, k * P:(k + 1) * P],
                                                   env.ident[:])
                last.then_inc(pt_done, 1)

            def values(b, p, ks):
                if ks[0] == 0:
                    pe.wait_ge(pt_evac, b * PT_USES + (NB * p + NB - 1 + 2))
                    pe.wait_ge(pj_evac, uses_before(b, 2 * NB * (p // 2)))
                    pe.wait_ge(ot_evac, b * PAIRS + (p + 1))
                for k in ks:
                    for h in range(2):
                        col = (p % 2) * P + h * DH
                        last = nc.tensor.matmul(ot_ps[h * DH:(h + 1) * DH, k * P:N],
                                                v_sb[:, (p // 2) % 2, k, col:col + DH], pT[:, p % 2, h, k, k * P:N],
                                                start=k == 0, stop=k == NB - 1)
                if ks[-1] == NB - 1:
                    last.then_inc(ot_done, 1)

            def out_project(bank, tiles, pairs):
                passes = [(o, w) for o, w in ((o_hi, wo_hi), (o_hi, wo_lo), (o_lo, wo_hi))]
                for j, t in enumerate(tiles):
                    for r in pairs:
                        for n, (o, w) in enumerate(passes):
                            last = nc.tensor.matmul(bank[:, j * D:(j + 1) * D], o[:, r, t * P:(t + 1) * P], w[:, r, :],
                                                    start=j == 0 and r == 0 and n == 0,
                                                    stop=r == PAIRS - 1 and n == len(passes) - 1, skip_group_check=True)
                return last

            for n, piece in enumerate(AHEAD):
                project(piece, n, 1)
            scores(0, 0)
            scores(0, 1)

            def batch(b, is_last):
                for u in range(UNITS):
                    p, qb = divmod(u, NB)
                    if u + S_RING < UNITS or not is_last:
                        scores(b, u + S_RING)
                    if u > 0:
                        turn(b, u - 1)
                    piece = piece_at(u)
                    if piece and not (is_last and of_next(piece)):
                        project(piece, uses_before(b, u), b + 1 + of_next(piece))
                    if p > 0 and qb in (1, 2):
                        values(b, p - 1, (2 * qb - 2, 2 * qb - 1))
                turn(b, UNITS - 1)
                uses = uses_before(b, UNITS) - (len([u for u in order if of_next(piece_at(u))]) if is_last else 0)
                pe.wait_ge(pj_evac, uses)
                pe.wait_ge(ot_evac, b * PAIRS + PAIRS)
                out_project(pj_ps, (0, 1), range(PAIRS - 1))
                values(b, PAIRS - 1, (0, 1, 2, 3))
                pe.wait_ge(pt_evac, b * PT_USES + (UNITS + 1))
                out_project(pt_ps[:, 0, :], (2, 3), range(PAIRS - 1))
                pe.wait_ge(ot_evac, b * PAIRS + (PAIRS + 1))
                out_project(pj_ps, (0, 1), (PAIRS - 1,)).then_inc(pj_done, 1)
                out_project(pt_ps[:, 0, :], (2, 3), (PAIRS - 1,)).then_inc(pt_done, 1)

            over_batches(pe, batch)

        @block.vector
        def _(dve):
            dve.sem_inc(ot_evac, 1)

            def split_x(batches):
                dve.wait_ge(xhi_done, batches)
                nc.vector.tensor_tensor(x_lo[:], x_sb[:], x_hi[:].bitcast(F32), ALU.subtract).then_inc(x_split, 1)

            def low(piece, highs):
                kind, which, part = piece
                if kind == "v":
                    return
                hi, lo = nat[kind][:, 0, :], nat[kind][:, 1, :]
                dve.wait_ge(hi_done, highs + 1)
                if kind == "q":
                    nc.vector.scalar_tensor_tensor(out=lo, in0=pj_ps[:], scalar=SCALE, in1=hi.bitcast(F32),
                                                   op0=ALU.mult, op1=ALU.subtract).then_inc(pj_evac, 1)
                else:
                    nc.vector.tensor_tensor(lo, pj_ps[:], hi.bitcast(F32), ALU.subtract).then_inc(pj_evac, 1)

            def maxima(b, u):
                dve.wait_ge(s_done, b * UNITS + (u + 1))
                nc.vector.tensor_reduce(nmax[:, u % P_RING, :], s_ps[:, u % S_RING], AX_X, ALU.max, negate=True)\
                    .then_inc(max_done, 1)

            def mask(b, u):
                qb = u % NB
                dve.wait_ge(max_done, b * UNITS + (u + 1))
                diagonal = s_ps[:, u % S_RING, :, qb * P:(qb + 1) * P]
                nc.vector.tensor_tensor(diagonal, diagonal, env.causal[:], ALU.add).then_inc(masked, 1)

            def add_eps(b, u):
                dve.wait_ge(exp_done, b * UNITS + (u + 1))
                d = den[:, u % P_RING, :]
                nc.vector.tensor_scalar(d, d, SOFTMAX_EPS, None, ALU.add).then_inc(den_step, 1)

            def invert(b, u):
                dve.wait_ge(den_step, b * UNITS + (u + 1))
                nc.vector.reciprocal(rden[:, u % P_RING, :], den[:, u % P_RING, :]).then_inc(rden_ready, 1)

            def normalise(b, u):
                dve.wait_ge(rden_ready, b * UNITS + (u + 1))
                for h in range(2):
                    pr = probs[:, u % P_RING, h, 0:(u % NB + 1) * P]
                    last = nc.vector.tensor_scalar(pr, pr, rden[:, u % P_RING, h:h + 1], None, ALU.mult)
                last.then_inc(normed, 1)

            def output_low(b, p):
                dve.wait_ge(ohi_done, b * PAIRS + (p + 1))
                nc.vector.tensor_tensor(o_lo[:, p, :], ot_ps[:], o_hi[:, p, :].bitcast(F32), ALU.subtract).then_inc(ot_evac, 1)

            split_x(1)
            highs = 0
            for n, piece in enumerate(AHEAD):
                low(piece, highs)
                highs += piece[0] != "v"
            for u in range(S_RING):
                maxima(0, u)
                mask(0, u)
            for step in (add_eps, invert, normalise):
                step(0, 0)

            def batch(b, is_last):
                for u in range(UNITS):
                    p, qb = divmod(u, NB)
                    scored = u + S_RING < UNITS or not is_last
                    summed = u + 1 < UNITS or not is_last
                    if scored:
                        maxima(b, u + S_RING)
                    if summed:
                        add_eps(b, u + 1)
                    if scored:
                        mask(b, u + S_RING)
                    if summed:
                        invert(b, u + 1)
                    piece = piece_at(u)
                    if piece and not (is_last and of_next(piece)):
                        low(piece, highs_before(b, u))
                    if summed:
                        normalise(b, u + 1)
                    if p > 0 and qb == 3:
                        output_low(b, p - 1)
                    if u == UNITS - 2 * NB and not is_last:
                        split_x(b + 2)
                output_low(b, PAIRS - 1)
                uses = uses_before(b, UNITS) - (len([u for u in order if of_next(piece_at(u))]) if is_last else 0)
                dve.wait_ge(pj_done, uses + 1)
                dve.wait_ge(ao_out, b * 16 + 16)
                nc.vector.tensor_copy(ao[:, 0:2, :], pj_ps[:].rearrange("p (j n) -> p j n", j=2)).then_inc(pj_evac, 1)

            over_batches(dve, batch)

        @block.scalar
        def _(act):
            act.sem_inc(pt_evac, 1)

            def split_x(batches, pj):
                act.wait_ge(x_in, batches * 16)
                if pj is not None:
                    act.wait_ge(pj_done, pj)
                nc.scalar.copy(x_hi[:], x_sb[:]).then_inc(xhi_done, 1)

            def high(piece, used, stack_before, b):
                kind, which, part = piece
                act.wait_ge(pj_done, used + 1)
                if kind == "v":
                    if b is not None:
                        act.wait_ge(ot_done, b * PAIRS + 2 * which)
                    dst = v_sb[:, which % 2, 2 * part:2 * part + 2, :]
                    nc.scalar.copy(dst, pj_ps[:].rearrange("p (j n) -> p j n", j=2)).then_inc(pj_evac, 1)
                    return
                if stack_before is not None:
                    act.wait_ge(*stack_before)
                nc.scalar.activation(nat[kind][:, 0, :], pj_ps[:], ACT.Copy, scale=SCALE if kind == "q" else 1.0)\
                    .then_inc(hi_done, 1)

            def exps(b, u):
                qb = u % NB
                act.wait_ge(masked, b * UNITS + (u + 1))
                if u >= P_RING:
                    act.wait_ge(pt_done, b * PT_USES + (u + 1))
                elif not (isinstance(b, int) and b == 0 and u < S_RING):
                    act.wait_ge(pt_done, b * PT_USES + u)
                n = (qb + 1) * P
                for h in range(2):
                    last = nc.scalar.activation(probs[:, u % P_RING, h, 0:n], s_ps[:, u % S_RING, h, 0:n], ACT.Exp,
                                                bias=nmax[:, u % P_RING, h:h + 1], accum_out=den[:, u % P_RING, h:h + 1])
                last.then_inc(exp_done, 1)

            def turned(b, u):
                p, qb = divmod(u, NB)
                act.wait_ge(pt_done, b * PT_USES + (u + 1 + P_RING))
                if qb == 0:
                    act.wait_ge(ot_done, b * PAIRS + (p + 1))
                src = pt_ps[:, :, 0:(qb + 1) * P].rearrange("p h (k q) -> p h k q", q=P)
                nc.scalar.copy(pT[:, p % 2, :, 0:qb + 1, qb * P:(qb + 1) * P], src).then_inc(pt_evac, 1)

            def output_high(b, p):
                act.wait_ge(ot_done, b * PAIRS + (p + 3))
                if p == 0:
                    act.wait_ge(pt_done, b * PT_USES + P_RING)
                nc.scalar.copy(o_hi[:, p, :], ot_ps[:]).then_inc(ohi_done, 1)

            split_x(1, None)
            for n, piece in enumerate(AHEAD):
                high(piece, n, (stacked[0], STACKS) if piece[1] == 1 and piece[0] in "qk" else None, None)
            exps(0, 0)
            exps(0, 1)

            def batch(b, is_last):
                for u in range(UNITS):
                    p, qb = divmod(u, NB)
                    if u > 0:
                        turned(b, u - 1)
                    piece = piece_at(u)
                    if piece and not (is_last and of_next(piece)):
                        high(piece, uses_before(b, u), (stacked[(p + 1) % 2], b * (STACKS * PAIRS // 2) + STACKS * ((p + 1) // 2 + 1)), b)
                    if u + S_RING < UNITS or not is_last:
                        exps(b, u + S_RING)
                    if p > 0 and qb == 2:
                        output_high(b, p - 1)
                    if u == UNITS - 2 * NB and not is_last:
                        split_x(b + 2, uses_before(b, UNITS - 2 * NB))
                turned(b, UNITS - 1)
                output_high(b, PAIRS - 1)
                act.wait_ge(pt_done, b * PT_USES + (PT_USES + P_RING))
                act.wait_ge(ao_out, b * 16 + 16)
                nc.scalar.copy(ao[:, 2:4, :], pt_ps[:, 0, :].rearrange("p (j n) -> p j n", j=2)).then_inc(pt_evac, 1)

            over_batches(act, batch)

        @block.gpsimd
        def _(pool):
            PER = TOP_K * NB
            ids = env.token[:].rearrange("p (k t) -> p k t", k=TOP_K)
            slots = env.write_slot[:].rearrange("p (k t) -> p k t", k=TOP_K)

            with pool.Fori(0, B) as b:
                for u in range(UNITS):
                    if u == 0:
                        nc.gpsimd.tensor_copy(ids8[:], ids[:, :, bass.ds(b * NB, NB)]).then_inc(slots_copied, 1)
                        nc.gpsimd.tensor_copy(slot8[:], slots[:, :, bass.ds(b * NB, NB)]).then_inc(slots_copied, 1)
                    if u % 3 == 1 and u // 3 < PER:
                        n = u // 3
                        if n == 0:
                            pool.wait_ge(slots_copied, b * 2 + 2)
                            pool.sem_inc(turnstile, 1)
                        k, j = divmod(n, NB)
                        nc.gpsimd.indirect_dma_start(
                            out=env.ids_dram, out_offset=bass.IndirectOffsetOnAxis(ap=slot8[:, k, j:j + 1].bitcast(U32), axis=0),
                            in_=ids8[:, k, j:j + 1], in_offset=None, bounds_check=env.SLOTS - 1, oob_is_err=False,
                            compute_op=ALU.bypass).then_inc(scattered, 16)
                pool.wait_ge(scattered, b * (16 * PER) + 16 * PER)

        @block.sync
        def _(sp):
            sp.sem_inc(ao_out, 16)
            sp.dma_start(x_sb[:], env.xnT_dram[0]).then_inc(x_in, 16)
            a_dram = env.attn_dram.rearrange("(b j p) d -> b p j d", p=P, j=NB)

            def one(t, b):
                return t[b] if isinstance(b, int) else t[bass.ds(b, 1)].rearrange("o p j d -> (o p) j d")

            def raw(t):
                return t.bitcast(F32)

            HALF = (slice(0, DH), slice(DH, P))

            def stack_q(par):
                for h in range(2):
                    for part in range(2):
                        sp.dma_start(raw(q_st[HALF[part], par, h, :]), raw(nat["q"][HALF[h], part, :])).then_inc(stacked[par], 16)

            def stack_k(par):
                for h in range(2):
                    for to in range(2):
                        sp.dma_start(raw(k_st[HALF[to], par, h]), raw(nat["k"][HALF[h]])).then_inc(stacked[par], 16)

            for par in range(2):
                sp.wait_ge(pj_evac, (1, 5)[par])
                stack_q(par)
                sp.wait_ge(pj_evac, (2, 6)[par])
                stack_k(par)

            def batch(b, is_last):
                if not is_last:
                    sp.wait_ge(x_split, b + 1)
                    sp.dma_start(x_sb[:], one(env.xnT_dram, b + 1)).then_inc(x_in, 16)
                for p in range(PAIRS):
                    u = NB * p + NB - 2
                    if is_last and of_next(piece_at(u)):
                        continue
                    sp.wait_ge(s_done, b * UNITS + NB * (p + 1))
                    sp.sem_inc(turnstile, 1)
                    sp.wait_ge(pj_evac, uses_before(b, u) + 1)
                    stack_q(p % 2)
                    sp.wait_ge(pj_evac, uses_before(b, u) + 2)
                    stack_k(p % 2)
                uses = uses_before(b, UNITS) - (len([u for u in order if of_next(piece_at(u))]) if is_last else 0)
                sp.wait_ge(pj_evac, uses + 1)
                sp.wait_ge(pt_evac, b * PT_USES + (PT_USES + 1))
                sp.dma_start(one(a_dram, b), ao[:]).then_inc(ao_out, 16)

            over_batches(sp, batch)
            sp.wait_ge(ao_out, 16 * (B + 1))


def phase_experts(nc, env, routed):
    B, NB, KC, D, E, F, T = env.B, env.NB, env.KC, env.D, env.E, env.F, env.tiles
    FB = F // P
    GROUPS = E if routed else B // 2
    W = env.CAP // 2 if routed else NB * P
    BLOCKS = [(t, min(P, W - t)) for t in range(0, W, P)]
    R = len(BLOCKS)
    name = "e" if routed else "f"

    with ExitStack() as cx:
        def sb(n, shape, dt=F32):
            return cx.enter_context(nc.sbuf_tensor(f"{name}_{n}", shape, dt))

        def ps(n, shape):
            return cx.enter_context(nc.psum_tensor(f"{name}_{n}", shape, F32))

        def sem(n):
            return cx.enter_context(nc.semaphore(f"{name}_{n}"))

        w13_hi = sb("w13_hi", [P, 2, KC, F], F32R)
        w13_lo = sb("w13_lo", [P, 2, KC, F], F32R)
        w2_hi = sb("w2_hi", [P, FB, D], F32R)
        w2_lo = sb("w2_lo", [P, FB, D], F32R)
        w13_st = sb("w13_st", [P, 2, KC, F])
        w2_st = sb("w2_st", [P, FB, D])
        x_hi = sb("x_hi", [P, 2, KC, W], F32R)
        x_lo = sb("x_lo", [P, 2, KC, W], F32R)
        silu = sb("silu", [P, 2, W])
        g = sb("g", [P, 2, W])
        g_hi = sb("g_hi", [P, FB, W], F32R)
        g_lo = sb("g_lo", [P, FB, W], F32R)
        ab_ps = ps("ab_ps", [P, 2, 2, 512])
        y_ps = ps("y_ps", [P, 2, 512])

        turnstile = sem("turnstile")
        w_in = sem("w_in")
        w13hi_done = sem("w13hi_done")
        w13_ready = sem("w13_ready")
        w2hi_done = sem("w2hi_done")
        w2_ready = sem("w2_ready")
        xhi_done = sem("xhi_done")
        x_ready = sem("x_ready")
        ab_done = sem("ab_done")
        silu_done = sem("silu_done")
        g_done = sem("g_done")
        ghi_done = sem("ghi_done")
        glo_done = sem("glo_done")
        y_done = sem("y_done")
        y_read = sem("y_read")

        if routed:
            ids = sb("ids", [P, 2, R], I32)
            xg = sb("xg", [P, 2, R, D])
            y_sb = sb("y_sb", [P, 2, R, D])
            xT_ps = ps("xT_ps", [P, KC, 512])
            ids_in = [sem("ids_in0"), sem("ids_in1")]
            gathered = [sem("gathered0"), sem("gathered1")]
            xT_done = sem("xT_done")
            y_out = [sem("y_out0"), sem("y_out1")]
        else:
            hT = sb("hT", [P, 2, KC, W])
            base = sb("base", [P, 2, NB, D])
            attn = sb("attn", [P, 2, NB, D])
            bo = sb("bo", [P, 1, D])
            yg = sb("yg", [P, 2, TOP_K * NB, D])
            slot8 = sb("slot8", [P, 2, TOP_K, NB], I32)
            gate8 = sb("gate8", [P, 2, TOP_K, NB])
            bo_in = sem("bo_in")
            hT_in = [sem("hT_in0"), sem("hT_in1")]
            base_in = [sem("base_in0"), sem("base_in1")]
            base_step = sem("base_step")
            base_ready = sem("base_ready")
            slots_copied = sem("slots_copied")
            gathered = [sem("gathered0"), sem("gathered1")]
            acc_step = sem("acc_step")
            gate_step = sem("gate_step")
            out_out = [sem("out_out0"), sem("out_out1")]

        def w_views(e):
            if not routed:
                return env.W1s.rearrange("(c p) f -> p c f", p=P), env.W3s.rearrange("(c p) f -> p c f", p=P), \
                    env.W2s.rearrange("(n p) d -> p n d", p=P)

            def pick(t):
                return t[e] if isinstance(e, int) else t[bass.ds(e, 1)].rearrange("o a b -> (o a) b")
            return pick(env.W1).rearrange("(c p) f -> p c f", p=P), pick(env.W3).rearrange("(c p) f -> p c f", p=P), \
                pick(env.W2).rearrange("(n p) d -> p n d", p=P)

        AHEAD, TURN_AT = 2, 5

        def ahead_of(s, is_last):
            if s == 0:
                return AHEAD
            return 0 if routed or is_last else AHEAD

        def begun(s):
            return AHEAD if s == 1 or not routed else 0

        def over_groups(eng, group):
            with eng.Fori(0, GROUPS - 1) as i:
                group(i, False)
            group(GROUPS - 1, True)

        block = cx.enter_context(nc.Block())

        @block.tensor
        def _(pe):
            pe.sem_inc(y_done, R)
            if routed:
                pe.sem_inc(xT_done, 2)

            def hidden(c, s, blocks):
                if blocks[0] == 0:
                    pe.wait_ge(x_ready, c + 1)
                for f in blocks:
                    pe.wait_ge(g_done, c * FB + (f + 1))
                    for m in range(2):
                        passes = [(w, x, k) for k in range(KC) for w, x in ((w13_hi, x_hi), (w13_hi, x_lo), (w13_lo, x_hi))]
                        for n, (w, x, k) in enumerate(passes):
                            last = nc.tensor.matmul(ab_ps[:, f % 2, m, 0:W], w[:, m, k, f * P:(f + 1) * P], x[:, s, k, :],
                                                    start=n == 0, stop=n == len(passes) - 1)
                    last.then_inc(ab_done, 1)

            def rows(c, s):
                pe.wait_ge(glo_done, c * FB + (FB + 2))
                for j, (t, n_t) in enumerate(BLOCKS):
                    pe.wait_ge(y_read, c * R + (j + 1))
                    passes = [(a, w, f) for f in range(FB) for a, w in ((g_hi, w2_hi), (g_hi, w2_lo), (g_lo, w2_hi))]
                    for n, (a, w, f) in enumerate(passes):
                        last = nc.tensor.matmul(y_ps[0:n_t, (s * R + j) % 2, 0:D], a[:, f, t:t + n_t], w[:, f, :],
                                                start=n == 0, stop=n == len(passes) - 1)
                    last.then_inc(y_done, 1)

            def turn(c, s, i):
                pe.wait_ge(gathered[s], i * (16 * R) + 16 * R)
                if not isinstance(c, int) or c > 0:
                    pe.wait_ge(x_ready, c)
                for k in range(KC):
                    for j, (t, n_t) in enumerate(BLOCKS):
                        last = nc.tensor.transpose(xT_ps[:, k, t:t + n_t], xg[0:n_t, s, j, k * P:(k + 1) * P],
                                                   env.ident[0:n_t, 0:n_t])
                last.then_inc(xT_done, 1)

            if routed:
                turn(0, 0, 0)
            else:
                pe.wait_ge(w13_ready, 1)
                pe.wait_ge(w2_ready, 1)
                hidden(0, 0, range(AHEAD))

            def group(i, is_last):
                for s in range(2):
                    c = i * 2 + s
                    if routed and s == 0:
                        pe.wait_ge(w13_ready, i + 1)
                    hidden(c, s, range(begun(s), TURN_AT))
                    if routed and not (is_last and s == 1):
                        turn(c + 1, 1 - s, i + s)
                    hidden(c, s, range(TURN_AT, FB))
                    if ahead_of(s, is_last):
                        hidden(c + 1, 1 - s, range(AHEAD))
                    if routed and s == 0:
                        pe.wait_ge(w2_ready, i + 1)
                    rows(c, s)

            over_groups(pe, group)

        @block.scalar
        def _(act):
            def split_w13(e):
                act.wait_ge(w_in, e * 48 + 48)
                nc.scalar.copy(w13_hi[:], w13_st[:]).then_inc(w13hi_done, 1)

            def split_w2():
                nc.scalar.copy(w2_hi[:], w2_st[:]).then_inc(w2hi_done, 1)

            def silu_of(c, f):
                act.wait_ge(ab_done, c * FB + (f + 1))
                nc.scalar.activation(silu[:, f % 2, :], ab_ps[:, f % 2, 0, 0:W], ACT.Silu).then_inc(silu_done, 1)

            def g_high(c, f):
                act.wait_ge(g_done, c * FB + (f + 3))
                if f == 0:
                    act.wait_ge(y_done, c * R + R)
                nc.scalar.copy(g_hi[:, f, :], g[:, f % 2, :]).then_inc(ghi_done, 1)

            def gate(c, s, i, is_last):
                if begun(s):
                    g_high(c, 0)
                for f in range(begun(s), FB):
                    silu_of(c, f)
                    if f > 0:
                        g_high(c, f - 1)
                    if f == TURN_AT and not (is_last and s == 1):
                        split_x(c + 1, 1 - s, i + s)
                if ahead_of(s, is_last):
                    silu_of(c + 1, 0)
                g_high(c, FB - 1)
                if ahead_of(s, is_last):
                    silu_of(c + 1, 1)

            def split_x(c, s, i):
                if routed:
                    act.wait_ge(xT_done, c + 3)
                    nc.scalar.copy(x_hi[:, s], xT_ps[:, :, 0:W]).then_inc(xhi_done, 1)
                else:
                    act.wait_ge(hT_in[s], i * 16 + 16)
                    nc.scalar.copy(x_hi[:, s], hT[:, s]).then_inc(xhi_done, 1)

            def rows_out(c, s, i):
                act.wait_ge(y_out[s], i * (16 * R) + 16 * R)
                for j, (t, n_t) in enumerate(BLOCKS):
                    act.wait_ge(y_done, c * R + (j + 1 + R))
                    nc.scalar.copy(y_sb[0:n_t, s, j, :], y_ps[0:n_t, (s * R + j) % 2, 0:D]).then_inc(y_read, 1)

            if routed:
                act.sem_inc(y_read, 2)
                for s in range(2):
                    act.sem_inc(y_out[s], 16 * R)
            split_w13(0)
            split_w2()
            split_x(0, 0, 0)
            if not routed:
                for f in range(AHEAD):
                    silu_of(0, f)

            def group(i, is_last):
                for s in range(2):
                    c = i * 2 + s
                    gate(c, s, i, is_last)
                    if routed and s == 1 and not is_last:
                        split_w13(i + 1)
                    if routed:
                        rows_out(c, s, i)
                    if routed and s == 1 and not is_last:
                        split_w2()

            over_groups(act, group)

        @block.vector
        def _(dve):
            dve.sem_inc(g_done, 2)
            dve.sem_inc(glo_done, 2)

            def split_w13(e):
                dve.wait_ge(w13hi_done, e + 1)
                nc.vector.tensor_tensor(w13_lo[:], w13_st[:], w13_hi[:].bitcast(F32), ALU.subtract).then_inc(w13_ready, 1)

            def split_w2(e):
                dve.wait_ge(w2hi_done, e + 1)
                nc.vector.tensor_tensor(w2_lo[:], w2_st[:], w2_hi[:].bitcast(F32), ALU.subtract).then_inc(w2_ready, 1)

            def g_of(c, f):
                dve.wait_ge(silu_done, c * FB + (f + 1))
                dve.wait_ge(glo_done, c * FB + (f + 1))
                nc.vector.tensor_tensor(g[:, f % 2, :], silu[:, f % 2, :], ab_ps[:, f % 2, 1, 0:W],
                                        ALU.mult).then_inc(g_done, 1)

            def g_low(c, f):
                dve.wait_ge(ghi_done, c * FB + (f + 1))
                nc.vector.tensor_tensor(g_lo[:, f, :], g[:, f % 2, :], g_hi[:, f, :].bitcast(F32),
                                        ALU.subtract).then_inc(glo_done, 1)

            def gate(c, s, is_last):
                if begun(s):
                    g_low(c, 0)
                for f in range(begun(s), FB):
                    g_of(c, f)
                    if f > 0:
                        g_low(c, f - 1)
                    if f == TURN_AT and not (is_last and s == 1):
                        split_x(c + 1, 1 - s)
                if ahead_of(s, is_last):
                    g_of(c + 1, 0)
                g_low(c, FB - 1)
                if ahead_of(s, is_last):
                    g_of(c + 1, 1)

            def split_x(c, s):
                dve.wait_ge(xhi_done, c + 1)
                src = xT_ps[:, :, 0:W] if routed else hT[:, s]
                nc.vector.tensor_tensor(x_lo[:, s], src, x_hi[:, s].bitcast(F32), ALU.subtract).then_inc(x_ready, 1)

            def total(c, s, i):
                gates = env.gates[:].rearrange("p (k t) -> p k t", k=TOP_K)
                at = slice(c * NB, c * NB + NB) if isinstance(c, int) else bass.ds(c * NB, NB)
                nc.vector.tensor_copy(gate8[:, s], gates[:, :, at]).then_inc(gate_step, 1)
                dve.wait_ge(base_ready, c + 1)
                dve.wait_ge(gathered[s], i * (16 * TOP_K * NB) + 16 * TOP_K * NB)
                dve.wait_ge(gate_step, c + 1)
                for k in range(TOP_K):
                    for j in range(NB):
                        last = nc.vector.scalar_tensor_tensor(out=base[:, s, j, :], in0=yg[:, s, k * NB + j, :],
                                                              scalar=gate8[:, s, k, j:j + 1], in1=base[:, s, j, :],
                                                              op0=ALU.mult, op1=ALU.add)
                    last.then_inc(acc_step, 1)
                    dve.wait_ge(acc_step, c * 2 + (k + 5))
                for j in range(NB):
                    dve.wait_ge(y_done, c * R + (j + 1 + R))
                    last = nc.vector.tensor_tensor(base[:, s, j, :], base[:, s, j, :], y_ps[:, (s * R + j) % 2, 0:D], ALU.add)
                    last.then_inc(y_read, 1)

            split_w13(0)
            split_w2(0)
            split_x(0, 0)
            if not routed:
                for f in range(AHEAD):
                    g_of(0, f)
                dve.sem_inc(y_read, 2)
                dve.sem_inc(acc_step, 4)

            def group(i, is_last):
                for s in range(2):
                    c = i * 2 + s
                    gate(c, s, is_last)
                    if routed and s == 1 and not is_last:
                        split_w13(i + 1)
                        split_w2(i + 1)
                    if not routed:
                        total(c, s, i)

            over_groups(dve, group)

        @block.gpsimd
        def _(pool):
            def gather_tokens(c, s, i):
                pool.wait_ge(ids_in[s], i * (16 * R) + 16 * R)
                pool.wait_ge(xT_done, c + 1)
                pool.sem_inc(turnstile, 1)
                for j, (t, n_t) in enumerate(BLOCKS):
                    nc.gpsimd.indirect_dma_start(
                        out=xg[0:n_t, s, j, :], out_offset=None, in_=env.h_dram,
                        in_offset=bass.IndirectOffsetOnAxis(ap=ids[0:n_t, s, j:j + 1].bitcast(U32), axis=0),
                        compute_op=ALU.bypass).then_inc(gathered[s], 16)

            def gather_rows(c, s, i):
                slots = env.read_slot[:].rearrange("p (k t) -> p k t", k=TOP_K)
                pool.wait_ge(acc_step, c * 2 + 2)
                nc.gpsimd.tensor_copy(slot8[:, s], slots[:, :, bass.ds(c * NB, NB)]).then_inc(slots_copied, 1)
                pool.wait_ge(slots_copied, c + 1)
                pool.sem_inc(turnstile, 1)
                for k in range(TOP_K):
                    for j in range(NB):
                        nc.gpsimd.indirect_dma_start(
                            out=yg[:, s, k * NB + j, :], out_offset=None, in_=env.ye_dram,
                            in_offset=bass.IndirectOffsetOnAxis(ap=slot8[:, s, k, j:j + 1].bitcast(U32), axis=0),
                            compute_op=ALU.bypass).then_inc(gathered[s], 16)
                pool.wait_ge(base_in[s], i * 32 + 32)
                nc.gpsimd.tensor_tensor(base[:, s], base[:, s], attn[:, s], ALU.add).then_inc(base_step, 1)
                pool.wait_ge(base_step, c + 1)
                nc.gpsimd.tensor_tensor(base[:, s], base[:, s], bo[:].broadcast_to([P, NB, D]), ALU.add).then_inc(base_ready, 1)

            if routed:
                with pool.Fori(0, GROUPS) as i:
                    for s in range(2):
                        gather_tokens(i * 2 + s, s, i)
            else:
                pool.wait_ge(bo_in, 16)
                with pool.Fori(0, GROUPS) as i:
                    for s in range(2):
                        gather_rows(i * 2 + s, s, i)

        @block.sync
        def _(sp):
            def weights(e):
                w1, w3, w2 = w_views(e)
                sp.dma_start(w13_st[:, 0], w1).then_inc(w_in, 16)
                sp.dma_start(w13_st[:, 1], w3).then_inc(w_in, 16)
                sp.dma_start(w2_st[:], w2).then_inc(w_in, 16)

            def one(t, b):
                return t[b] if isinstance(b, int) else t[bass.ds(b, 1)].rearrange("o p j d -> (o p) j d")

            def rows_of(t, c, t0, n_t):
                if isinstance(c, int):
                    return t[c * W + t0:c * W + t0 + n_t, :]
                return t[bass.ds(c * W + t0, n_t), :]

            def load_ids(c, s):
                for j, (t, n_t) in enumerate(BLOCKS):
                    sp.dma_start(ids[0:n_t, s, j:j + 1], rows_of(env.ids_dram, c, t, n_t)).then_inc(ids_in[s], 16)

            def load_batch(c, s):
                sp.dma_start(hT[:, s], one(env.hT_dram, c)).then_inc(hT_in[s], 16)

            def load_base(c, s):
                sp.dma_start(base[:, s], one(env.x.rearrange("b (j p) d -> b p j d", p=P), c)).then_inc(base_in[s], 16)
                sp.dma_start(attn[:, s], one(env.attn_dram.rearrange("(b j p) d -> b p j d", p=P, j=NB), c)).then_inc(base_in[s], 16)

            weights(0)
            if routed:
                for s in range(2):
                    load_ids(s, s)
            else:
                sp.dma_start(bo[:, 0, :], env.bo.rearrange("(a d) -> a d", a=1).broadcast_to([P, D])).then_inc(bo_in, 16)
                for s in range(2):
                    load_batch(s, s)
                    load_base(s, s)

            def group(i, is_last):
                if routed and not is_last:
                    sp.wait_ge(w13_ready, i + 1)
                    sp.wait_ge(w2_ready, i + 1)
                    weights(i + 1)
                for s in range(2):
                    c = i * 2 + s
                    if routed:
                        if not is_last:
                            sp.wait_ge(gathered[s], i * (16 * R) + 16 * R)
                            load_ids(c + 2, s)
                        for j, (t, n_t) in enumerate(BLOCKS):
                            sp.wait_ge(y_read, c * R + (j + 3))
                            sp.dma_start(rows_of(env.ye_dram, c, t, n_t), y_sb[0:n_t, s, j, :]).then_inc(y_out[s], 16)
                    else:
                        if not is_last:
                            sp.wait_ge(x_ready, c + 1)
                            load_batch(c + 2, s)
                        sp.wait_ge(y_read, c * R + (R + 2))
                        sp.dma_start(one(env.out.rearrange("b (j p) d -> b p j d", p=P), c), base[:, s]).then_inc(out_out[s], 16)
                        if not is_last:
                            sp.wait_ge(out_out[s], i * 16 + 16)
                            load_base(c + 2, s)

            over_groups(sp, group)
            for s in range(2):
                if routed:
                    sp.wait_ge(y_out[s], 16 * R * (GROUPS + 1))
                else:
                    sp.wait_ge(out_out[s], 16 * GROUPS)


def transformer_layer(nc, x, Wq, Wkv, Wo, bo, ln_g, ln_b, Wr, W1, W3, W2, W1s, W3s, W2s, out):
    B, N, D = x.shape
    E, _, F = W1.shape
    NB, tokens = N // P, B * N
    CAP = -(-5 * CAPACITY_TOKENS * TOP_K // (4 * E))
    SLOTS = -(-E * CAP // P) * P
    assert N % P == 0 and D % P == 0 and B % 2 == 0 and CAP % 2 == 0

    with ExitStack() as cx:
        def sb(name, shape, dt=F32):
            return cx.enter_context(nc.sbuf_tensor(name, shape, dt))

        def dram(name, shape, dt=F32):
            return nc.dram_tensor(name, shape, dt, kind="Internal").ap()

        T = tokens // P
        env = Env(
            B=B, NB=NB, KC=D // P, D=D, E=E, F=F, DH=Wq.shape[1] // HEADS, CAP=CAP, SLOTS=SLOTS, tiles=T,
            x=x, Wq=Wq, Wkv=Wkv, Wo=Wo, bo=bo, ln_g=ln_g, ln_b=ln_b, Wr=Wr, W1=W1, W3=W3, W2=W2,
            W1s=W1s, W3s=W3s, W2s=W2s, out=out,
            xnT_dram=dram("xnT_dram", (B, P, D // P, N)), hT_dram=dram("hT_dram", (B, P, D // P, N)),
            h_dram=dram("h_dram", (tokens, D)), attn_dram=dram("attn_dram", (tokens, D)),
            ids_dram=dram("ids_dram", (SLOTS, 1), I32), ye_dram=dram("ye_dram", (E * CAP, D)),
            ident=sb("ident", [P, P]), upper=sb("upper", [P, P], BF16), ones=sb("ones", [P, P], BF16),
            causal=sb("causal", [P, 2, P]), logits=sb("logits", [P, T, E]),
            gates=sb("gates", [P, TOP_K * T]), token=sb("token", [P, TOP_K * T], I32),
            read_slot=sb("read_slot", [P, TOP_K * T], I32), write_slot=sb("write_slot", [P, TOP_K * T], I32))
        phase_constants(nc, env)
        phase_norm(nc, env)
        phase_route(nc, env)
        phase_attention(nc, env)
        phase_experts(nc, env, routed=True)
        phase_experts(nc, env, routed=False)


_INS = ["L0_attn_x", "L0_attn_Wq", "L0_attn_Wkv", "L0_attn_Wo", "L0_attn_bo", "L0_ffn_ln_g", "L0_ffn_ln_b", "L0_ffn_Wr",
        "L0_ffn_W1", "L0_ffn_W3", "L0_ffn_W2", "L0_ffn_W1s", "L0_ffn_W3s", "L0_ffn_W2s"]


def kernel(**inputs):
    import numpy as np
    import concourse.bacc as bacc
    from concourse.bass_utils import run_bass_kernel_spmd

    nc = bacc.Bacc("TRN2", target_bir_lowering=False, num_devices=1)
    arrays, args = {}, []
    for name in _INS:
        a = np.ascontiguousarray(inputs[name])
        arrays[f"in_{name}"] = a
        args.append(nc.dram_tensor(f"in_{name}", a.shape, mybir.dt.from_np(a.dtype), kind="ExternalInput").ap())
    x = arrays["in_L0_attn_x"]
    out = nc.dram_tensor("out", x.shape, mybir.dt.from_np(x.dtype), kind="ExternalOutput").ap()
    transformer_layer(nc, *args, out)
    result = run_bass_kernel_spmd(nc, [arrays], core_ids=[0])
    return result.results[0]["out"]
```

```python
from collections import namedtuple
from contextlib import ExitStack

import concourse.bass as bass
from concourse import mybir

ALU = mybir.AluOpType
ACT = mybir.ActivationFunctionType
AX_X = mybir.AxisListType.X
F32 = mybir.dt.float32
F32R = mybir.dt.float32r
BF16 = mybir.dt.bfloat16
I32 = mybir.dt.int32
U32 = mybir.dt.uint32

P = 128
HEADS = 16
LN_EPS = 1e-5
SOFTMAX_EPS = 1e-8
TOP_K = 2
CAPACITY_TOKENS = 4 * 512
LOWEST = -3.0e38

Env = namedtuple("Env", """
    B NB KC D E F DH CAP SLOTS INNER tiles
    x Wq Wkv Wo ln_g ln_b Wr bo W1 W3 W2 W1s W3s W2s out out_rows
    xnT_dram h_dram queue_dram
    ident upper before ones causal logits weight empty entry write_slot""")
Ahead = namedtuple("Ahead", "pT0 qk_in w13_stage queue tokens w_in queue_in first_gathered")


CONSTANTS = 14


def make_constants(nc, env, pool, made):
    T, E = env.tiles, env.E
    nc.gpsimd.memset(env.ident[:], 0.0).then_inc(made, 1)
    nc.gpsimd.memset(env.upper[:], 1.0).then_inc(made, 1)
    nc.gpsimd.memset(env.ones[:], 1.0).then_inc(made, 1)
    nc.gpsimd.memset(env.causal[:], 0.0).then_inc(made, 1)
    nc.gpsimd.memset(env.before[:], 1.0).then_inc(made, 1)
    nc.gpsimd.iota(env.weight[:], [[0, T], [-1, E]], base=E, channel_multiplier=0,
                   allow_small_or_imprecise_dtypes=True).then_inc(made, 1)
    for column in range(2):
        nc.gpsimd.iota(env.entry[:, :, column], [[0, TOP_K], [P, T]], base=0, channel_multiplier=1).then_inc(made, 1)
    nc.gpsimd.memset(env.empty[:], 0).then_inc(made, 1)
    pool.wait_ge(made, 9)
    nc.gpsimd.memset(env.empty[:, :, 1], T * P).then_inc(made, 1)
    nc.gpsimd.affine_select(out=env.ident[:], in_=env.ident[:], compare_op=ALU.not_equal, fill=1.0, base=0,
                            pattern=[[-1, P]], channel_multiplier=1).then_inc(made, 1)
    nc.gpsimd.affine_select(out=env.upper[:], in_=env.upper[:], compare_op=ALU.is_ge, fill=0.0, base=0,
                            pattern=[[1, P]], channel_multiplier=-1).then_inc(made, 1)
    nc.gpsimd.affine_select(out=env.before[:], in_=env.before[:], compare_op=ALU.is_ge, fill=0.0, base=-1,
                            pattern=[[1, P]], channel_multiplier=-1).then_inc(made, 1)
    nc.gpsimd.affine_select(out=env.causal[:], in_=env.causal[:], compare_op=ALU.is_ge, fill=LOWEST, base=0,
                            pattern=[[0, 2], [-1, P]], channel_multiplier=1).then_inc(made, 1)
    pool.wait_ge(made, CONSTANTS)


Router = namedtuple("Router", """
    onehot onehot16 a rest top mark totals pos start kept slot diff total gate totals_ps place_ps
    step onehot_ready counted totals_ready placed diff_ready exp_ready""")


def router(nc, env, cx, counts_ps):
    T, E = env.tiles, env.E
    ROWS = TOP_K * T
    assert ROWS == P and E <= 8

    def sb(name, shape, dt=F32):
        return cx.enter_context(nc.sbuf_tensor("r_" + name, shape, dt))

    def sem(name):
        return cx.enter_context(nc.semaphore("r_" + name))

    return Router(
        onehot=sb("onehot", [P, ROWS, E]), onehot16=sb("onehot16", [P, ROWS, E], BF16),
        a=sb("a", [P, T, E]), rest=sb("rest", [P, T, E]),
        top=sb("top", [P, TOP_K, T]), mark=sb("mark", [P, ROWS]), totals=sb("totals", [P, E, P], BF16),
        pos=sb("pos", [P, ROWS]), start=sb("start", [P, ROWS]),
        kept=sb("kept", [P, ROWS]), slot=sb("slot", [P, ROWS]), diff=sb("diff", [P, T]),
        total=sb("total", [P, T]), gate=sb("gate", [P, TOP_K, T]),
        totals_ps=counts_ps[:, 0, 0:E], place_ps=counts_ps.rearrange("p k (e r) -> p (k e) r", r=P),
        step=sem("step"),
        onehot_ready=sem("onehot_ready"),
        counted=sem("counted"),
        totals_ready=sem("totals_ready"),
        placed=sem("placed"),
        diff_ready=sem("diff_ready"),
        exp_ready=sem("exp_ready"))


CHOICE = 5


def route_done(dve, r, instruction, n):
    instruction.then_inc(r.step, 1)
    dve.wait_ge(r.step, n)


def route_choice(nc, env, dve, r, logits, k, n):
    T, E = env.tiles, env.E
    rows = slice(k * T, k * T + T)

    def per_token(t):
        return t.unsqueeze(2).broadcast_to([P, T, E])

    route_done(dve, r, nc.vector.tensor_reduce(r.top[:, k, :], logits, AX_X, ALU.max), n + 1)
    route_done(dve, r, nc.vector.tensor_tensor(r.a[:], logits, per_token(r.top[:, k, :]), ALU.is_equal), n + 2)
    route_done(dve, r, nc.vector.tensor_tensor(r.a[:], r.a[:], env.weight[:], ALU.mult), n + 3)
    route_done(dve, r, nc.vector.tensor_reduce(r.mark[:, rows], r.a[:], AX_X, ALU.max), n + 4)
    route_done(dve, r, nc.vector.tensor_tensor(r.onehot[:, rows, :], env.weight[:], per_token(r.mark[:, rows]),
                                               ALU.is_equal), n + 5)


def route_first(nc, env, dve, r):
    route_choice(nc, env, dve, r, env.logits[:], 0, 0)


def route_rest(nc, env, dve, r):
    route_done(dve, r, nc.vector.tensor_scalar(r.a[:], r.onehot[:, 0:env.tiles, :], LOWEST, None, ALU.mult), CHOICE + 1)
    route_done(dve, r, nc.vector.tensor_tensor(r.rest[:], env.logits[:], r.a[:], ALU.add), CHOICE + 2)


def route_second(nc, env, dve, r):
    route_choice(nc, env, dve, r, r.rest[:], 1, CHOICE + 2)
    nc.vector.tensor_copy(r.onehot16[:], r.onehot[:]).then_inc(r.onehot_ready, 1)
    nc.vector.tensor_tensor(r.diff[:], r.top[:, 1, :], r.top[:, 0, :], ALU.subtract).then_inc(r.diff_ready, 1)


def route_count(nc, env, pe, r):
    pe.wait_ge(r.onehot_ready, 1)
    for e in range(env.E):
        last = nc.tensor.matmul(r.totals_ps[:, e:e + 1], r.onehot16[:, :, e], env.ones[:, 0:1], start=True, stop=True)
    last.then_inc(r.counted, 1)


def route_totals(nc, env, dve, r):
    dve.wait_ge(r.counted, 1)
    nc.vector.tensor_copy(r.totals[:], r.totals_ps.unsqueeze(2).broadcast_to([P, env.E, P])).then_inc(r.totals_ready, 1)


def route_place(nc, env, pe, r):
    pe.wait_ge(r.totals_ready, 1)
    for e in range(env.E):
        nc.tensor.matmul(r.place_ps[:, e, :], env.upper[:], r.onehot16[:, :, e], start=True, stop=False)
        last = nc.tensor.matmul(r.place_ps[:, e, :], r.totals[:, e, :], env.before[:], start=False, stop=True)
    last.then_inc(r.placed, 1)


def route_positions(nc, env, dve, r):
    n = 2 * CHOICE + 2
    dve.wait_ge(r.placed, 1)
    by_row = r.place_ps[:, 0:env.E, :].rearrange("p e r -> p r e")
    route_done(dve, r, nc.vector.tensor_tensor(r.onehot[:], by_row, r.onehot[:], ALU.mult), n + 1)
    route_done(dve, r, nc.vector.tensor_reduce(r.pos[:], r.onehot[:], AX_X, ALU.add), n + 2)


def route_slots(nc, env, dve, r):
    n, E, CAP, SLOTS = 2 * CHOICE + 4, env.E, env.CAP, env.SLOTS
    route_done(dve, r, nc.vector.tensor_scalar(r.start[:], r.mark[:], -float(CAP), float(E * CAP - 1), ALU.mult, ALU.add), n + 1)
    route_done(dve, r, nc.vector.tensor_scalar(r.kept[:], r.pos[:], float(CAP), float(SLOTS), ALU.is_gt, ALU.mult), n + 2)
    route_done(dve, r, nc.vector.tensor_tensor(r.slot[:], r.pos[:], r.start[:], ALU.add), n + 3)
    route_done(dve, r, nc.vector.tensor_tensor(r.slot[:], r.slot[:], r.kept[:], ALU.add), n + 4)
    nc.vector.tensor_copy(env.write_slot[:], r.slot[:])


def route_exp(nc, act, r):
    act.wait_ge(r.diff_ready, 1)
    nc.scalar.activation(r.gate[:, 1, :], r.diff[:], ACT.Exp).then_inc(r.exp_ready, 1)


def route_gates(nc, env, dve, r):
    n, T = 2 * CHOICE + 8, env.tiles
    gates = env.entry[:, :, 2].bitcast(F32)
    dve.wait_ge(r.exp_ready, 1)
    route_done(dve, r, nc.vector.tensor_scalar(r.total[:], r.gate[:, 1, :], 1.0, None, ALU.add), n + 1)
    route_done(dve, r, nc.vector.reciprocal(r.gate[:, 0, :], r.total[:]), n + 2)
    nc.vector.tensor_copy(gates[:, 0:T], r.gate[:, 0, :])
    nc.vector.tensor_tensor(gates[:, T:], r.gate[:, 1, :], r.gate[:, 0, :], ALU.mult)


def phase_norm_shared(nc, env, ahead):
    B, NB, KC, D, E, F = env.B, env.NB, env.KC, env.D, env.E, env.F
    N, FB = NB * P, F // P
    LEAD = 3
    AHEAD = 2
    TURN_XN, TURN_H, SCORE = 3, 5, 7
    COUNT = 7

    with ExitStack() as cx:
        def sb(name, shape, dt=F32):
            return cx.enter_context(nc.sbuf_tensor("n_" + name, shape, dt))

        def ps(name, shape):
            return cx.enter_context(nc.psum_tensor("n_" + name, shape, F32))

        def sem(name):
            return cx.enter_context(nc.semaphore("n_" + name))

        x_sb = sb("x", [P, 2, NB, D])
        xn_sb = sb("xn", [P, 2, NB, D])
        z_sb = sb("z", [P, 2, NB, D])
        h_sb = sb("h", [P, 2, NB, D])
        xnT_sb = sb("xnT", [P, 2, KC, N])
        hT_sb = sb("hT", [P, KC, N])
        base = sb("base", [P, 2, NB, D])
        g_sb = sb("g", [P, 1, D])
        b_sb = sb("b", [P, 1, D])
        bo_sb = sb("bo", [P, 1, D])
        wr_sb = sb("wr", [P, KC, E])
        stats = sb("stats", [P, 2, NB, 6])
        mv = sb("mv", [P, 2, NB, 2])
        ve = sb("ve", [P, 2, NB])
        sd = sb("sd", [P, 2, NB])
        rs = sb("rs", [P, 2, NB])
        tmp = sb("tmp", [P, 2, NB])
        w13_hi = sb("w13_hi", [P, 2, KC, F], F32R)
        w13_lo = sb("w13_lo", [P, 2, KC, F], F32R)
        w2_hi = sb("w2_hi", [P, FB, D], F32R)
        w2_lo = sb("w2_lo", [P, FB, D], F32R)
        w_st = ahead.w13_stage
        w2_st = w_st[:, 0].rearrange("p c (n d) -> p (c n) d", d=D)
        x_hi = sb("x_hi", [P, 2, KC, N], F32R)
        x_lo = sb("x_lo", [P, 2, KC, N], F32R)
        silu = sb("silu", [P, 2, N])
        gated = sb("gated", [P, 2, N])
        g_hi = sb("g_hi", [P, FB, N], F32R)
        g_lo = sb("g_lo", [P, FB, N], F32R)
        ab_ps = ps("ab_ps", [P, 2, 2, N])
        y_ps = ps("y_ps", [P, 2, 512])
        t_ps = ps("t_ps", [P, KC, N])
        lg_ps = t_ps[:, 0, 0:NB * E].rearrange("p (j e) -> p j e", e=E)

        r = router(nc, env, cx, t_ps[:])

        made = sem("made")
        params_in = sem("params_in")
        queue_init = sem("queue_init")
        x_in = [sem("x_in0"), sem("x_in1")]
        dve_step = sem("dve_step")
        turnstile = sem("turnstile")
        ve_ready = sem("ve_ready")
        sd_ready = sem("sd_ready")
        xn_ready = sem("xn_ready")
        z_ready = sem("z_ready")
        z_scaled = sem("z_scaled")
        h_ready = sem("h_ready")
        t_done = sem("t_done")
        t_evac = sem("t_evac")
        xnT_out = [sem("xnT_out0"), sem("xnT_out1")]
        h_out = [sem("h_out0"), sem("h_out1")]
        w_in = sem("w_in")
        w2_in = sem("w2_in")
        whi_done = sem("whi_done")
        w_ready = sem("w_ready")
        x_ready = sem("x_ready")
        ab_done = sem("ab_done")
        silu_done = sem("silu_done")
        g_done = sem("g_done")
        ghi_done = sem("ghi_done")
        glo_done = sem("glo_done")
        y_done = sem("y_done")
        y_read = sem("y_read")
        base_in = [sem("base_in0"), sem("base_in1")]
        base_ready = sem("base_ready")
        base_out = [sem("base_out0"), sem("base_out1")]

        def of_batches(t):
            return t.rearrange("b (j p) d -> b p j d", p=P)

        h_dram = env.h_dram.rearrange("(b j p) d -> b p j d", p=P, j=NB)

        def one(t, b):
            return t[b] if isinstance(b, int) else t[bass.ds(b, 1)].rearrange("o p j d -> (o p) j d")

        def later(batch, n):
            k, s, half = batch
            return k + n, (s + n) % 2, half + (s + n) // 2

        def exists(batch):
            return not isinstance(batch[0], int) or 0 <= batch[0] < B

        def known(k):
            return isinstance(k, int)

        def over_chunks(eng, chunk):
            with eng.Fori(0, B // 2 - 2) as i:
                for s in range(2):
                    chunk((i * 2 + s, s, i))
            for k in range(B - 4, B):
                chunk((k, k % 2, k // 2))

        def xn_use(k):
            return k if known(k) and k < 2 else k * 3 - 2

        def h_use(k):
            return 2 if known(k) and k == 0 else k * 3 + (2 if not known(k) or k < B - 1 else 1)

        def logits_use(k):
            return h_use(k) + 1

        block = cx.enter_context(nc.Block())

        @block.sync
        def _(sp):
            x_dram, out_dram = of_batches(env.x), of_batches(env.out)
            for s in range(2):
                sp.dma_start(x_sb[:, s], x_dram[s]).then_inc(x_in[s], 16)
            for src, dst in ((env.ln_g, g_sb), (env.ln_b, b_sb), (env.bo, bo_sb)):
                row = src.rearrange("(a d) -> a d", a=1).broadcast_to([P, D])
                sp.dma_start(dst[:, 0, :], row).then_inc(params_in, 16)
            sp.dma_start(wr_sb[:], env.Wr.rearrange("(c p) e -> p c e", p=P)).then_inc(params_in, 16)
            sp.dma_start(w_st[:, 0], env.W1s.rearrange("(c p) f -> p c f", p=P)).then_inc(w_in, 16)
            sp.dma_start(w_st[:, 1], env.W3s.rearrange("(c p) f -> p c f", p=P)).then_inc(w_in, 16)

            def load_x(batch):
                k, s, _ = batch
                sp.wait_ge(xn_ready, k - 1)
                sp.dma_start(x_sb[:, s], one(x_dram, k)).then_inc(x_in[s], 16)

            def store_xnT(batch):
                k, s, _ = batch
                sp.wait_ge(t_evac, xn_use(k) + 1)
                sp.dma_start(one(env.xnT_dram, k), xnT_sb[:, s]).then_inc(xnT_out[s], 16)

            def store_h(batch):
                k, s, _ = batch
                sp.wait_ge(h_ready, k + 3)
                sp.dma_start(one(h_dram, k), h_sb[:, s]).then_inc(h_out[s], 16)

            load_x((2, 0, 1))
            sp.wait_ge(w_ready, 1)
            sp.dma_start(w2_st, env.W2s.rearrange("(n p) d -> p n d", p=P)).then_inc(w2_in, 16)
            load_x((3, 1, 1))
            for s in range(2):
                sp.dma_start(base[:, s], x_dram[s]).then_inc(base_in[s], 16)
            sp.wait_ge(made, CONSTANTS)
            sp.dma_start(env.queue_dram.rearrange("(p c) o -> p c o", p=P), env.empty[:]).then_inc(queue_init, 16)
            store_xnT((0, 0, 0))
            store_xnT((1, 1, 0))
            store_h((0, 0, 0))
            sp.wait_ge(w_ready, 2)
            for n in range(2):
                sp.dma_start(attention_stage(env, ahead.pT0, n), attention_weights(env)[n]).then_inc(ahead.qk_in[n], 16)

            def chunk(batch):
                c, s, half = batch
                if exists(n := later(batch, 1)):
                    store_h(n)
                if exists(n := later(batch, 2)):
                    store_xnT(n)
                if exists(n := later(batch, 4)):
                    load_x(n)
                sp.wait_ge(y_read, c * NB + (NB + 2))
                sp.dma_start(one(out_dram, c), base[:, s]).then_inc(base_out[s], 16)
                if exists(n := later(batch, 2)):
                    sp.wait_ge(base_out[s], half * 16 + 16)
                    sp.dma_start(base[:, s], one(x_dram, n[0])).then_inc(base_in[s], 16)

            over_chunks(sp, chunk)
            for s in range(2):
                for q in (xnT_out, h_out):
                    sp.wait_ge(q[s], 16 * (B // 2) + 16)
                sp.wait_ge(base_out[s], 16 * (B // 2))
            sp.wait_ge(queue_init, 16)

        @block.tensor
        def _(pe):
            pe.sem_inc(y_done, NB)
            pe.wait_ge(made, CONSTANTS)

            def transposes(src):
                for k in range(KC):
                    for j in range(NB):
                        last = nc.tensor.transpose(t_ps[:, k, j * P:(j + 1) * P], src[:, j, k * P:(k + 1) * P], env.ident[:])
                return last

            def turn_xn(batch):
                k, s, _ = batch
                pe.wait_ge(xn_ready, k + 1)
                if not (known(k) and k == 0):
                    pe.wait_ge(t_evac, xn_use(k))
                transposes(xn_sb[:, s]).then_inc(t_done, 1)

            def turn_h(batch):
                k, s, _ = batch
                pe.wait_ge(h_ready, k + 3)
                pe.wait_ge(t_evac, h_use(k))
                transposes(h_sb[:, s]).then_inc(t_done, 1)

            def score(batch):
                pe.wait_ge(t_evac, logits_use(batch[0]))
                for j in range(NB):
                    for k in range(KC):
                        last = nc.tensor.matmul(lg_ps[:, j, :], hT_sb[:, k, j * P:(j + 1) * P], wr_sb[:, k, :],
                                                start=k == 0, stop=k == KC - 1)
                last.then_inc(t_done, 1)

            def hidden(batch, f):
                c, s, _ = batch
                if f == 0:
                    pe.wait_ge(x_ready, c + 1)
                pe.wait_ge(g_done, c * FB + (f + 1))
                for m in range(2):
                    passes = [(w, x, k) for k in range(KC) for w, x in ((w13_hi, x_hi), (w13_hi, x_lo), (w13_lo, x_hi))]
                    for n, (w, x, k) in enumerate(passes):
                        last = nc.tensor.matmul(ab_ps[:, f % 2, m, :], w[:, m, k, f * P:(f + 1) * P], x[:, s, k, :],
                                                start=n == 0, stop=n == len(passes) - 1)
                last.then_inc(ab_done, 1)

            def rows(batch):
                c = batch[0]
                pe.wait_ge(glo_done, c * FB + (FB + 1))
                for j in range(NB):
                    pe.wait_ge(y_read, c * NB + (j + 1))
                    passes = [(a, w, f) for f in range(FB) for a, w in ((g_hi, w2_hi), (g_hi, w2_lo), (g_lo, w2_hi))]
                    for n, (a, w, f) in enumerate(passes):
                        if j == 0 and n == len(passes) - 3:
                            pe.wait_ge(glo_done, c * FB + (FB + 2))
                        last = nc.tensor.matmul(y_ps[:, j % 2, 0:D], a[:, f, j * P:(j + 1) * P], w[:, f, :],
                                                start=n == 0, stop=n == len(passes) - 1)
                    last.then_inc(y_done, 1)

            first = (0, 0, 0)
            turn_xn(first)
            turn_xn(later(first, 1))
            turn_h(first)
            pe.wait_ge(params_in, 64)
            pe.wait_ge(w_ready, 1)
            for f in range(AHEAD):
                hidden(first, f)
            score(first)

            def chunk(batch):
                for f in range(AHEAD, FB):
                    if f == TURN_XN and exists(n := later(batch, 2)):
                        turn_xn(n)
                    if f == TURN_H and exists(n := later(batch, 1)):
                        turn_h(n)
                    if f == SCORE and exists(n := later(batch, 1)):
                        score(n)
                    if f == COUNT and not exists(later(batch, 1)):
                        route_count(nc, env, pe, r)
                    hidden(batch, f)
                if exists(n := later(batch, 1)):
                    for f in range(AHEAD):
                        hidden(n, f)
                else:
                    route_place(nc, env, pe, r)
                pe.wait_ge(w_ready, 2)
                rows(batch)

            over_chunks(pe, chunk)

        @block.scalar
        def _(act):
            for s in range(2):
                act.sem_inc(xnT_out[s], 16)

            def evacuate_xn(batch):
                k, s, half = batch
                act.wait_ge(t_done, xn_use(k) + 1)
                act.wait_ge(xnT_out[s], half * 16 + 16)
                nc.scalar.copy(xnT_sb[:, s], t_ps[:]).then_inc(t_evac, 1)

            def evacuate_h(batch):
                k, s, _ = batch
                act.wait_ge(t_done, h_use(k) + 1)
                if not (known(k) and k == 0):
                    act.wait_ge(x_ready, k)
                nc.scalar.copy(hT_sb[:], t_ps[:])
                nc.scalar.copy(x_hi[:, s], t_ps[:]).then_inc(t_evac, 1)

            def evacuate_logits(batch):
                k = batch[0]
                act.wait_ge(t_done, logits_use(k) + 1)
                at = slice(k * NB, k * NB + NB) if known(k) else bass.ds(k * NB, NB)
                nc.scalar.copy(env.logits[:, at, :], lg_ps).then_inc(t_evac, 1)

            def root(batch):
                k = batch[0]
                sel = slice(0 if exists(batch) else 1, 1 if known(k) and k == 0 else 2)
                act.wait_ge(ve_ready, k + 1)
                nc.scalar.activation(sd[:, sel], ve[:, sel], ACT.Sqrt).then_inc(sd_ready, 1)

            def silu_of(c, f):
                act.wait_ge(ab_done, c * FB + (f + 1))
                nc.scalar.activation(silu[:, f % 2, :], ab_ps[:, f % 2, 0, :], ACT.Silu).then_inc(silu_done, 1)

            def g_high(c, f):
                act.wait_ge(g_done, c * FB + (f + 3))
                if f == 0:
                    act.wait_ge(y_done, c * NB + NB)
                nc.scalar.copy(g_hi[:, f, :], gated[:, f % 2, :]).then_inc(ghi_done, 1)

            first = (0, 0, 0)
            root(first)
            evacuate_xn(first)
            root(later(first, 1))
            act.wait_ge(w_in, 32)
            nc.scalar.copy(w13_hi[:], w_st[:]).then_inc(whi_done, 1)
            evacuate_xn(later(first, 1))
            root(later(first, 2))
            evacuate_h(first)
            act.wait_ge(w2_in, 16)
            nc.scalar.copy(w2_hi[:], w2_st).then_inc(whi_done, 1)
            for f in range(AHEAD):
                silu_of(0, f)
            evacuate_logits(first)

            def chunk(batch):
                c = batch[0]
                g_high(c, 0)
                for f in range(AHEAD, FB):
                    if f == TURN_XN and exists(n := later(batch, 2)):
                        evacuate_xn(n)
                    if f == TURN_H and exists(n := later(batch, 1)):
                        evacuate_h(n)
                    if f == SCORE and exists(n := later(batch, 1)):
                        evacuate_logits(n)
                    silu_of(c, f)
                    g_high(c, f - 1)
                if exists(later(batch, 1)):
                    silu_of(c + 1, 0)
                g_high(c, FB - 1)
                if exists(later(batch, 1)):
                    silu_of(c + 1, 1)
                if exists(later(batch, LEAD - 1)):
                    root(later(batch, LEAD))
                if not exists(later(batch, 1)):
                    route_exp(nc, act, r)

            over_chunks(act, chunk)

        @block.vector
        def _(dve):
            PER = 4 * NB + 5
            FIRST = 2 * NB + 5
            dve.sem_inc(g_done, 2)
            dve.sem_inc(glo_done, 2)
            dve.sem_inc(y_read, 2)

            def halves_of(batch):
                k = batch[0]
                both = [n for n, b in enumerate((batch, later(batch, -1))) if exists(b)]
                return both, (k * PER + (FIRST - PER) if not known(k) or k > 0 else 0)

            def statistics(batch, n):
                k, s, half = batch
                src = x_sb[:, s] if n == 0 else xn_sb[:, 1 - s]
                if n == 0:
                    dve.wait_ge(x_in[s], half * 16 + 16)
                else:
                    dve.wait_ge(xn_ready, k)
                for j in range(NB):
                    nc.vector.bn_stats(stats[:, n, j, :], src[:, j, :]).then_inc(dve_step, 1)

            def aggregate(batch):
                k = batch[0]
                both, c = halves_of(batch)
                n_rows = NB * len(both)
                dve.wait_ge(dve_step, c + n_rows)
                if not known(k) or k > 1:
                    dve.wait_ge(z_ready, k - 1)
                dve.sem_inc(turnstile, 1)
                for n in both:
                    for j in range(NB):
                        nc.vector.bn_aggr(mv[:, n, j, :], stats[:, n, j, :]).then_inc(dve_step, 1)
                dve.wait_ge(dve_step, c + 2 * n_rows)
                sel = slice(both[0], both[-1] + 1)
                nc.vector.tensor_scalar(ve[:, sel], mv[:, sel, :, 1], LN_EPS, None, ALU.add).then_inc(ve_ready, 1)

            def invert(batch):
                k = batch[0]
                both, c = halves_of(batch)
                n_rows = NB * len(both)
                sel = slice(both[0], both[-1] + 1)
                dve.wait_ge(sd_ready, k + 1)
                nc.vector.reciprocal(rs[:, sel], sd[:, sel]).then_inc(dve_step, 1)
                dve.wait_ge(dve_step, c + (2 * n_rows + 1))
                nc.vector.tensor_tensor(tmp[:, sel], ve[:, sel], rs[:, sel], ALU.mult).then_inc(dve_step, 1)
                dve.wait_ge(dve_step, c + (2 * n_rows + 2))
                nc.vector.tensor_tensor(tmp[:, sel], tmp[:, sel], rs[:, sel], ALU.mult).then_inc(dve_step, 1)
                dve.wait_ge(dve_step, c + (2 * n_rows + 3))
                nc.vector.tensor_scalar(tmp[:, sel], tmp[:, sel], -0.5, 1.5, ALU.mult, ALU.add).then_inc(dve_step, 1)
                dve.wait_ge(dve_step, c + (2 * n_rows + 4))
                nc.vector.tensor_tensor(rs[:, sel], rs[:, sel], tmp[:, sel], ALU.mult).then_inc(dve_step, 1)

            def apply(batch, n):
                k, s, _ = batch
                both, c = halves_of(batch)
                if n not in both:
                    return
                dve.wait_ge(dve_step, c + (2 * NB * len(both) + 5))
                if n == 1:
                    dve.wait_ge(h_ready, k)
                elif not known(k) or k > 1:
                    dve.wait_ge(t_done, xn_use(k - 2) + 1)
                src, dst = ((x_sb[:, s], xn_sb[:, s]), (xn_sb[:, 1 - s], z_sb[:, 1 - s]))[n]
                for j in range(NB):
                    last = nc.vector.tensor_scalar(dst[:, j, :], src[:, j, :], mv[:, n, j, 0:1], rs[:, n, j:j + 1],
                                                   ALU.subtract, ALU.mult)
                last.then_inc((xn_ready, z_ready)[n], 1)

            def step(batch):
                for n in halves_of(batch)[0]:
                    statistics(batch, n)
                aggregate(batch)
                invert(batch)
                for n in range(2):
                    apply(batch, n)

            def x_low(batch):
                k, s, _ = batch
                dve.wait_ge(t_evac, h_use(k) + 1)
                nc.vector.tensor_tensor(x_lo[:, s], hT_sb[:], x_hi[:, s].bitcast(F32), ALU.subtract).then_inc(x_ready, 1)

            def g_of(c, f):
                dve.wait_ge(silu_done, c * FB + (f + 1))
                dve.wait_ge(glo_done, c * FB + (f + 1))
                nc.vector.tensor_tensor(gated[:, f % 2, :], silu[:, f % 2, :], ab_ps[:, f % 2, 1, :],
                                        ALU.mult).then_inc(g_done, 1)

            def g_low(c, f):
                dve.wait_ge(ghi_done, c * FB + (f + 1))
                nc.vector.tensor_tensor(g_lo[:, f, :], gated[:, f % 2, :], g_hi[:, f, :].bitcast(F32),
                                        ALU.subtract).then_inc(glo_done, 1)

            def add_rows(batch, j):
                c, s, _ = batch
                if j == 0:
                    dve.wait_ge(base_ready, c + 1)
                dve.wait_ge(y_done, c * NB + (j + 1 + NB))
                nc.vector.tensor_tensor(base[:, s, j, :], base[:, s, j, :], y_ps[:, j % 2, 0:D], ALU.add).then_inc(y_read, 1)

            first = (0, 0, 0)
            step(first)
            step(later(first, 1))
            dve.wait_ge(whi_done, 1)
            nc.vector.tensor_tensor(w13_lo[:], w_st[:], w13_hi[:].bitcast(F32), ALU.subtract).then_inc(w_ready, 1)
            third = later(first, 2)
            for n in range(2):
                statistics(third, n)
            aggregate(third)
            invert(third)
            x_low(first)
            for n in range(2):
                apply(third, n)
            for f in range(AHEAD):
                g_of(0, f)
            dve.wait_ge(whi_done, 2)
            nc.vector.tensor_tensor(w2_lo[:], w2_st, w2_hi[:].bitcast(F32), ALU.subtract).then_inc(w_ready, 1)

            def chunk(batch):
                c = batch[0]
                ahead = later(batch, LEAD)
                runs = exists(ahead) or exists(later(ahead, -1))
                g_low(c, 0)
                for f in range(AHEAD, FB):
                    g_of(c, f)
                    g_low(c, f - 1)
                    if f == 2 and runs and exists(ahead):
                        statistics(ahead, 0)
                    if f == 3 and runs:
                        statistics(ahead, 1)
                    if f == 4 and runs:
                        aggregate(ahead)
                    if f == TURN_H and exists(n := later(batch, 1)):
                        x_low(n)
                    if not exists(later(batch, 1)):
                        if f == 2:
                            dve.wait_ge(t_evac, logits_use(c) + 1)
                            route_first(nc, env, dve, r)
                        if f == 3:
                            route_rest(nc, env, dve, r)
                        if f == 4:
                            route_second(nc, env, dve, r)
                        if f == COUNT - 1:
                            route_totals(nc, env, dve, r)
                if exists(later(batch, 1)):
                    g_of(c + 1, 0)
                g_low(c, FB - 1)
                if exists(later(batch, 1)):
                    g_of(c + 1, 1)
                if runs:
                    invert(ahead)
                    apply(ahead, 0)
                add_rows(batch, 0)
                if runs:
                    apply(ahead, 1)
                if not exists(later(batch, 1)):
                    route_positions(nc, env, dve, r)
                add_rows(batch, 1)
                if not exists(later(batch, 1)):
                    route_slots(nc, env, dve, r)
                    route_gates(nc, env, dve, r)
                for j in range(2, NB):
                    add_rows(batch, j)

            over_chunks(dve, chunk)

        @block.gpsimd
        def _(pool):
            pool.sem_inc(h_ready, 2)
            for s in range(2):
                pool.sem_inc(h_out[s], 16)
            g_row, b_row = g_sb[:].broadcast_to([P, NB, D]), b_sb[:].broadcast_to([P, NB, D])
            make_constants(nc, env, pool, made)
            bo_row = bo_sb[:].broadcast_to([P, NB, D])
            pool.wait_ge(params_in, 64)

            def chunk(batch):
                k, s, half = batch
                pool.wait_ge(z_ready, k + 1)
                nc.gpsimd.tensor_tensor(z_sb[:, s], z_sb[:, s], g_row, ALU.mult).then_inc(z_scaled, 1)
                pool.wait_ge(z_scaled, k + 1)
                pool.wait_ge(h_out[s], half * 16 + 16)
                if not (known(k) and k < 2):
                    pool.wait_ge(t_done, h_use(k - 2) + 1)
                nc.gpsimd.tensor_tensor(h_sb[:, s], z_sb[:, s], b_row, ALU.add).then_inc(h_ready, 1)
                pool.wait_ge(base_in[s], half * 16 + 16)
                nc.gpsimd.tensor_tensor(base[:, s], base[:, s], bo_row, ALU.add).then_inc(base_ready, 1)

            for s in range(2):
                chunk((s, s, 0))
            with pool.Fori(1, B // 2) as i:
                for s in range(2):
                    chunk((i * 2 + s, s, i))


def attention_weights(env):
    wkv = env.Wkv.rearrange("(c p) (m n) -> m p c n", p=P, m=2)
    return [env.Wq.rearrange("(c p) n -> p c n", p=P), wkv[0], wkv[1], env.Wo.rearrange("(r p) n -> p r n", p=P)]


def attention_stage(env, room, n):
    flat = room[:, n % 2].rearrange("p k q -> p (k q)")
    return flat.rearrange("p (c n) -> p c n", n=env.INNER if n < 3 else env.D)


def phase_attention(nc, env, ahead):
    B, NB, KC, D, DH = env.B, env.NB, env.KC, env.D, env.DH
    N = NB * P
    PAIRS = HEADS // 2
    UNITS = PAIRS * NB
    INNER = HEADS * DH
    SCALE = float(DH) ** -0.5
    S_RING, P_RING = 2, 4
    STACKS = 16 * 8

    with ExitStack() as cx:
        def sb(name, shape, dt=F32):
            return cx.enter_context(nc.sbuf_tensor(name, shape, dt))

        def sem(name):
            return cx.enter_context(nc.semaphore(name))

        w_hi, w_lo = sb("a_w_hi", [P, 3, KC, INNER], F32R), sb("a_w_lo", [P, 3, KC, INNER], F32R)
        wo_hi, wo_lo = sb("a_wo_hi", [P, PAIRS, D], F32R), sb("a_wo_lo", [P, PAIRS, D], F32R)
        x_hi, x_lo = sb("a_x_hi", [P, KC, N], F32R), sb("a_x_lo", [P, KC, N], F32R)
        pT = (ahead.pT0, sb("a_pT1", [P, 2, NB, N]))
        splits = [(w_hi[:, 0], w_lo[:, 0]), (w_hi[:, 1], w_lo[:, 1]), (w_hi[:, 2], w_lo[:, 2]), (wo_hi[:], wo_lo[:])]
        ON_DVE = 2
        assert KC * INNER == PAIRS * D == NB * N

        def stage(n):
            return attention_stage(env, pT[n // 2], n)

        x_sb = ahead.tokens[:].rearrange("p s j d -> p (s j d)")[:, 0:KC * N].rearrange("p (k n) -> p k n", k=KC)
        v_sb = sb("a_v", [P, 2, NB, 2 * P])
        nat = {m: sb(f"a_{m}_halves", [P, 2, N], F32R) for m in "qk"}
        q_st = sb("a_q_stack", [P, 2, 2, N], F32R)
        k_st = sb("a_k_stack", [P, 2, 2, 2, N], F32R)
        probs = sb("a_probs", [P, P_RING, 2, N])
        o_hi = sb("a_o_hi", [P, 4, N], F32R)
        o_lo = sb("a_o_lo", [P, 4, N], F32R)
        part = sb("a_part", [P, 2, 2, D])
        ao = sb("a_ao", [P, NB, D])
        nmax = sb("a_nmax", [P, P_RING, 2])
        den = sb("a_den", [P, P_RING, 2])
        rden = sb("a_rden", [P, P_RING, 2])
        entry8 = sb("a_entry8", [P, TOP_K, NB, 3], I32)
        slot8 = sb("a_slot8", [P, TOP_K, NB], I32)
        s_ps = cx.enter_context(nc.psum_tensor("a_s_ps", [P, S_RING, 2, N], F32))
        pt_ps = cx.enter_context(nc.psum_tensor("a_pt_ps", [P, 2, N], F32))
        ot_ps = cx.enter_context(nc.psum_tensor("a_ot_ps", [P, N], F32))
        pj_ps = cx.enter_context(nc.psum_tensor("a_pj_ps", [P, N], F32))

        turnstile = sem("a_turnstile")
        w_in = [*ahead.qk_in, sem("a_wv_in"), sem("a_wo_in")]
        whi_done = sem("a_whi_done")
        w_ready = [sem(f"a_w_ready{n}") for n in range(4)]
        x_in = sem("a_x_in")
        xhi_done = sem("a_xhi_done")
        x_split = sem("a_x_split")
        pj_done = sem("a_pj_done")
        pj_evac = sem("a_pj_evac")
        hi_done = sem("a_hi_done")
        stacked = [sem("a_stacked0"), sem("a_stacked1")]
        s_done = sem("a_s_done")
        max_done = sem("a_max_done")
        masked = sem("a_masked")
        exp_done = sem("a_exp_done")
        den_step = sem("a_den_step")
        rden_ready = sem("a_rden_ready")
        normed = sem("a_normed")
        pt_done = sem("a_pt_done")
        pt_evac = sem("a_pt_evac")
        part_added = sem("a_part_added")
        ot_done = sem("a_ot_done")
        ohi_done = sem("a_ohi_done")
        ot_evac = sem("a_ot_evac")
        ao_out = sem("a_ao_out")
        slots_copied = sem("a_slots_copied")
        entered = sem("a_entered")
        scattered = sem("a_scattered")

        TAIL = 2 * NB + 2

        def known(b):
            return isinstance(b, int)

        def has_unit(b, u):
            return not known(b) or 0 <= b * UNITS + u < B * UNITS

        def has_pair(b, p):
            return has_unit(b, p * NB)

        def over_batches(eng, batch):
            batch(0, UNITS)
            with eng.Fori(1, B - 1) as b:
                batch(b, UNITS)
            batch(B - 1, UNITS)
            batch(B, TAIL)

        def piece_at(u):
            p, qb = divmod(u, NB)
            if qb >= 2:
                return ("qk"[qb - 2], p + 2, 0)
            return ("v", (p + 1) // 2, qb) if p % 2 == 1 else ("o", p // 2 - 2, qb)

        def first_pair(piece):
            return piece[1] * (1 if piece[0] in "qk" else 2)

        def has_piece(b, u):
            return has_pair(b, first_pair(piece_at(u)))

        def of_next(piece):
            return first_pair(piece) >= PAIRS

        FIRST_SCORES = 3
        AHEAD = [("q", 0, 0), ("k", 0, 0), ("v", 0, 0), ("v", 0, 1), ("q", 1, 0), ("k", 1, 0)]

        def uses_before(b, u):
            if not known(b):
                return b * UNITS + (u + uses_before(1, 0) - UNITS)
            return len(AHEAD) + len([n for n in range(b * UNITS + u) if has_piece(*divmod(n, UNITS))])

        def highs_before(b, u):
            return b * (2 * PAIRS) + (4 + 2 * (u // NB) + max(u % NB - 2, 0))

        block = cx.enter_context(nc.Block())

        @block.tensor
        def _(pe):
            pe.sem_inc(pt_done, P_RING)
            pe.sem_inc(ot_done, 2)

            def project(piece, used, batches):
                kind, which, part = piece
                pe.wait_ge(x_split, batches)
                if not isinstance(used, int) or used > 0:
                    pe.wait_ge(pj_evac, used)
                if kind in "qk":
                    m, r = "qk".index(kind), which % PAIRS
                    passes = [(w, x, c) for c in range(KC) for w, x in ((w_hi, x_hi), (w_hi, x_lo), (w_lo, x_hi))]
                    for n, (w, x, c) in enumerate(passes):
                        last = nc.tensor.matmul(pj_ps[:], w[:, m, c, r * P:(r + 1) * P], x[:, c, :],
                                                start=n == 0, stop=n == len(passes) - 1)
                else:
                    g = which % (PAIRS // 2)
                    passes = [(w, x, c) for c in range(KC) for w, x in ((w_hi, x_hi), (w_lo, x_hi), (w_hi, x_lo))]
                    for j in range(2):
                        t = 2 * part + j
                        for n, (w, x, c) in enumerate(passes):
                            last = nc.tensor.matmul(pj_ps[:, j * 2 * P:(j + 1) * 2 * P], x[:, c, t * P:(t + 1) * P],
                                                    w[:, 2, c, g * 2 * P:(g + 1) * 2 * P],
                                                    start=n == 0, stop=n == len(passes) - 1)
                last.then_inc(pj_done, 1)

            def scores(b, u):
                p, qb = divmod(u, NB)
                if not (known(b) and b * UNITS + u < S_RING):
                    pe.wait_ge(exp_done, b * UNITS + (u - S_RING + 1))
                if qb == 0:
                    pe.wait_ge(stacked[p % 2], b * (STACKS * PAIRS // 2) + STACKS * (p // 2 + 1))
                for h in range(2):
                    lhsT = q_st[:, p % 2, h, qb * P:(qb + 1) * P]
                    nc.tensor.matmul(s_ps[:, u % S_RING, h, :], lhsT, k_st[:, p % 2, h, 0, :], start=True, stop=False)
                    last = nc.tensor.matmul(s_ps[:, u % S_RING, h, :], lhsT, k_st[:, p % 2, h, 1, :], start=False, stop=True)
                last.then_inc(s_done, 1)

            def turn(b, u):
                qb = u % NB
                pe.wait_ge(normed, b * UNITS + (u + 1))
                pe.wait_ge(pt_evac, b * UNITS + (u + 1))
                for h in range(2):
                    for k in range(qb + 1):
                        last = nc.tensor.transpose(pt_ps[:, h, k * P:(k + 1) * P], probs[:, u % P_RING, h, k * P:(k + 1) * P],
                                                   env.ident[:])
                last.then_inc(pt_done, 1)

            def values(b, p, ks):
                if ks[0] == 0:
                    pe.wait_ge(pt_evac, b * UNITS + (NB * p + NB - 1 + 2))
                    pe.wait_ge(pj_evac, uses_before(b, 2 * NB * (p // 2)))
                    pe.wait_ge(ot_evac, b * PAIRS + (p + 1))
                for k in ks:
                    for h in range(2):
                        col = (p % 2) * P + h * DH
                        last = nc.tensor.matmul(ot_ps[h * DH:(h + 1) * DH, k * P:N],
                                                v_sb[:, (p // 2) % 2, k, col:col + DH], pT[p % 2][:, h, k, k * P:N],
                                                start=k == 0, stop=k == NB - 1)
                if ks[-1] == NB - 1:
                    last.then_inc(ot_done, 1)

            def out_project(b, g, half, used):
                pe.wait_ge(pj_evac, used)
                pe.wait_ge(ot_evac, b * PAIRS + (2 * g + 3))
                passes = [(r, o, w) for r in (2 * g, 2 * g + 1) for o, w in ((o_hi, wo_hi), (o_hi, wo_lo), (o_lo, wo_hi))]
                for j in range(2):
                    t = 2 * half + j
                    for n, (r, o, w) in enumerate(passes):
                        last = nc.tensor.matmul(pj_ps[:, j * D:(j + 1) * D], o[:, r % 4, t * P:(t + 1) * P], w[:, r % PAIRS, :],
                                                start=j == 0 and n == 0, stop=n == len(passes) - 1, skip_group_check=True)
                last.then_inc(pj_done, 1)

            for n, piece in enumerate(AHEAD):
                pe.wait_ge(w_ready["qkv".index(piece[0])], 1)
                project(piece, n, 1)
                if n == FIRST_SCORES:
                    scores(0, 0)
            scores(0, 1)
            pe.wait_ge(w_ready[3], 1)

            def batch(b, steps):
                for u in range(steps):
                    p, qb = divmod(u, NB)
                    if has_unit(b, u + S_RING):
                        scores(b, u + S_RING)
                    if has_unit(b, u - 1):
                        turn(b, u - 1)
                    if has_piece(b, u):
                        piece = piece_at(u)
                        if piece[0] == "o":
                            out_project(b, piece[1], piece[2], uses_before(b, u))
                        else:
                            project(piece, uses_before(b, u), b + 1 + of_next(piece))
                    if qb in (1, 2) and has_pair(b, p - 1):
                        values(b, p - 1, (2 * qb - 2, 2 * qb - 1))

            over_batches(pe, batch)

        @block.vector
        def _(dve):
            dve.sem_inc(ot_evac, 1)

            def split_x(batches):
                dve.wait_ge(xhi_done, batches)
                nc.vector.tensor_tensor(x_lo[:], x_sb[:], x_hi[:].bitcast(F32), ALU.subtract).then_inc(x_split, 1)

            def low(piece, highs):
                kind, which, part = piece
                if kind not in "qk":
                    return
                hi, lo = nat[kind][:, 0, :], nat[kind][:, 1, :]
                dve.wait_ge(hi_done, highs + 1)
                if kind == "q":
                    nc.vector.scalar_tensor_tensor(out=lo, in0=pj_ps[:], scalar=SCALE, in1=hi.bitcast(F32),
                                                   op0=ALU.mult, op1=ALU.subtract).then_inc(pj_evac, 1)
                else:
                    nc.vector.tensor_tensor(lo, pj_ps[:], hi.bitcast(F32), ALU.subtract).then_inc(pj_evac, 1)

            def maxima(b, u):
                dve.wait_ge(s_done, b * UNITS + (u + 1))
                nc.vector.tensor_reduce(nmax[:, u % P_RING, :], s_ps[:, u % S_RING], AX_X, ALU.max, negate=True)\
                    .then_inc(max_done, 1)

            def mask(b, u):
                qb = u % NB
                dve.wait_ge(max_done, b * UNITS + (u + 1))
                diagonal = s_ps[:, u % S_RING, :, qb * P:(qb + 1) * P]
                nc.vector.tensor_tensor(diagonal, diagonal, env.causal[:], ALU.add).then_inc(masked, 1)

            def add_eps(b, u):
                dve.wait_ge(exp_done, b * UNITS + (u + 1))
                d = den[:, u % P_RING, :]
                nc.vector.tensor_scalar(d, d, SOFTMAX_EPS, None, ALU.add).then_inc(den_step, 1)

            def invert(b, u):
                dve.wait_ge(den_step, b * UNITS + (u + 1))
                nc.vector.reciprocal(rden[:, u % P_RING, :], den[:, u % P_RING, :]).then_inc(rden_ready, 1)

            def normalise(b, u):
                dve.wait_ge(rden_ready, b * UNITS + (u + 1))
                for h in range(2):
                    pr = probs[:, u % P_RING, h, 0:(u % NB + 1) * P]
                    last = nc.vector.tensor_scalar(pr, pr, rden[:, u % P_RING, h:h + 1], None, ALU.mult)
                last.then_inc(normed, 1)

            def output_low(b, p):
                dve.wait_ge(ohi_done, b * PAIRS + (p + 1))
                nc.vector.tensor_tensor(o_lo[:, p % 4, :], ot_ps[:], o_hi[:, p % 4, :].bitcast(F32),
                                        ALU.subtract).then_inc(ot_evac, 1)

            def weights_low(n):
                hi, lo = splits[n]
                dve.wait_ge(whi_done, n + 1)
                nc.vector.tensor_tensor(lo, stage(n), hi.bitcast(F32), ALU.subtract).then_inc(w_ready[n], 1)

            weights_low(0)
            split_x(1)
            weights_low(1)
            highs = 0
            for n, piece in enumerate(AHEAD):
                low(piece, highs)
                highs += piece[0] != "v"
                if n == FIRST_SCORES:
                    maxima(0, 0)
                    mask(0, 0)
            maxima(0, 1)
            mask(0, 1)
            for step in (add_eps, invert, normalise):
                step(0, 0)

            def batch(b, steps):
                for u in range(steps):
                    p, qb = divmod(u, NB)
                    scored, summed = has_unit(b, u + S_RING), has_unit(b, u + 1)
                    if scored:
                        maxima(b, u + S_RING)
                    if summed:
                        add_eps(b, u + 1)
                    if scored:
                        mask(b, u + S_RING)
                    if summed:
                        invert(b, u + 1)
                    if has_piece(b, u):
                        low(piece_at(u), highs_before(b, u))
                    if summed:
                        normalise(b, u + 1)
                    if qb == 3 and has_pair(b, p - 1):
                        output_low(b, p - 1)
                    if u == UNITS - 2 * NB and has_unit(b, UNITS):
                        split_x(b + 2)

            over_batches(dve, batch)

        @block.scalar
        def _(act):
            act.sem_inc(pt_evac, 1)

            def split_x(batches, pj):
                act.wait_ge(x_in, batches * 16)
                if pj is not None:
                    act.wait_ge(pj_done, pj)
                nc.scalar.copy(x_hi[:], x_sb[:]).then_inc(xhi_done, 1)

            def high(piece, used, stack_before, b):
                kind, which, half = piece
                act.wait_ge(pj_done, used + 1)
                two_tiles = pj_ps[:].rearrange("p (j n) -> p j n", j=2)
                if kind == "o":
                    act.wait_ge(part_added, b * PAIRS + (2 * which + half + 1))
                    nc.scalar.copy(part[:, half], two_tiles).then_inc(pj_evac, 1)
                elif kind == "v":
                    if b is not None:
                        act.wait_ge(ot_done, b * PAIRS + 2 * which)
                    nc.scalar.copy(v_sb[:, which % 2, 2 * half:2 * half + 2, :], two_tiles).then_inc(pj_evac, 1)
                else:
                    if stack_before is not None:
                        act.wait_ge(*stack_before)
                    nc.scalar.activation(nat[kind][:, 0, :], pj_ps[:], ACT.Copy, scale=SCALE if kind == "q" else 1.0)\
                        .then_inc(hi_done, 1)

            def exps(b, u):
                act.wait_ge(masked, b * UNITS + (u + 1))
                act.wait_ge(pt_done, b * UNITS + (u + 1))
                n = (u % NB + 1) * P
                for h in range(2):
                    last = nc.scalar.activation(probs[:, u % P_RING, h, 0:n], s_ps[:, u % S_RING, h, 0:n], ACT.Exp,
                                                bias=nmax[:, u % P_RING, h:h + 1], accum_out=den[:, u % P_RING, h:h + 1])
                last.then_inc(exp_done, 1)

            def turned(b, u):
                p, qb = divmod(u, NB)
                act.wait_ge(pt_done, b * UNITS + (u + 1 + P_RING))
                if qb == 0:
                    act.wait_ge(ot_done, b * PAIRS + (p + 1))
                src = pt_ps[:, :, 0:(qb + 1) * P].rearrange("p h (k q) -> p h k q", q=P)
                nc.scalar.copy(pT[p % 2][:, :, 0:qb + 1, qb * P:(qb + 1) * P], src).then_inc(pt_evac, 1)

            def output_high(b, p):
                act.wait_ge(ot_done, b * PAIRS + (p + 3))
                if has_pair(b, p - 4):
                    act.wait_ge(pj_done, uses_before(b, 2 * NB * (p // 2) + 2))
                nc.scalar.copy(o_hi[:, p % 4, :], ot_ps[:]).then_inc(ohi_done, 1)

            def weights_high(n):
                act.wait_ge(w_in[n], 16)
                nc.scalar.copy(splits[n][0], stage(n)).then_inc(whi_done, 1)

            weights_high(0)
            split_x(1, None)
            weights_high(1)
            for n, piece in enumerate(AHEAD):
                if n in (0, 3):
                    weights_high(2 if n == 0 else 3)
                high(piece, n, (stacked[0], STACKS) if piece[1] == 1 and piece[0] in "qk" else None, None)
                if n == FIRST_SCORES:
                    exps(0, 0)
            exps(0, 1)
            for ready in w_ready:
                act.wait_ge(ready, 1)

            def batch(b, steps):
                for u in range(steps):
                    p, qb = divmod(u, NB)
                    if has_unit(b, u - 1):
                        turned(b, u - 1)
                    if has_piece(b, u):
                        high(piece_at(u), uses_before(b, u),
                             (stacked[(p + 1) % 2], b * (STACKS * PAIRS // 2) + STACKS * ((p + 1) // 2 + 1)), b)
                    if has_unit(b, u + S_RING):
                        exps(b, u + S_RING)
                    if qb == 2 and has_pair(b, p - 1):
                        output_high(b, p - 1)
                    if u == UNITS - 2 * NB and has_unit(b, UNITS):
                        split_x(b + 2, uses_before(b, u))

            over_batches(act, batch)

        @block.gpsimd
        def _(pool):
            PER = TOP_K * NB
            entries = env.entry[:].rearrange("p (k t) o -> p k t o", k=TOP_K)
            slots = env.write_slot[:].rearrange("p (k t) -> p k t", k=TOP_K)
            out = env.out.rearrange("b (j p) d -> b p j d", p=P)
            pool.sem_inc(part_added, 2)
            for n in range(ON_DVE, len(splits)):
                hi, lo = splits[n]
                pool.wait_ge(whi_done, n + 1)
                nc.gpsimd.tensor_tensor(lo, stage(n), hi.bitcast(F32), ALU.subtract).then_inc(w_ready[n], 1)

            def enter(b):
                nc.gpsimd.tensor_copy(entry8[:], entries[:, :, bass.ds(b * NB, NB)]).then_inc(slots_copied, 1)
                nc.gpsimd.tensor_copy(slot8[:], slots[:, :, bass.ds(b * NB, NB)]).then_inc(slots_copied, 1)
                pool.wait_ge(slots_copied, b * 2 + 2)
                pool.sem_inc(turnstile, 1)
                for n in range(PER):
                    k, j = divmod(n, NB)
                    nc.gpsimd.indirect_dma_start(
                        out=env.queue_dram, out_offset=bass.IndirectOffsetOnAxis(ap=slot8[:, k, j:j + 1].bitcast(U32), axis=0),
                        in_=entry8[:, k, j, :], in_offset=None, bounds_check=env.SLOTS - 1, oob_is_err=False,
                        compute_op=ALU.bypass).then_inc(scattered, 16)
                pool.wait_ge(scattered, b * (16 * PER) + 16 * PER)

            def add_part(b, g, half, used):
                pool.wait_ge(pj_evac, used + 1)
                pool.sem_inc(turnstile, 1)
                both = ao[:, 2 * half:2 * half + 2, :]
                if g % 4 == 0:
                    nc.gpsimd.tensor_copy(both, part[:, half]).then_inc(part_added, 1)
                else:
                    pool.wait_ge(part_added, b * PAIRS + (2 * g + half + 1))
                    nc.gpsimd.tensor_tensor(both, both, part[:, half], ALU.add).then_inc(part_added, 1)

            def add_batch(b):
                pool.wait_ge(part_added, b * PAIRS + 2)
                pool.sem_inc(turnstile, 1)
                at = out[b - 1] if known(b) else out[bass.ds(b - 1, 1)].rearrange("o p j d -> (o p) j d")
                nc.gpsimd.dma_start(at, ao[:], accum_op=ALU.add).then_inc(ao_out, 16)

            def batch(b, steps):
                for u in range(steps):
                    kind, g, half = piece_at(u)
                    if u == 2 * NB + 2 and has_unit(b, 0):
                        enter(b)
                        if not has_unit(b, UNITS):
                            pool.sem_inc(entered, 1)
                    if kind != "o" or not has_piece(b, u):
                        continue
                    if g == 0 and half == 0 and has_pair(b, -1):
                        pool.wait_ge(ao_out, b * 16)
                        pool.sem_inc(turnstile, 1)
                    add_part(b, g, half, uses_before(b, u))
                    if g == -1 and half == 1:
                        add_batch(b)
                if not has_unit(b, UNITS) and has_unit(b, 0):
                    pool.wait_ge(x_split, B)
                    gather_first(nc, env, pool, ahead)

            over_batches(pool, batch)
            pool.wait_ge(ao_out, B * 16)

        @block.sync
        def _(sp):

            sp.dma_start(x_sb[:], env.xnT_dram[0]).then_inc(x_in, 16)
            for n in (2, 3):
                sp.dma_start(stage(n), attention_weights(env)[n]).then_inc(w_in[n], 16)

            def one(t, b):
                return t[b] if isinstance(b, int) else t[bass.ds(b, 1)].rearrange("o p j d -> (o p) j d")

            def raw(t):
                return t.bitcast(F32)

            HALF = (slice(0, DH), slice(DH, P))

            def stack_q(par):
                for h in range(2):
                    for part in range(2):
                        sp.dma_start(raw(q_st[HALF[part], par, h, :]), raw(nat["q"][HALF[h], part, :])).then_inc(stacked[par], 16)

            def stack_k(par):
                for h in range(2):
                    for to in range(2):
                        sp.dma_start(raw(k_st[HALF[to], par, h]), raw(nat["k"][HALF[h]])).then_inc(stacked[par], 16)

            for par in range(2):
                sp.wait_ge(pj_evac, (1, 5)[par])
                stack_q(par)
                sp.wait_ge(pj_evac, (2, 6)[par])
                stack_k(par)

            def batch(b, steps):
                if has_unit(b, UNITS):
                    sp.wait_ge(x_split, b + 1)
                    sp.dma_start(x_sb[:], one(env.xnT_dram, b + 1)).then_inc(x_in, 16)
                for u in range(2, steps, NB):
                    p = u // NB
                    if not has_piece(b, u):
                        continue
                    sp.wait_ge(s_done, b * UNITS + NB * (p + 1))
                    sp.sem_inc(turnstile, 1)
                    sp.wait_ge(pj_evac, uses_before(b, u) + 1)
                    stack_q(p % 2)
                    sp.wait_ge(pj_evac, uses_before(b, u) + 2)
                    stack_k(p % 2)

            over_batches(sp, batch)
            sp.wait_ge(entered, 1)
            load_first_queues(nc, env, sp, ahead)
            sp.wait_ge(ot_done, B * PAIRS - 2 + 3)
            load_w13(nc, env, sp, ahead, 0)


def chunk_blocks(env):
    W = env.CAP // 2
    return [(t, min(P, W - t)) for t in range(0, W, P)]


def of_expert(t, e):
    t = t[e] if isinstance(e, int) else t[bass.ds(e, 1)].rearrange("o a b -> (o a) b")
    return t.rearrange("(c p) n -> p c n", p=P)


def load_w13(nc, env, sp, ahead, e):
    for m, t in enumerate((env.W1, env.W3)):
        sp.dma_start(ahead.w13_stage[:, m], of_expert(t, e)).then_inc(ahead.w_in[m], 16)


def load_queue(nc, env, sp, ahead, c, q):
    for j, (t, n_t) in enumerate(chunk_blocks(env)):
        at = slice(c * env.CAP // 2 + t, c * env.CAP // 2 + t + n_t) if isinstance(c, int) else bass.ds(c * (env.CAP // 2) + t, n_t)
        sp.dma_start(ahead.queue[0:n_t, q, j, :], env.queue_dram[at, :]).then_inc(ahead.queue_in[q], 16)


def load_first_queues(nc, env, sp, ahead):
    for c in range(2):
        load_queue(nc, env, sp, ahead, c, c)


def gather_tokens(nc, env, ahead, q, gathered):
    for j, (t, n_t) in enumerate(chunk_blocks(env)):
        nc.gpsimd.indirect_dma_start(
            out=ahead.tokens[0:n_t, q % 2, j, :], out_offset=None, in_=env.h_dram,
            in_offset=bass.IndirectOffsetOnAxis(ap=ahead.queue[0:n_t, q, j, 0:1].bitcast(U32), axis=0),
            compute_op=ALU.bypass).then_inc(gathered, 16)


def gather_first(nc, env, pool, ahead):
    loads = 16 * len(chunk_blocks(env))
    for c in range(2):
        pool.wait_ge(ahead.queue_in[c], loads)
        gather_tokens(nc, env, ahead, c, ahead.first_gathered)
    pool.wait_ge(ahead.first_gathered, 2 * loads)


def phase_routed(nc, env, ahead):
    KC, D, E, F = env.KC, env.D, env.E, env.F
    FB = F // P
    W = env.CAP // 2
    BLOCKS = chunk_blocks(env)
    R = len(BLOCKS)
    TOKENS = env.tiles * P
    AHEAD = 2
    TURN_AT = 5
    PIECES = 6
    SPLIT_AT = (2, 4, 7)

    with ExitStack() as cx:
        def sb(n, shape, dt=F32):
            return cx.enter_context(nc.sbuf_tensor("e_" + n, shape, dt))

        def ps(n, shape):
            return cx.enter_context(nc.psum_tensor("e_" + n, shape, F32))

        def sem(n):
            return cx.enter_context(nc.semaphore("e_" + n))

        w13_hi = sb("w13_hi", [P, 2, 2, KC, F], F32R)
        w13_lo = sb("w13_lo", [P, 2, 2, KC, F], F32R)
        w2_hi = sb("w2_hi", [P, 2, FB, D], F32R)
        w2_lo = sb("w2_lo", [P, 2, FB, D], F32R)
        w13_st = ahead.w13_stage
        w2_st = sb("w2_st", [P, FB, D])
        x_hi = sb("x_hi", [P, 2, KC, W], F32R)
        x_lo = sb("x_lo", [P, 2, KC, W], F32R)
        silu = sb("silu", [P, 2, W])
        gated = sb("gated", [P, 2, W])
        g_hi = sb("g_hi", [P, FB, W], F32R)
        g_lo = sb("g_lo", [P, FB, W], F32R)
        queue, xg = ahead.queue, ahead.tokens
        y_sb = sb("y_sb", [P, 2, R, D])
        ab_ps = ps("ab_ps", [P, 2, 2, 512])
        y_ps = ps("y_ps", [P, 2, 512])
        xT_ps = ps("xT_ps", [P, KC, 512])

        turnstile = sem("turnstile")
        w_in, queue_in = ahead.w_in, ahead.queue_in
        whi_done = sem("whi_done")
        wlo_done = sem("wlo_done")
        gathered = sem("gathered")
        xg_ready = sem("xg_ready")
        xT_done = sem("xT_done")
        xhi_done = sem("xhi_done")
        x_ready = sem("x_ready")
        ab_done = sem("ab_done")
        silu_done = sem("silu_done")
        g_done = sem("g_done")
        ghi_done = sem("ghi_done")
        glo_done = sem("glo_done")
        y_done = sem("y_done")
        y_read = sem("y_read")
        y_free = sem("y_free")
        added = sem("added")

        def numbered(c):
            return c, c // 2, c % 4, c // 4

        PEELED = E - (E - 1) // 2 * 2

        def over_chunks(eng, chunk):
            with eng.Fori(0, (E - 1) // 2) as i:
                for q in range(4):
                    chunk((i * 4 + q, i * 2 + q // 2, q, i))
            for c in range(2 * (E - PEELED), 2 * E):
                chunk(numbered(c))

        def later(chunk, n):
            c, e, q, i = chunk
            return c + n, e + (q % 2 + n) // 2, (q + n) % 4, i + (q + n) // 4

        def exists(chunk):
            return not isinstance(chunk[0], int) or chunk[0] < 2 * E

        def pieces(chunk):
            if not exists(later(chunk, 2)):
                return {}
            first = len(SPLIT_AT) * (chunk[2] % 2)
            return {f: first + n for n, f in enumerate(SPLIT_AT)}

        def piece(e_slot, n):
            if n < 4:
                m, k = divmod(n, 2)
                return w13_st[:, m, k], w13_hi[:, e_slot, m, k], w13_lo[:, e_slot, m, k]
            half = slice((n - 4) * FB // 2, (n - 3) * FB // 2)
            return w2_st[:, half], w2_hi[:, e_slot, half], w2_lo[:, e_slot, half]

        block = cx.enter_context(nc.Block())

        @block.sync
        def _(sp):
            def load_w2(e):
                sp.dma_start(w2_st[:], of_expert(env.W2, e)).then_inc(w_in[2], 16)

            load_w2(0)

            def chunk(now):
                c, e, q, _ = now
                if exists(n := later(now, 2)):
                    sp.wait_ge(y_free, c + 1)
                    load_queue(nc, env, sp, ahead, n[0], n[2])
                if q % 2 == 0 and exists(later(now, 2)):
                    sp.wait_ge(wlo_done, e * PIECES + PIECES)
                    load_w13(nc, env, sp, ahead, e + 1)
                    load_w2(e + 1)

            over_chunks(sp, chunk)

        @block.tensor
        def _(pe):
            pe.sem_inc(y_done, R)

            def hidden(chunk, blocks):
                c, e, q, _ = chunk
                w_slot, s = q // 2, q % 2
                if blocks[0] == 0:
                    pe.wait_ge(x_ready, c + 1)
                    if s == 0:
                        pe.wait_ge(wlo_done, e * PIECES + 4)
                for f in blocks:
                    pe.wait_ge(g_done, c * FB + (f + 1))
                    for m in range(2):
                        passes = [(w, x, k) for k in range(KC) for w, x in ((w13_hi, x_hi), (w13_hi, x_lo), (w13_lo, x_hi))]
                        for n, (w, x, k) in enumerate(passes):
                            last = nc.tensor.matmul(ab_ps[:, f % 2, m, 0:W], w[:, w_slot, m, k, f * P:(f + 1) * P], x[:, s, k, :],
                                                    start=n == 0, stop=n == len(passes) - 1)
                    last.then_inc(ab_done, 1)

            def rows(chunk):
                c, e, q, _ = chunk
                w_slot, s = q // 2, q % 2
                if s == 0:
                    pe.wait_ge(wlo_done, e * PIECES + PIECES)
                pe.wait_ge(glo_done, c * FB + (FB + 1))
                for j, (t, n_t) in enumerate(BLOCKS):
                    pe.wait_ge(y_read, c * R + (j + 1))
                    passes = [(a, w, f) for f in range(FB) for a, w in ((g_hi, w2_hi), (g_hi, w2_lo), (g_lo, w2_hi))]
                    for n, (a, w, f) in enumerate(passes):
                        if j == 0 and n == len(passes) - 3:
                            pe.wait_ge(glo_done, c * FB + (FB + 2))
                        last = nc.tensor.matmul(y_ps[0:n_t, (s * R + j) % 2, 0:D], a[:, f, t:t + n_t], w[:, w_slot, f, :],
                                                start=n == 0, stop=n == len(passes) - 1)
                    last.then_inc(y_done, 1)

            def turn(chunk):
                c, e, q, _ = chunk
                s = q % 2
                pe.wait_ge(xg_ready, c + 1)
                if not isinstance(c, int) or c > 0:
                    pe.wait_ge(x_ready, c)
                for k in range(KC):
                    for j, (t, n_t) in enumerate(BLOCKS):
                        last = nc.tensor.transpose(xT_ps[:, k, t:t + n_t], xg[0:n_t, s, j, k * P:(k + 1) * P],
                                                   env.ident[0:n_t, 0:n_t])
                last.then_inc(xT_done, 1)

            first = numbered(0)
            turn(first)
            hidden(first, range(AHEAD))

            def chunk(now):
                following = later(now, 1)
                hidden(now, range(AHEAD, TURN_AT))
                if exists(following):
                    turn(following)
                hidden(now, range(TURN_AT, FB))
                if exists(following):
                    hidden(following, range(AHEAD))
                rows(now)

            over_chunks(pe, chunk)

        @block.scalar
        def _(act):
            def split_w(e, e_slot, n):
                act.wait_ge(w_in[n // 2], e * 16 + 16)
                stage, hi, _ = piece(e_slot, n)
                nc.scalar.copy(hi, stage).then_inc(whi_done, 1)

            def split_x(chunk):
                c, _, q, _ = chunk
                act.wait_ge(xT_done, c + 1)
                nc.scalar.copy(x_hi[:, q % 2], xT_ps[:, :, 0:W]).then_inc(xhi_done, 1)

            def silu_of(c, f):
                act.wait_ge(ab_done, c * FB + (f + 1))
                nc.scalar.activation(silu[:, f % 2, :], ab_ps[:, f % 2, 0, 0:W], ACT.Silu).then_inc(silu_done, 1)

            def g_high(c, f):
                act.wait_ge(g_done, c * FB + (f + 3))
                if f == 0:
                    act.wait_ge(y_done, c * R + R)
                nc.scalar.copy(g_hi[:, f, :], gated[:, f % 2, :]).then_inc(ghi_done, 1)

            def rows_out(chunk):
                c, _, q, i = chunk
                s = q % 2
                act.wait_ge(queue_in[q], i * (16 * R) + 16 * R)
                act.wait_ge(y_free, c + 1)
                for j, (t, n_t) in enumerate(BLOCKS):
                    act.wait_ge(y_done, c * R + (j + 1 + R))
                    nc.scalar.mul(y_sb[0:n_t, s, j, :], y_ps[0:n_t, (s * R + j) % 2, 0:D],
                                  queue[0:n_t, q, j, 2:3].bitcast(F32)).then_inc(y_read, 1)

            act.sem_inc(y_read, 2)
            first = numbered(0)
            for n in range(PIECES):
                if n == 2:
                    split_x(first)
                split_w(0, 0, n)
            for f in range(AHEAD):
                silu_of(0, f)

            def chunk(now):
                c, e, q, _ = now
                following = later(now, 1)
                splits = pieces(now)
                g_high(c, 0)
                for f in range(AHEAD, FB):
                    silu_of(c, f)
                    g_high(c, f - 1)
                    if f == TURN_AT and exists(following):
                        split_x(following)
                    if f in splits:
                        split_w(e + 1, 1 - q // 2, splits[f])
                if exists(following):
                    silu_of(c + 1, 0)
                g_high(c, FB - 1)
                if exists(following):
                    silu_of(c + 1, 1)
                rows_out(now)

            over_chunks(act, chunk)

        @block.vector
        def _(dve):
            dve.sem_inc(g_done, 2)
            dve.sem_inc(glo_done, 2)

            def split_w(e, e_slot, n):
                dve.wait_ge(whi_done, e * PIECES + (n + 1))
                stage, hi, lo = piece(e_slot, n)
                nc.vector.tensor_tensor(lo, stage, hi.bitcast(F32), ALU.subtract).then_inc(wlo_done, 1)

            def split_x(chunk):
                c, _, q, _ = chunk
                dve.wait_ge(xhi_done, c + 1)
                nc.vector.tensor_tensor(x_lo[:, q % 2], xT_ps[:, :, 0:W], x_hi[:, q % 2].bitcast(F32),
                                        ALU.subtract).then_inc(x_ready, 1)

            def g_of(c, f):
                dve.wait_ge(silu_done, c * FB + (f + 1))
                dve.wait_ge(glo_done, c * FB + (f + 1))
                nc.vector.tensor_tensor(gated[:, f % 2, :], silu[:, f % 2, :], ab_ps[:, f % 2, 1, 0:W],
                                        ALU.mult).then_inc(g_done, 1)

            def g_low(c, f):
                dve.wait_ge(ghi_done, c * FB + (f + 1))
                nc.vector.tensor_tensor(g_lo[:, f, :], gated[:, f % 2, :], g_hi[:, f, :].bitcast(F32),
                                        ALU.subtract).then_inc(glo_done, 1)

            first = numbered(0)
            for n in range(PIECES):
                if n == 2:
                    split_x(first)
                split_w(0, 0, n)
            for f in range(AHEAD):
                g_of(0, f)

            def chunk(now):
                c, e, q, _ = now
                following = later(now, 1)
                splits = pieces(now)
                g_low(c, 0)
                for f in range(AHEAD, FB):
                    g_of(c, f)
                    g_low(c, f - 1)
                    if f == TURN_AT and exists(following):
                        split_x(following)
                    if f in splits:
                        split_w(e + 1, 1 - q // 2, splits[f])
                if exists(following):
                    g_of(c + 1, 0)
                g_low(c, FB - 1)
                if exists(following):
                    g_of(c + 1, 1)

            over_chunks(dve, chunk)

        @block.gpsimd
        def _(pool):
            pool.sem_inc(y_free, 2)
            pool.sem_inc(xg_ready, 2)

            def gather(chunk):
                c, e, q, i = chunk
                pool.wait_ge(queue_in[q], i * (16 * R) + 16 * R)
                pool.sem_inc(turnstile, 1)
                pool.wait_ge(xT_done, c - 1)
                pool.sem_inc(turnstile, 1)
                gather_tokens(nc, env, ahead, q, gathered)
                pool.wait_ge(gathered, (c - 1) * (16 * R))
                pool.sem_inc(xg_ready, 1)

            def add_rows(chunk):
                c, _, q, _ = chunk
                pool.wait_ge(y_read, c * R + (R + 2))
                pool.sem_inc(turnstile, 1)
                for j, (t, n_t) in enumerate(BLOCKS):
                    nc.gpsimd.indirect_dma_start(
                        out=env.out_rows, out_offset=bass.IndirectOffsetOnAxis(ap=queue[0:n_t, q, j, 1:2].bitcast(U32), axis=0),
                        in_=y_sb[0:n_t, q % 2, j, :], in_offset=None, bounds_check=TOKENS - 1, oob_is_err=False,
                        compute_op=ALU.add).then_inc(added, 16)
                pool.wait_ge(added, c * (16 * R) + 16 * R)
                pool.sem_inc(y_free, 1)

            def chunk(now):
                if exists(n := later(now, 2)):
                    gather(n)
                add_rows(now)

            over_chunks(pool, chunk)


def transformer_layer(nc, x, Wq, Wkv, Wo, bo, ln_g, ln_b, Wr, W1, W3, W2, W1s, W3s, W2s, out):
    B, N, D = x.shape
    E, _, F = W1.shape
    NB, tokens = N // P, B * N
    CAP = -(-5 * CAPACITY_TOKENS * TOP_K // (4 * E))
    SLOTS = -(-E * CAP // P) * P
    assert N % P == 0 and D % P == 0 and B % 2 == 0 and CAP % 2 == 0

    with ExitStack() as cx:
        def sb(name, shape, dt=F32):
            return cx.enter_context(nc.sbuf_tensor(name, shape, dt))

        def dram(name, shape, dt=F32):
            return nc.dram_tensor(name, shape, dt, kind="Internal").ap()

        T = tokens // P
        env = Env(
            B=B, NB=NB, KC=D // P, D=D, E=E, F=F, DH=Wq.shape[1] // HEADS, CAP=CAP, SLOTS=SLOTS, INNER=Wq.shape[1], tiles=T,
            x=x, Wq=Wq, Wkv=Wkv, Wo=Wo, ln_g=ln_g, ln_b=ln_b, Wr=Wr, bo=bo, W1=W1, W3=W3, W2=W2, W1s=W1s, W3s=W3s, W2s=W2s,
            out=out, out_rows=out.rearrange("b n d -> (b n) d"),
            xnT_dram=dram("xnT_dram", (B, P, D // P, N)), h_dram=dram("h_dram", (tokens, D)),
            queue_dram=dram("queue_dram", (SLOTS, 3), I32),
            ident=sb("ident", [P, P]), upper=sb("upper", [P, P], BF16), before=sb("before", [P, P], BF16),
            ones=sb("ones", [P, P], BF16), causal=sb("causal", [P, 2, P]), logits=sb("logits", [P, T, E]),
            weight=sb("weight", [P, T, E]), empty=sb("empty", [P, SLOTS // P, 3], I32),
            entry=sb("entry", [P, TOP_K * T, 3], I32), write_slot=sb("write_slot", [P, TOP_K * T], I32))

        KC, R = D // P, len(chunk_blocks(env))
        pT0 = sb("pT0", [P, 2, NB, N])
        room = pT0[:].rearrange("p h k q -> p (h k q)")
        assert 2 * KC * F <= 2 * NB * N
        ahead = Ahead(
            pT0=pT0, qk_in=[cx.enter_context(nc.semaphore(f"w{m}_in")) for m in "qk"],
            w13_stage=room[:, 0:2 * KC * F].rearrange("p (m c f) -> p m c f", m=2, c=KC),
            queue=sb("queue", [P, 4, R, 3], I32), tokens=sb("tokens", [P, 2, R, D]),
            w_in=[cx.enter_context(nc.semaphore(f"w{m}_in")) for m in (1, 3, 2)],
            queue_in=[cx.enter_context(nc.semaphore(f"queue_in{q}")) for q in range(4)],
            first_gathered=cx.enter_context(nc.semaphore("first_gathered")))
        phase_norm_shared(nc, env, ahead)
        phase_attention(nc, env, ahead)
        phase_routed(nc, env, ahead)


_INS = ["L0_attn_x", "L0_attn_Wq", "L0_attn_Wkv", "L0_attn_Wo", "L0_attn_bo", "L0_ffn_ln_g", "L0_ffn_ln_b", "L0_ffn_Wr",
        "L0_ffn_W1", "L0_ffn_W3", "L0_ffn_W2", "L0_ffn_W1s", "L0_ffn_W3s", "L0_ffn_W2s"]


def kernel(**inputs):
    import numpy as np
    import concourse.bacc as bacc
    from concourse.bass_utils import run_bass_kernel_spmd

    nc = bacc.Bacc("TRN2", target_bir_lowering=False, num_devices=1)
    arrays, args = {}, []
    for name in _INS:
        a = np.ascontiguousarray(inputs[name])
        arrays[f"in_{name}"] = a
        args.append(nc.dram_tensor(f"in_{name}", a.shape, mybir.dt.from_np(a.dtype), kind="ExternalInput").ap())
    x = arrays["in_L0_attn_x"]
    out = nc.dram_tensor("out", x.shape, mybir.dt.from_np(x.dtype), kind="ExternalOutput").ap()
    transformer_layer(nc, *args, out)
    result = run_bass_kernel_spmd(nc, [arrays], core_ids=[0])
    return result.results[0]["out"]
```
